# Optimizing a Trainium2 kernel written in Bass

```python
import numpy as np
import jax
import jax.numpy as jnp

def _softmax(x, axis=-1):
    return jax.nn.softmax(x, axis=axis)

def _gelu(x):
    return jax.nn.gelu(x, approximate=True)

def _silu(x):
    return jax.nn.silu(x)

def _sigmoid(x):
    return jax.nn.sigmoid(x)

def _layernorm(x, axis=-1, eps=1e-05):
    m = jnp.mean(x, axis=axis, keepdims=True)
    v = jnp.var(x, axis=axis, keepdims=True)
    return (x - m) / jnp.sqrt(v + eps)

def _scatter_add(tgt, idx, src, axis=0):
    return tgt.at[idx].add(src)

def _segment_sum(src, seg, n):
    return jax.ops.segment_sum(src, seg, n)
kernel_name = 'mk_adaln_d2_jaxref_r8_c8bb19'

def setup_inputs(seed: int=0):
    np.random.seed(seed)
    _w = jnp.asarray

    def _L0_attn_setup():
        import jax, jax.numpy as jnp
        import numpy as np
        N_HEADS = 16

        def _rope_tables(seq_len, head_dim, dtype):
            inv_freq = 1.0 / 10000.0 ** (jnp.arange(0, head_dim, 2, dtype=jnp.float32) / head_dim)
            t = jnp.arange(seq_len, dtype=jnp.float32)
            freqs = t[:, None] * inv_freq[None, :]
            return (jnp.cos(freqs).astype(dtype), jnp.sin(freqs).astype(dtype))

        def _apply_rope(x, cos, sin):
            d = x.shape[-1]
            x1, x2 = (x[..., :d // 2], x[..., d // 2:])
            return jnp.concatenate([x1 * cos - x2 * sin, x1 * sin + x2 * cos], axis=-1)
        key = jax.random.key(seed)
        k1, k2, k3, k4 = jax.random.split(key, 4)
        B, N, C = (2, 256, 128)
        x = jax.random.normal(k1, (B, N, C), dtype=jnp.float32)
        w_qkv = jax.random.normal(k2, (C, 3 * C), dtype=jnp.float32) * C ** (-0.5)
        w_proj = jax.random.normal(k3, (C, C), dtype=jnp.float32) * C ** (-0.5)
        b_proj = jax.random.normal(k4, (C,), dtype=jnp.float32) * 0.02
        return {'x': x, 'w_qkv': w_qkv, 'w_proj': w_proj, 'b_proj': b_proj}
    _L0_attn_in = _L0_attn_setup()

    def _L0_ffn_setup():
        import jax, jax.numpy as jnp
        import numpy as np
        TOP_K = 2

        def _ffn(x, gw, uw, dw):
            return jax.nn.silu(x @ gw.T) * (x @ uw.T) @ dw.T
        key = jax.random.key(seed)
        ks = jax.random.split(key, 8)
        w = lambda k, shape: jax.random.normal(k, shape, jnp.float32) * 0.02
        return dict(x=jax.random.normal(ks[0], (4, 256, 128), jnp.float32), gate_w=w(ks[1], (8, 128)), expert_gate=w(ks[2], (8, 352, 128)), expert_up=w(ks[3], (8, 352, 128)), expert_down=w(ks[4], (8, 128, 352)), shared_gate=w(ks[5], (352, 128)), shared_up=w(ks[6], (352, 128)), shared_down=w(ks[7], (128, 352)))
    _L0_ffn_in = _L0_ffn_setup()
    _L0_c = _w((lambda *s: np.random.randn(*s).astype(np.float32) * 0.05)(8, 128))
    _L0_wmod = _w((lambda *s: np.random.randn(*s).astype(np.float32) * 0.05)(128, 6 * 128) * 128 ** (-0.5))

    def _L1_attn_setup():
        import math
        import jax, jax.numpy as jnp
        import numpy as np
        D_MODEL = 128
        N_HEAD = 16
        HEAD_DIM = D_MODEL // N_HEAD
        T = 1.0
        EPS = 1e-05

        def _layernorm(t, gamma, beta):
            m = t.mean(axis=-1, keepdims=True)
            var = ((t - m) ** 2).mean(axis=-1, keepdims=True)
            return (t - m) * jax.lax.rsqrt(var + EPS) * gamma + beta
        key = jax.random.key(seed)
        k1, k2, k3 = jax.random.split(key, 3)
        B, S = (4, 256)
        scale = 1.0 / math.sqrt(D_MODEL)
        return {'x': jax.random.normal(k1, (B, S, D_MODEL), dtype=jnp.float32), 'w_qkv': jax.random.normal(k2, (D_MODEL, 3 * D_MODEL), dtype=jnp.float32) * scale, 'w_proj': jax.random.normal(k3, (D_MODEL, D_MODEL), dtype=jnp.float32) * scale, 'q_gamma': jnp.ones((HEAD_DIM,), dtype=jnp.float32), 'q_beta': jnp.zeros((HEAD_DIM,), dtype=jnp.float32), 'k_gamma': jnp.ones((HEAD_DIM,), dtype=jnp.float32), 'k_beta': jnp.zeros((HEAD_DIM,), dtype=jnp.float32)}
    _L1_attn_in = _L1_attn_setup()

    def _L1_ffn_setup():
        import jax, jax.numpy as jnp
        import numpy as np
        DIM = 128
        DEPTH = 2
        HEADS = 8
        DIM_HEAD = 64
        WINDOW = 64
        INNER = HEADS * DIM_HEAD
        HID = int(DIM * 4 * 2 / 3)
        B, N = (2, 1024)
        QK_SCALE = 8.0

        def shift_token(t):
            t1, t2 = jnp.split(t, 2, axis=-1)
            t2 = jnp.pad(t2, ((0, 0), (1, 0), (0, 0)))[:, :-1]
            return jnp.concatenate([t1, t2], axis=-1)

        def l2norm(t):
            return t / jnp.clip(jnp.linalg.norm(t, axis=-1, keepdims=True), 1e-12)

        def rotate_half(x):
            x1, x2 = jnp.split(x, 2, axis=-1)
            return jnp.concatenate([-x2, x1], axis=-1)

        def rotary_xpos(q, k):
            n = q.shape[-2]
            half_idx = jnp.arange(0, DIM_HEAD, 2, dtype=jnp.float32)
            inv_freq = 1.0 / 10000.0 ** (half_idx / DIM_HEAD)
            t = jnp.arange(n, dtype=jnp.float32)
            freqs = t[:, None] * inv_freq[None, :]
            freqs = jnp.concatenate([freqs, freqs], axis=-1)
            base = (half_idx + 0.4 * DIM_HEAD) / (1.4 * DIM_HEAD)
            power = (t - n // 2) / float(WINDOW // 2)
            scale = base[None, :] ** power[:, None]
            scale = jnp.concatenate([scale, scale], axis=-1)
            cos, sin = (jnp.cos(freqs), jnp.sin(freqs))
            q = q * cos * scale + rotate_half(q) * sin * scale
            k = k * cos / scale + rotate_half(k) * sin / scale
            return (q, k)

        def local_attention(q, k, v):
            b, h, n, d = q.shape
            w = n // WINDOW
            bq = q.reshape(b, h, w, WINDOW, d) * QK_SCALE
            bk = k.reshape(b, h, w, WINDOW, d)
            bv = v.reshape(b, h, w, WINDOW, d)

            def look_around(t):
                p = jnp.pad(t, ((0, 0), (0, 0), (1, 0), (0, 0), (0, 0)))
                return jnp.concatenate([p[:, :, :w], p[:, :, 1:]], axis=3)
            bk, bv = (look_around(bk), look_around(bv))
            bt = jnp.arange(n).reshape(w, WINDOW)
            btp = jnp.pad(bt, ((1, 0), (0, 0)), constant_values=-1)
            btk = jnp.concatenate([btp[:w], btp[1:]], axis=1)
            sim = jnp.einsum('bhwid,bhwjd->bhwij', bq, bk)
            i = bt[:, :, None]
            j = btk[:, None, :]
            mask = (i < j) | (i > j + WINDOW) | (j == -1)
            sim = jnp.where(mask, -jnp.finfo(sim.dtype).max, sim)
            attn = jax.nn.softmax(sim, axis=-1)
            out = jnp.einsum('bhwij,bhwjd->bhwid', attn, bv)
            return out.reshape(b, h, n, d)

        def _layer(x, wqkv, qs, ksc, wo, lg, lb, w1, b1, w2, b2):
            b, n, _ = x.shape
            h = shift_token(x)
            qkv = h @ wqkv
            q, k, v = jnp.split(qkv, 3, axis=-1)
            to_heads = lambda t: t.reshape(b, n, HEADS, DIM_HEAD).transpose(0, 2, 1, 3)
            q, k, v = (to_heads(q), to_heads(k), to_heads(v))
            q = l2norm(q) * qs
            k = l2norm(k) * ksc
            q, k = rotary_xpos(q, k)
            o = local_attention(q, k, v)
            o = o.transpose(0, 2, 1, 3).reshape(b, n, INNER)
            x = x + o @ wo
            h = shift_token(x)
            mu = h.mean(-1, keepdims=True)
            var = h.var(-1, keepdims=True)
            h = (h - mu) / jnp.sqrt(var + 1e-05) * lg + lb
            h = h @ w1 + b1
            a, g = jnp.split(h, 2, axis=-1)
            h = a * jax.nn.gelu(g, approximate=False)
            x = x + h @ w2 + b2
            return x
        key = jax.random.key(seed)
        ks = jax.random.split(key, 6)
        return {'x': jax.random.normal(ks[0], (B, N, DIM), jnp.float32), 'wqkv': jax.random.normal(ks[1], (DEPTH, DIM, 3 * INNER), jnp.float32) * 0.02, 'q_scale': jnp.ones((DEPTH, DIM_HEAD), jnp.float32), 'k_scale': jnp.ones((DEPTH, DIM_HEAD), jnp.float32), 'wo': jax.random.normal(ks[2], (DEPTH, INNER, DIM), jnp.float32) * 0.02, 'ln_g': jnp.ones((DEPTH, DIM), jnp.float32), 'ln_b': jnp.zeros((DEPTH, DIM), jnp.float32), 'w1': jax.random.normal(ks[3], (DEPTH, DIM, 2 * HID), jnp.float32) * 0.02, 'b1': jnp.zeros((DEPTH, 2 * HID), jnp.float32), 'w2': jax.random.normal(ks[4], (DEPTH, HID, DIM), jnp.float32) * 0.02, 'b2': jnp.zeros((DEPTH, DIM), jnp.float32)}
    _L1_ffn_in = _L1_ffn_setup()
    _L1_c = _w((lambda *s: np.random.randn(*s).astype(np.float32) * 0.05)(8, 128))
    _L1_wmod = _w((lambda *s: np.random.randn(*s).astype(np.float32) * 0.05)(128, 6 * 128) * 128 ** (-0.5))
    _d = {'L0_attn_x': _L0_attn_in['x'], 'L0_attn_w_qkv': _L0_attn_in['w_qkv'], 'L0_attn_w_proj': _L0_attn_in['w_proj'], 'L0_attn_b_proj': _L0_attn_in['b_proj'], 'L0_ffn_gate_w': _L0_ffn_in['gate_w'], 'L0_ffn_expert_gate': _L0_ffn_in['expert_gate'], 'L0_ffn_expert_up': _L0_ffn_in['expert_up'], 'L0_ffn_expert_down': _L0_ffn_in['expert_down'], 'L0_ffn_shared_gate': _L0_ffn_in['shared_gate'], 'L0_ffn_shared_up': _L0_ffn_in['shared_up'], 'L0_ffn_shared_down': _L0_ffn_in['shared_down'], 'L0_c': _L0_c, 'L0_wmod': _L0_wmod, 'L1_attn_w_qkv': _L1_attn_in['w_qkv'], 'L1_attn_w_proj': _L1_attn_in['w_proj'], 'L1_attn_q_gamma': _L1_attn_in['q_gamma'], 'L1_attn_q_beta': _L1_attn_in['q_beta'], 'L1_attn_k_gamma': _L1_attn_in['k_gamma'], 'L1_attn_k_beta': _L1_attn_in['k_beta'], 'L1_ffn_wqkv': _L1_ffn_in['wqkv'], 'L1_ffn_q_scale': _L1_ffn_in['q_scale'], 'L1_ffn_k_scale': _L1_ffn_in['k_scale'], 'L1_ffn_wo': _L1_ffn_in['wo'], 'L1_ffn_ln_g': _L1_ffn_in['ln_g'], 'L1_ffn_ln_b': _L1_ffn_in['ln_b'], 'L1_ffn_w1': _L1_ffn_in['w1'], 'L1_ffn_b1': _L1_ffn_in['b1'], 'L1_ffn_w2': _L1_ffn_in['w2'], 'L1_ffn_b2': _L1_ffn_in['b2'], 'L1_c': _L1_c, 'L1_wmod': _L1_wmod}
    _x0 = _d['L0_attn_x']
    _d['L0_attn_x'] = jax.random.normal(jax.random.fold_in(jax.random.key(seed), 1), (8, 512, 128), dtype=_x0.dtype)
    del _x0
    return _d

def reference(L0_attn_x, L0_attn_w_qkv, L0_attn_w_proj, L0_attn_b_proj, L0_ffn_gate_w, L0_ffn_expert_gate, L0_ffn_expert_up, L0_ffn_expert_down, L0_ffn_shared_gate, L0_ffn_shared_up, L0_ffn_shared_down, L0_c, L0_wmod, L1_attn_w_qkv, L1_attn_w_proj, L1_attn_q_gamma, L1_attn_q_beta, L1_attn_k_gamma, L1_attn_k_beta, L1_ffn_wqkv, L1_ffn_q_scale, L1_ffn_k_scale, L1_ffn_wo, L1_ffn_ln_g, L1_ffn_ln_b, L1_ffn_w1, L1_ffn_b1, L1_ffn_w2, L1_ffn_b2, L1_c, L1_wmod):

    def _L0_attn_ref(x, w_qkv, w_proj, b_proj):
        import jax, jax.numpy as jnp
        import numpy as np
        N_HEADS = 16

        def _rope_tables(seq_len, head_dim, dtype):
            inv_freq = 1.0 / 10000.0 ** (jnp.arange(0, head_dim, 2, dtype=jnp.float32) / head_dim)
            t = jnp.arange(seq_len, dtype=jnp.float32)
            freqs = t[:, None] * inv_freq[None, :]
            return (jnp.cos(freqs).astype(dtype), jnp.sin(freqs).astype(dtype))

        def _apply_rope(x, cos, sin):
            d = x.shape[-1]
            x1, x2 = (x[..., :d // 2], x[..., d // 2:])
            return jnp.concatenate([x1 * cos - x2 * sin, x1 * sin + x2 * cos], axis=-1)
        B, N, C = x.shape
        H = N_HEADS
        d = C // H
        scale = d ** (-0.5)
        qkv = (x @ w_qkv).reshape(B, N, 3, H, d)
        qkv = jnp.transpose(qkv, (2, 0, 3, 1, 4))
        q, k, v = (qkv[0], qkv[1], qkv[2])
        cos, sin = _rope_tables(N, d, x.dtype)
        q = _apply_rope(q, cos, sin)
        k = _apply_rope(k, cos, sin)
        attn = jnp.einsum('bhqd,bhkd->bhqk', q, k) * scale
        attn = jax.nn.softmax(attn, axis=-1)
        out = jnp.einsum('bhqk,bhkd->bhqd', attn, v)
        out = jnp.transpose(out, (0, 2, 1, 3)).reshape(B, N, C)
        return out @ w_proj + b_proj

    def _L0_ffn_ref(x, gate_w, expert_gate, expert_up, expert_down, shared_gate, shared_up, shared_down):
        import jax, jax.numpy as jnp
        import numpy as np
        TOP_K = 2

        def _ffn(x, gw, uw, dw):
            return jax.nn.silu(x @ gw.T) * (x @ uw.T) @ dw.T
        B, S, H = x.shape
        xf = x.reshape(-1, H)
        T = xf.shape[0]
        E = expert_gate.shape[0]
        shared = _ffn(xf, shared_gate, shared_up, shared_down)
        logits = xf @ gate_w.T
        probs = jax.nn.softmax(logits, axis=-1)
        topw, topi = jax.lax.top_k(probs, TOP_K)
        topw = topw / (topw.sum(-1, keepdims=True) + 1e-20)
        comb = jnp.zeros((T, E), xf.dtype).at[jnp.arange(T)[:, None], topi].add(topw)

        def body(acc, ws):
            gw, uw, dw, wcol = ws
            return (acc + _ffn(xf, gw, uw, dw) * wcol[:, None], None)
        routed, _ = jax.lax.scan(body, jnp.zeros_like(xf), (expert_gate, expert_up, expert_down, comb.T))
        return (shared + routed).reshape(B, S, H)

    def _L1_attn_ref(x, w_qkv, w_proj, q_gamma, q_beta, k_gamma, k_beta):
        import math
        import jax, jax.numpy as jnp
        import numpy as np
        D_MODEL = 128
        N_HEAD = 16
        HEAD_DIM = D_MODEL // N_HEAD
        T = 1.0
        EPS = 1e-05

        def _layernorm(t, gamma, beta):
            m = t.mean(axis=-1, keepdims=True)
            var = ((t - m) ** 2).mean(axis=-1, keepdims=True)
            return (t - m) * jax.lax.rsqrt(var + EPS) * gamma + beta
        B, S, C = x.shape
        H, Dh = (N_HEAD, HEAD_DIM)
        qkv = (x @ w_qkv).reshape(B, S, 3, H, Dh)
        qkv = jnp.transpose(qkv, (2, 0, 3, 1, 4))
        q, k, v = (qkv[0], qkv[1], qkv[2])
        q = _layernorm(q, q_gamma, q_beta)
        k = _layernorm(k, k_gamma, k_beta)
        logits = jnp.einsum('bhsd,bhtd->bhst', q, k) / (math.sqrt(Dh) * T)
        att = jax.nn.softmax(logits, axis=-1)
        out = jnp.einsum('bhst,bhtd->bhsd', att, v)
        out = jnp.transpose(out, (0, 2, 1, 3)).reshape(B, S, C)
        return out @ w_proj

    def _L1_ffn_ref(x, wqkv, q_scale, k_scale, wo, ln_g, ln_b, w1, b1, w2, b2):
        import jax, jax.numpy as jnp
        import numpy as np
        DIM = 128
        DEPTH = 2
        HEADS = 8
        DIM_HEAD = 64
        WINDOW = 64
        INNER = HEADS * DIM_HEAD
        HID = int(DIM * 4 * 2 / 3)
        B, N = (2, 1024)
        QK_SCALE = 8.0

        def shift_token(t):
            t1, t2 = jnp.split(t, 2, axis=-1)
            t2 = jnp.pad(t2, ((0, 0), (1, 0), (0, 0)))[:, :-1]
            return jnp.concatenate([t1, t2], axis=-1)

        def l2norm(t):
            return t / jnp.clip(jnp.linalg.norm(t, axis=-1, keepdims=True), 1e-12)

        def rotate_half(x):
            x1, x2 = jnp.split(x, 2, axis=-1)
            return jnp.concatenate([-x2, x1], axis=-1)

        def rotary_xpos(q, k):
            n = q.shape[-2]
            half_idx = jnp.arange(0, DIM_HEAD, 2, dtype=jnp.float32)
            inv_freq = 1.0 / 10000.0 ** (half_idx / DIM_HEAD)
            t = jnp.arange(n, dtype=jnp.float32)
            freqs = t[:, None] * inv_freq[None, :]
            freqs = jnp.concatenate([freqs, freqs], axis=-1)
            base = (half_idx + 0.4 * DIM_HEAD) / (1.4 * DIM_HEAD)
            power = (t - n // 2) / float(WINDOW // 2)
            scale = base[None, :] ** power[:, None]
            scale = jnp.concatenate([scale, scale], axis=-1)
            cos, sin = (jnp.cos(freqs), jnp.sin(freqs))
            q = q * cos * scale + rotate_half(q) * sin * scale
            k = k * cos / scale + rotate_half(k) * sin / scale
            return (q, k)

        def local_attention(q, k, v):
            b, h, n, d = q.shape
            w = n // WINDOW
            bq = q.reshape(b, h, w, WINDOW, d) * QK_SCALE
            bk = k.reshape(b, h, w, WINDOW, d)
            bv = v.reshape(b, h, w, WINDOW, d)

            def look_around(t):
                p = jnp.pad(t, ((0, 0), (0, 0), (1, 0), (0, 0), (0, 0)))
                return jnp.concatenate([p[:, :, :w], p[:, :, 1:]], axis=3)
            bk, bv = (look_around(bk), look_around(bv))
            bt = jnp.arange(n).reshape(w, WINDOW)
            btp = jnp.pad(bt, ((1, 0), (0, 0)), constant_values=-1)
            btk = jnp.concatenate([btp[:w], btp[1:]], axis=1)
            sim = jnp.einsum('bhwid,bhwjd->bhwij', bq, bk)
            i = bt[:, :, None]
            j = btk[:, None, :]
            mask = (i < j) | (i > j + WINDOW) | (j == -1)
            sim = jnp.where(mask, -jnp.finfo(sim.dtype).max, sim)
            attn = jax.nn.softmax(sim, axis=-1)
            out = jnp.einsum('bhwij,bhwjd->bhwid', attn, bv)
            return out.reshape(b, h, n, d)

        def _layer(x, wqkv, qs, ksc, wo, lg, lb, w1, b1, w2, b2):
            b, n, _ = x.shape
            h = shift_token(x)
            qkv = h @ wqkv
            q, k, v = jnp.split(qkv, 3, axis=-1)
            to_heads = lambda t: t.reshape(b, n, HEADS, DIM_HEAD).transpose(0, 2, 1, 3)
            q, k, v = (to_heads(q), to_heads(k), to_heads(v))
            q = l2norm(q) * qs
            k = l2norm(k) * ksc
            q, k = rotary_xpos(q, k)
            o = local_attention(q, k, v)
            o = o.transpose(0, 2, 1, 3).reshape(b, n, INNER)
            x = x + o @ wo
            h = shift_token(x)
            mu = h.mean(-1, keepdims=True)
            var = h.var(-1, keepdims=True)
            h = (h - mu) / jnp.sqrt(var + 1e-05) * lg + lb
            h = h @ w1 + b1
            a, g = jnp.split(h, 2, axis=-1)
            h = a * jax.nn.gelu(g, approximate=False)
            x = x + h @ w2 + b2
            return x
        for l in range(DEPTH):
            x = _layer(x, wqkv[l], q_scale[l], k_scale[l], wo[l], ln_g[l], ln_b[l], w1[l], b1[l], w2[l], b2[l])
        return x
    x = L0_attn_x
    mod = (_silu(L0_c) @ L0_wmod).reshape(L0_c.shape[0], 6, 1, -1)
    sa, ca, ga, sb, cb, gb = (mod[:, 0], mod[:, 1], mod[:, 2], mod[:, 3], mod[:, 4], mod[:, 5])
    ga = (2 * (ga >= 0) - 1) * jnp.maximum(jnp.abs(ga), 0.25)
    gb = (2 * (gb >= 0) - 1) * jnp.maximum(jnp.abs(gb), 0.25)
    h = _layernorm(x, axis=-1) * (1 + ca) + sa
    x = x + ga * _L0_attn_ref(h, L0_attn_w_qkv, L0_attn_w_proj, L0_attn_b_proj)
    h = _layernorm(x, axis=-1) * (1 + cb) + sb
    x = x + gb * _L0_ffn_ref(h, L0_ffn_gate_w, L0_ffn_expert_gate, L0_ffn_expert_up, L0_ffn_expert_down, L0_ffn_shared_gate, L0_ffn_shared_up, L0_ffn_shared_down)
    mod = (_silu(L1_c) @ L1_wmod).reshape(L1_c.shape[0], 6, 1, -1)
    sa, ca, ga, sb, cb, gb = (mod[:, 0], mod[:, 1], mod[:, 2], mod[:, 3], mod[:, 4], mod[:, 5])
    ga = (2 * (ga >= 0) - 1) * jnp.maximum(jnp.abs(ga), 0.25)
    gb = (2 * (gb >= 0) - 1) * jnp.maximum(jnp.abs(gb), 0.25)
    h = _layernorm(x, axis=-1) * (1 + ca) + sa
    x = x + ga * _L1_attn_ref(h, L1_attn_w_qkv, L1_attn_w_proj, L1_attn_q_gamma, L1_attn_q_beta, L1_attn_k_gamma, L1_attn_k_beta)
    h = _layernorm(x, axis=-1) * (1 + cb) + sb
    x = x + gb * _L1_ffn_ref(h, L1_ffn_wqkv, L1_ffn_q_scale, L1_ffn_k_scale, L1_ffn_wo, L1_ffn_ln_g, L1_ffn_ln_b, L1_ffn_w1, L1_ffn_b1, L1_ffn_w2, L1_ffn_b2)
    return x

_drawn_inputs = setup_inputs


def setup_inputs(seed=0):
    import zlib

    import numpy as np

    out = dict(_drawn_inputs(seed))
    spreads = {'L1_attn_q_gamma': (1.0, 0.6),
     'L1_attn_q_beta': (0.0, 0.8),
     'L1_attn_k_gamma': (1.0, 0.6),
     'L1_attn_k_beta': (0.0, 2.0),
     'L1_ffn_q_scale': (1.0, 0.6),
     'L1_ffn_k_scale': (1.0, 0.6),
     'L1_ffn_ln_g': (1.0, 0.6),
     'L1_ffn_ln_b': (0.0, 0.8),
     'L1_ffn_b1': (0.0, 0.8),
     'L1_ffn_b2': (0.0, 0.8)}
    factors = {'L0_attn_b_proj': 8.0,
     'L0_ffn_gate_w': 8.0,
     'L0_ffn_expert_gate': 8.0,
     'L0_ffn_expert_up': 8.0,
     'L0_ffn_expert_down': 8.0,
     'L0_ffn_shared_gate': 8.0,
     'L0_ffn_shared_up': 8.0,
     'L0_ffn_shared_down': 8.0,
     'L1_ffn_wqkv': 7.537,
     'L1_ffn_wo': 7.58,
     'L1_ffn_w1': 8.0,
     'L1_ffn_w2': 8.0}
    for name, (base, spread) in spreads.items():
        noise = np.random.default_rng([zlib.crc32(name.encode()), seed]).standard_normal(out[name].shape)
        drawn = base * np.exp(spread * noise) if base else spread * noise
        out[name] = jnp.asarray(drawn.astype(out[name].dtype))
    for name, factor in factors.items():
        out[name] = (out[name] * factor).astype(out[name].dtype)
    return out
```

```python
import numpy as np
import concourse.bass as bass
from concourse import mybir
from contextlib import ExitStack

F32 = mybir.dt.float32
BF16 = mybir.dt.bfloat16
U32 = mybir.dt.uint32
ALU = mybir.AluOpType
ACT = mybir.ActivationFunctionType
AX = mybir.AxisListType

B, S, C = 8, 512, 128
SLOTS = 2
NT = S // 128
H, DH = 16, 8
GRP = 4
NG = H // GRP
E, HID = 8, 352
CH = [128, 128, 96]
LH, LD, WIN = 8, 64, 64
DEPTH = 2
GH = 341
GC = [128, 128, 85]
MASKED = -1e30
TERMS = 6
KR = TERMS * DH
KM = KR + 3


def columns(sizes):
    at, out = 0, {}
    for name, n in sizes:
        out[name] = (at, at + n)
        at += n
    return out, at


CONST_SIZES = [("ident", 128), ("center", 128), ("center8", 128), ("inv", 1), ("blk16", H), ("blk2", 2),
               ("sel4", GRP), ("iota8", E), ("cos", S), ("sin", S), ("xa", S), ("xb", S), ("xai", S),
               ("xbi", S), ("mask", 192), ("spread_o", NG * 128), ("spread_h", 2 * 128), ("spread_n", 4 * 128)]
ATT_SIZES = [("q0", 128), ("qr0", 128), ("k0", 128), ("kr0", 128), ("v0", 128), ("qT1", 128),
             ("kT1", 128), ("v1", 128), ("p0", NG * 128), ("p1", NG * 128)]
MOE_SIZES = [("gate", E), ("g", (E + 1) * HID), ("u", (E + 1) * HID), ("d", (E + 1) * 3 * 128)]
QKV = 4 * 128
FFN_ONE = [("q", QKV), ("qr", QKV), ("k", QKV), ("kr", QKV), ("v", QKV), ("wo", 4 * 128),
           ("w1", 2 * GH), ("w2", 3 * 128)]
VEC_SIZES = [("bproj", 1), ("qg", 1), ("qb", 1), ("kg", 1), ("kb", 1)] + [
    (f"{n}{d}", w) for d in range(DEPTH)
    for n, w in (("qs", 1), ("qsr", 1), ("ks", 1), ("ksr", 1), ("lg", 1), ("lb", 1), ("b1", 6), ("b2", 1))]
FFN_SIZES = [(f"{n}{d}", w) for d in range(DEPTH) for n, w in FFN_ONE]
CC, NC_ = columns(CONST_SIZES)
AC, NA_ = columns(ATT_SIZES)
MC, NM_ = columns(MOE_SIZES)
FC, NF_ = columns(FFN_SIZES)
VC, NV_ = columns(VEC_SIZES)


def constants():
    t = {}
    t["ident"] = np.eye(128)
    t["center"] = np.eye(128) - 1.0 / 128
    blk = np.kron(np.eye(H), np.ones((DH, DH))) / DH
    t["center8"] = np.eye(128) - blk
    t["inv"] = np.full((128, 1), 1.0 / 128)
    t["blk16"] = np.kron(np.eye(H), np.ones((DH, 1))) / DH
    t["blk2"] = np.kron(np.eye(2), np.ones((LD, 1)))
    sel = np.zeros((128, GRP))
    for j in range(GRP):
        sel[32 * j + DH, j] = 1.0
    t["sel4"] = sel
    t["iota8"] = np.tile(np.arange(E), (128, 1))
    f4 = np.float32
    tok = np.arange(S, dtype=f4)
    inv = (f4(1.0) / f4(10000.0) ** (np.arange(0, DH, 2, dtype=f4) / f4(DH))).astype(f4)
    fr = tok[None, :] * inv[:, None]
    cos, sin = np.cos(fr), np.sin(fr)
    t["cos"] = np.tile(np.concatenate([cos, cos]), (H, 1))
    t["sin"] = np.tile(np.concatenate([-sin, sin]), (H, 1))
    half = np.arange(0, LD, 2, dtype=f4)
    inv = (f4(1.0) / f4(10000.0) ** (half / f4(LD))).astype(f4)
    fr = tok[None, :] * inv[:, None]
    base = (half + f4(0.4 * LD)) / f4(1.4 * LD)
    scale = base[:, None] ** ((tok - S // 2) / f4(WIN // 2))[None, :]
    cos, sin = np.cos(fr), np.sin(fr)
    two = lambda a, b: np.tile(np.concatenate([a, b]), (2, 1))
    t["xa"] = two(cos * scale, cos * scale)
    t["xb"] = two(-sin * scale, sin * scale)
    t["xai"] = two(cos / scale, cos / scale)
    t["xbi"] = two(-sin / scale, sin / scale)
    i, j = np.arange(128)[:, None], np.arange(192)[None, :] - 64
    t["mask"] = np.where((i < j) | (i > j + WIN), MASKED, 0.0)
    o, h, n = np.zeros((128, NG, GRP, 32)), np.zeros((128, 2, H, DH)), np.zeros((128, 4, 2, LD))
    for g in range(NG):
        for k in range(GRP):
            o[GRP * g + k, g, k] = 1.0
    for k in range(2):
        for head in range(H):
            h[k * H + head, k, head] = 1.0
    for f in range(4):
        for k in range(2):
            n[(4 + f) * 2 + k, f, k] = 1.0
    t["spread_o"], t["spread_h"], t["spread_n"] = (a.reshape(128, -1) for a in (o, h, n))
    return np.concatenate([t[n].astype(np.float32) for n, _ in CONST_SIZES], axis=1)


def adaln_kernel(nc, x, consts, ones, att_w, moe_w, ffn_w, vec, cT, wmod, out):
    ctx = ExitStack()
    with ctx:
        def sb(name, shape, dt=F32):
            return ctx.enter_context(nc.sbuf_tensor(name, shape, dt))

        sems = []

        def sem(name):
            s = ctx.enter_context(nc.semaphore(name))
            sems.append(s)
            return s

        bank = [ctx.enter_context(nc.psum_tensor(f"bank{i}", [128, 512], F32)) for i in range(8)]

        cst = sb("cst", [128, NC_])
        aw = sb("aw", [128, NA_])
        mw = sb("mw", [128, NM_])
        fw = sb("fw", [128, NF_])
        vc = sb("vc", [128, NV_])
        wqc = sb("wqc", [128, 2, 128])
        mod = sb("mod", [128, 14, B])
        modu = sb("modu", [128, 14, SLOTS])

        def K(n):
            return cst[:, CC[n][0]:CC[n][1]]

        def AW(n):
            return aw[:, AC[n][0]:AC[n][1]]

        def MW(n):
            return mw[:, MC[n][0]:MC[n][1]]

        def FW(n, d):
            return fw[:, FC[f"{n}{d}"][0]:FC[f"{n}{d}"][1]]

        def V_(n):
            return vc[:, VC[n][0]:VC[n][1]]

        def MOD(l, j, u):
            return modu[:, 7 * l + j, u:u + 1]

        ident = K("ident")
        X = [sb(f"X{u}", [128, S]) for u in range(SLOTS)]
        Hh = [sb(f"H{u}", [128, S]) for u in range(SLOTS)]
        G = [sb(f"G{u}", [128, S]) for u in range(SLOTS)]
        SH = [sb(f"SH{u}", [128, S]) for u in range(SLOTS)]
        XC = [sb(f"XC{u}", [128, S]) for u in range(SLOTS)]
        SQ = [sb(f"SQ{u}", [128, S]) for u in range(SLOTS)]
        ve = sb("ve", [128, SLOTS, NT])
        rs = sb("rs", [128, SLOTS, NT])
        mhalf = sb("mhalf", [128, NT])
        eps24 = sb("eps_col", [128, 1])
        st128 = sb("st128", [128, SLOTS, 128])
        ARENA = 20480
        ar = sb("stage_memory", [128, ARENA])
        cur = [0]

        def part(n):
            a = cur[0]
            cur[0] += n
            assert cur[0] <= ARENA, cur[0]
            return ar[:, a:a + n]

        qst = part(H * S // 2).bitcast(BF16).rearrange("p (h t) -> p h t", h=H)
        kst32 = part(H * S // 2)
        kst = kst32.bitcast(BF16).rearrange("p (h t) -> p h t", h=H)
        vaug = [part(NT * H * 16).rearrange("p (t h c) -> p t h c", t=NT, h=H) for u in range(SLOTS)]
        PTB = 8
        pt = [part(S) for _ in range(PTB)]
        raw = [[part(S) for g in range(NG)] for u in range(SLOTS)]
        qf = [raw[u][0] for u in range(SLOTS)]
        kf = [raw[u][1] for u in range(SLOTS)]
        rem = [raw[u][2] for u in range(SLOTS)]
        ropet = [raw[u][3] for u in range(SLOTS)]
        cur[0] = 0
        off = 2 * H * S // 2 + SLOTS * NT * H * 16
        parts = [[ar[:, off + 1536 * u + 768 * i:off + 1536 * u + 768 * (i + 1)].bitcast(BF16)
                  .rearrange("p (j t) -> p j t", j=3) for i in range(2)] for u in range(SLOTS)]
        cb = [part(E * S).rearrange("p (e t) -> p e t", e=E) for u in range(SLOTS)]
        hx = [part(S) for _ in range(3)]
        sl = [part(S) for _ in range(3)]
        hd = [part(S) for _ in range(3)]
        cbT = [part(S) for u in range(SLOTS)]
        small = lambda n: [part(NT * n).rearrange("p (t e) -> p t e", t=NT) for u in range(SLOTS)]
        lg, top, topf, comb, c2, w2v = (small(n) for n in (E, 8, 8, E, E, 2))
        topi = [a.bitcast(U32) for a in small(8)]
        s4 = [part(NT) for u in range(SLOTS)]
        cur[0] = 0
        qk = [part(8 * S).rearrange("p (i t) -> p i t", i=8) for u in range(SLOTS)]
        vv = [part(NT * S).rearrange("p (t f) -> p t f", t=NT) for u in range(SLOTS)]
        prf = [part(4 * 256) for _ in range(3)]
        pr = [p.rearrange("p (a j k) -> p a j k", a=2, j=2) for p in prf]
        ptc = [part(512) for _ in range(2)]
        ptp = [part(512) for _ in range(2)]
        xt = [part(S) for _ in range(2)]
        tab = part(4 * S).rearrange("p (i t) -> p i t", i=4)
        qs = ptc
        sqr = ptp
        glu = [prf[0][:, 0:S], prf[1][:, 0:S]]
        ghd = [ptc[0], ptc[1]]
        cur[0] = 0

        mx = [sb(f"mx{i}", [128, 16]) for i in range(2)]
        mneg = sb("mneg", [16, 128])
        m3 = [sb(f"m3_{i}", [16, 3, 128], BF16) for i in range(2)]
        rec = sb("rec", [128, SLOTS, NG * NT * GRP])
        lm = [sb(f"lm{i}", [128, 2, 2]) for i in range(3)]
        lsum = [sb(f"lsum{i}", [128, 2, 2]) for i in range(3)]
        lrec = [sb(f"lrec{i}", [128, 2, 2]) for i in range(3)]

        scr = nc.dram_tensor("scr_parts", (2, SLOTS, 2, 3, 128, S), BF16, kind="Internal").ap()
        scr_c = nc.dram_tensor("scr_comb", (SLOTS, E, S), F32, kind="Internal").ap()

        s_load = sem("s_load")
        s_pe0 = sem("s_pe0")
        s_act0 = sem("s_act0")
        s_dve0 = sem("s_dve0")
        s_pool0 = sem("s_pool0")
        ct = ar[:, 0:2 * B]
        wm = ar[:, 1024:1024 + 2 * 6 * C].rearrange("p (l n) -> p l n", l=2)
        mtmp = ar[:, 4096:4096 + 2 * 4 * B].rearrange("p (l j b) -> p l j b", l=2, j=4)
        with nc.Block() as block:
            @block.sync
            def _(sp):
                for dst, src in ((ct, cT), (wm, wmod.rearrange("l p n -> p l n")), (vc[:, :], vec),
                                 (cst[:, :], consts), (aw[:, :], att_w), (mw[:, :], moe_w), (fw[:, :], ffn_w)):
                    sp.dma_start(dst, src).then_inc(s_load, 16)
                sp.wait_ge(s_load, 16 * 7)

            @block.gpsimd
            def _(pool):
                nc.gpsimd.memset(mhalf[:, :], -0.5).then_inc(s_pool0, 1)
                nc.gpsimd.memset(eps24[:, :], 1e-5).then_inc(s_pool0, 1)
                for u in range(SLOTS):
                    nc.gpsimd.memset(SH[u][:, :], 0.0).then_inc(s_pool0, 1)

            @block.scalar
            def _(act):
                act.wait_ge(s_load, 16 * 7)
                nc.scalar.activation(ct, ct, ACT.Silu).then_inc(s_act0, 1)

            @block.tensor
            def _(pe):
                pe.wait_ge(s_load, 16 * 7)
                pe.wait_ge(s_act0, 1)
                for l in range(2):
                    for j in range(6):
                        nc.tensor.matmul(bank[0][:, (6 * l + j) * B:(6 * l + j + 1) * B],
                                         wm[:, l, j * C:(j + 1) * C], ct[:, l * B:(l + 1) * B],
                                         start=True, stop=True).then_inc(s_pe0, 1)
                for i, n in enumerate(("qT1", "kT1")):
                    nc.tensor.matmul(bank[1][:, i * 128:(i + 1) * 128], AW(n), K("center8"),
                                     start=True, stop=True).then_inc(s_pe0, 1)

            @block.vector
            def _(dve):
                done = [0]

                def step(ins):
                    done[0] += 1
                    ins.then_inc(s_dve0, 1)
                    dve.wait_ge(s_dve0, done[0])

                dve.wait_ge(s_pe0, 14)
                step(nc.vector.tensor_copy(wqc[:, :, :], bank[1][:, 0:256].rearrange("p (i c) -> p i c", i=2)))
                m = mod[:, :, :].rearrange("p (l j) b -> p l j b", l=2)
                step(nc.vector.tensor_copy(m[:, :, 0:6, :],
                                           bank[0][:, 0:12 * B].rearrange("p (l j b) -> p l j b", l=2, j=6)))
                for j in (1, 4):
                    step(nc.vector.tensor_scalar(m[:, :, j, :], m[:, :, j, :], 1.0, None, ALU.add))
                for j in (2, 5):
                    g, a, s = m[:, :, j, :], mtmp[:, :, 0, :], mtmp[:, :, 1, :]
                    step(nc.vector.tensor_scalar(a, g, -1.0, None, ALU.mult))
                    step(nc.vector.tensor_tensor(a, a, g, ALU.max))
                    step(nc.vector.tensor_scalar(s, g, 0.0, 2.0, ALU.is_ge, ALU.mult))
                    step(nc.vector.tensor_scalar(s, s, 1.0, None, ALU.subtract))
                    step(nc.vector.tensor_scalar(a, a, 0.25, None, ALU.max))
                    step(nc.vector.tensor_tensor(g, a, s, ALU.mult))
                step(nc.vector.tensor_scalar(m[:, :, 6, :], m[:, :, 2, :], V_("bproj"), None, ALU.mult))
                step(nc.vector.tensor_scalar(m[:, 1, 6, :], m[:, 1, 2, :], 0.0, None, ALU.mult))

        x_in = sem("x_in"); x_tr = sem("x_tr"); x_ready = sem("x_ready"); mod_ready = sem("mod_ready")
        dve_link = sem("dve_link"); zeroed = sem("zeroed"); sp_first = sem("sp_first"); l_evp = sem("l_evp")
        ln_cent = sem("ln_cent"); ln_xc = sem("ln_xc"); ln_sq = sem("ln_sq"); ln_stat = sem("ln_stat")
        ln_var = sem("ln_var"); ln_rstd = sem("ln_rstd"); ln_bc = sem("ln_bc"); ln_h = sem("ln_h")
        at_prod = sem("at_prod"); at_used = sem("at_used"); at_v = sem("at_v")
        at_sq = sem("at_sq"); at_stat = sem("at_stat"); at_ve = sem("at_ve"); at_sd = sem("at_sd")
        at_rs = sem("at_rs"); at_bc = sem("at_bc"); at_rt = sem("at_rt"); at_rc = sem("at_rc")
        den_tr = sem("den_tr"); den_cp = sem("den_cp"); f_rt = sem("f_rt"); f_rc = sem("f_rc"); at_f = sem("at_f")
        sp_hi = sem("sp_hi"); sp_r = sem("sp_r"); sp_mid = sem("sp_mid"); sp_done = sem("sp_done")
        vaug_one = sem("vaug_one")
        st_wr = [sem(f"st_wr{u}") for u in range(SLOTS)]
        st_rd = [sem(f"st_rd{u}") for u in range(SLOTS)]
        a_mm = sem("a_mm"); a_mx = sem("a_mx"); m_tr = sem("m_tr"); m_spl = sem("m_spl"); m_row = sem("m_row")
        s_mm = sem("s_mm"); e_done = sem("e_done"); pv_done = sem("pv_done"); o_raw = sem("o_raw")
        den_mm = sem("den_mm"); den_rec = sem("den_rec"); den_bc = sem("den_bc"); o_norm = sem("o_norm")
        y_att = sem("y_att"); t_att = sem("t_att"); x_att = sem("x_att")
        gt_mm = sem("gt_mm"); gt_sub = sem("gt_sub"); gt_exp = sem("gt_exp"); gt_comb = sem("gt_comb")
        gt_tr = sem("gt_tr"); gt_row = sem("gt_row"); cb_wr = sem("cb_wr")
        cb_rd = [sem(f"cb_rd{u}") for u in range(SLOTS)]
        hx_ready = sem("hx_ready"); mo_g = sem("mo_g"); mo_u = sem("mo_u"); mo_sl = sem("mo_sl")
        mo_hd = sem("mo_hd"); mo_dn = sem("mo_dn"); x_moe = sem("x_moe")
        sh_ready = sem("sh_ready"); tb_ready = sem("tb_ready")
        f_main = sem("f_main"); f_rot = sem("f_rot"); f_cp = sem("f_cp"); f_sq = sem("f_sq")
        f_t1 = sem("f_t1"); f_t2 = sem("f_t2"); f_tt = sem("f_tt"); f_stat = sem("f_stat")
        f_v = sem("f_v"); f_vc = sem("f_vc"); f_n2 = sem("f_n2"); f_sd = sem("f_sd"); f_rn = sem("f_rn")
        f_bc = sem("f_bc"); f_kn = sem("f_kn")
        l_s = sem("l_s"); l_mk = sem("l_mk"); l_nm = sem("l_nm"); l_ex = sem("l_ex"); l_p = sem("l_p")
        l_tr = sem("l_tr"); l_ev = sem("l_ev"); l_pv = sem("l_pv"); l_o = sem("l_o")
        wo_mm = sem("wo_mm"); z_att = sem("z_att")
        w1_mm = sem("w1_mm"); w1_gl = sem("w1_gl"); w1_hd = sem("w1_hd"); w2_mm = sem("w2_mm"); z_ffn = sem("z_ffn")
        x_last = sem("x_last"); o_tr = sem("o_tr"); o_ev = sem("o_ev"); o_dma = sem("o_dma")
        turn_sems = sems[5:]
        first, last = turn_sems[0].num, turn_sems[-1].num
        assert last - first == len(turn_sems) - 1

        xv = x.rearrange("(w u) (t p) c -> u p w t c", p=128, u=SLOTS)
        ov = out.rearrange("(w u) (t p) c -> u p w t c", p=128, u=SLOTS)
        xin = [G[u][:, :].rearrange("p (o t c) -> p o t c", o=1, t=NT) for u in range(SLOTS)]
        slots = range(SLOTS)
        NU = SLOTS * NG
        LNS = 6

        with nc.Fori(0, B // SLOTS) as turn:
            with nc.Block() as block:
                @block.sync
                def _(sp):
                    for u in slots:
                        sp.dma_start(xin[u], xv[u, :, bass.ds(turn, 1), :, :]).then_inc(x_in, 16)
                    for l in range(2):
                        for u in slots:
                            for i in range(2):
                                sp.wait_ge(sp_done, (l * SLOTS + u) * 2 + i + 1)
                                sp.dma_start(scr[l, u, i, :, :, :].rearrange("j p t -> p j t"),
                                             parts[u][i]).then_inc(st_wr[u], 16)
                            sp.wait_ge(st_wr[u], 32 * (l + 1))
                            if l:
                                sp.wait_ge(x_att, 2)
                            heads = scr[l, u, :, :, :, :].rearrange("i j (h d) t -> i j d h t", h=H)
                            base = 64 * u
                            for r, j in enumerate((0, 0, 0, 1, 1, 2)):
                                sp.dma_start(qst[base + 8 * r:base + 8 * r + 8, :, :],
                                             heads[0, j, :, :, :]).then_inc(st_rd[u], 16)
                            for r, j in enumerate((0, 1, 2, 0, 1, 0)):
                                sp.dma_start(kst[base + 8 * r:base + 8 * r + 8, :, :],
                                             heads[1, j, :, :, :]).then_inc(st_rd[u], 16)
                            sp.dma_start(kst32[base + KR:base + KM, :], ones).then_inc(st_rd[u], 16)
                        for n in range(NU):
                            u, g = divmod(n, NG)
                            sp.wait_ge(m_spl, l * NU + n + 1)
                            for j in range(3):
                                row = 64 * u + KR + j
                                sp.dma_start(qst[row:row + 1, GRP * g:GRP * g + GRP, :]
                                             .rearrange("o h (t c) -> o (h t) c", t=NT),
                                             m3[n % 2][:, j, :]).then_inc(m_row, 16)
                        if l == 0:
                            for u in slots:
                                sp.wait_ge(gt_row, u + 1)
                                sp.dma_start(scr_c[u, :, :], cbT[u][0:E, :]).then_inc(cb_wr, 16)
                                sp.wait_ge(cb_wr, 16 * (u + 1))
                                sp.dma_start(cb[u], scr_c[u, :, :].partition_broadcast(128)).then_inc(cb_rd[u], 16)
                    for u in slots:
                        sp.wait_ge(o_ev, u + 1)
                        sp.dma_start(ov[u, :, bass.ds(turn, 1), :, :],
                                     G[u][:, :].rearrange("p (o t c) -> p o t c", o=1, t=NT)).then_inc(o_dma, 16)
                    sp.wait_ge(o_dma, 16 * SLOTS)

                @block.tensor
                def _(pe):
                    mm = nc.tensor.matmul

                    def layer_norm(i, src, ready):
                        for u in slots:
                            ready(u)
                            mm(bank[u][:, :], K("center"), src[u][:, :], start=True, stop=True).then_inc(ln_cent, 1)
                        for u in slots:
                            k = i * SLOTS + u + 1
                            pe.wait_ge(ln_sq, k)
                            for t in range(NT):
                                r = mm(bank[2 + u][:, t:t + 1], SQ[u][:, t * 128:(t + 1) * 128], K("inv"),
                                       start=True, stop=True)
                            r.then_inc(ln_stat, 1)
                        for u in slots:
                            pe.wait_ge(ln_rstd, i * SLOTS + u + 1)
                            for t in range(NT):
                                r = mm(bank[4 + u][:, t * 128:(t + 1) * 128],
                                       rs[:, u, t:t + 1].to_broadcast([128, 128]), ident, start=True, stop=True)
                            r.then_inc(ln_bc, 1)

                    def to_rows(dst, src, k):
                        for t in range(NT):
                            r = nc.tensor.transpose(dst[0:k, t * 128:(t + 1) * 128], src[:, t * k:(t + 1) * k], ident)
                        return r

                    def attention(l):
                        lnk = (0, 2)[l] * SLOTS
                        pe.wait_ge(ln_xc, lnk + SLOTS)
                        for u in slots:
                            pe.wait_ge(ln_h, lnk + u + 1)
                            ws = (AW("q0"), AW("qr0"), AW("k0"), AW("kr0")) if l == 0 else (wqc[:, 0, :], wqc[:, 1, :])
                            vb = bank[(4, 1)[u]] if l == 0 else bank[4 + u]
                            for i, w in enumerate(ws):
                                if l == 0:
                                    if u and i == 0:
                                        pe.wait_ge(ln_h, lnk + SLOTS)
                                    if u and i == 3:
                                        pe.wait_ge(at_used, 1)
                                    dst = bank[(i, (5, 6, 7, 0)[i])[u]]
                                else:
                                    dst = bank[2 * u + i]
                                mm(dst[:, :], w, Hh[u][:, :], start=True, stop=True).then_inc(at_prod, 1)
                            if l == 0 and u:
                                pe.wait_ge(at_used, 2)
                            for t in range(NT):
                                r = mm(vb[:, t * 128:(t + 1) * 128], Hh[u][:, t * 128:(t + 1) * 128], AW(f"v{l}"),
                                       start=True, stop=True)
                            r.then_inc(at_prod, 1)
                        if l == 1:
                            for u in slots:
                                for i in range(2):
                                    pe.wait_ge(at_sq, 2 * u + i + 1)
                                    for t in range(NT):
                                        r = mm(bank[6 + u][:, (2 * t + i) * H:(2 * t + i + 1) * H],
                                               (SQ[u], G[u])[i][:, t * 128:(t + 1) * 128], K("blk16"),
                                               start=True, stop=True)
                                r.then_inc(at_stat, 1)
                            for u in slots:
                                pe.wait_ge(at_rs, u + 1)
                                to_rows(bank[6 + u], st128[:, u, :], 2 * H).then_inc(at_rt, 1)
                            for u in slots:
                                pe.wait_ge(at_rc, u + 1)
                                pe.wait_ge(at_v, SLOTS + u + 1)
                                for i in range(2):
                                    mm(bank[(4 + u, 6 + u)[i]][:, :], K("spread_h")[0:2 * H, i * 128:(i + 1) * 128],
                                       XC[u][0:2 * H, :], start=True, stop=True).then_inc(at_bc, 1)

                        def score_for_max(n, s):
                            u, g = divmod(n, NG)
                            hh, t = divmod(s, NT)
                            i = l * NU * 16 + n * 16 + s
                            if s == 0 and g == 0:
                                pe.wait_ge(st_rd[u], 13 * 16 * (l + 1))
                                if n == 0:
                                    pe.wait_ge(sp_done, (l * SLOTS + SLOTS) * 2)
                                    pe.wait_ge(at_v, (l + 1) * SLOTS)
                            if n * 16 + s >= 2:
                                pe.wait_ge(a_mx, i - 1)
                            h = GRP * g + hh
                            p = 64 * u
                            mm(bank[i % 2][:, :], qst[p:p + KR, h, t * 128:(t + 1) * 128], kst[p:p + KR, h, :],
                               start=True, stop=True).then_inc(a_mm, 1)

                        def transpose_max(n):
                            pe.wait_ge(a_mx, l * NU * 16 + (n + 1) * 16)
                            if n:
                                pe.wait_ge(m_spl, l * NU + n)
                            nc.tensor.transpose(bank[7][0:16, 0:128], mx[n % 2][:, :], ident).then_inc(m_tr, 1)

                        def score_minus_max(n, t, hh):
                            u, g = divmod(n, NG)
                            v = n * 16 + t * GRP + hh
                            if t == 0 and hh == 0:
                                pe.wait_ge(m_row, 48 * (l * NU + n + 1))
                            if v >= 4:
                                pe.wait_ge(e_done, l * NU * 16 + v - 3)
                            h = GRP * g + hh
                            p = 64 * u
                            mm(bank[2 + v % 4][:, :], kst[p:p + KM, h, t * 128:(t + 1) * 128], qst[p:p + KM, h, :],
                               start=True, stop=True).then_inc(s_mm, 1)

                        def weigh_values(n, t):
                            u, g = divmod(n, NG)
                            v = n * 16 + t * GRP
                            pe.wait_ge(e_done, l * NU * 16 + v + GRP)
                            if t == 0 and n:
                                pe.wait_ge(o_raw, l * NU + n)
                            for hh in range(GRP):
                                r = mm(bank[6][32 * hh:32 * hh + 16, :], vaug[u][:, t, GRP * g + hh, :],
                                       pt[(v + hh) % PTB], start=(t == 0), stop=(t == NT - 1))
                            r.then_inc(pv_done, 1)

                        for s in range(16):
                            score_for_max(0, s)
                        transpose_max(0)
                        for s in range(16):
                            score_for_max(1, s)
                        for n in range(NU):
                            for t in range(NT):
                                for hh in range(GRP):
                                    score_minus_max(n, t, hh)
                                    if n + 2 < NU:
                                        score_for_max(n + 2, t * GRP + hh)
                                if t == 1 and n + 1 < NU:
                                    transpose_max(n + 1)
                                if t:
                                    weigh_values(n, t - 1)
                                elif n:
                                    weigh_values(n - 1, NT - 1)
                        weigh_values(NU - 1, NT - 1)

                        for u in slots:
                            pe.wait_ge(o_raw, l * NU + (u + 1) * NG)
                            for g in range(NG):
                                for t in range(NT):
                                    a = (t * NG + g) * GRP
                                    r = mm(bank[u][:, a:a + GRP], raw[u][g][:, t * 128:(t + 1) * 128], K("sel4"),
                                           start=True, stop=True)
                            r.then_inc(den_mm, 1)
                        for u in slots:
                            pe.wait_ge(den_rec, l * SLOTS + u + 1)
                            to_rows(bank[2 + u], rec[:, u, :], H).then_inc(den_tr, 1)
                        for u in slots:
                            pe.wait_ge(den_cp, l * SLOTS + u + 1)
                            for g in range(NG):
                                k = l * NU + u * NG + g
                                if u * NG + g >= 4:
                                    pe.wait_ge(o_norm, k - 3)
                                mm(bank[4 + g][:, :], K("spread_o")[0:H, g * 128:(g + 1) * 128], XC[u][0:H, :],
                                   start=True, stop=True).then_inc(den_bc, 1)
                        for u in slots:
                            for g in range(NG):
                                pe.wait_ge(o_norm, l * NU + u * NG + g + 1)
                                r = mm(bank[u][:, :], AW(f"p{l}")[:, g * 128:(g + 1) * 128], raw[u][g],
                                       start=(g == 0), stop=(g == NG - 1))
                            r.then_inc(y_att, 1)

                    def moe():
                        pe.wait_ge(ln_xc, 2 * SLOTS)
                        for u in slots:
                            pe.wait_ge(ln_h, SLOTS + u + 1)
                            for t in range(NT):
                                r = mm(bank[u][:, t * E:(t + 1) * E], Hh[u][:, t * 128:(t + 1) * 128], MW("gate"),
                                       start=True, stop=True)
                            r.then_inc(gt_mm, 1)
                        for u in slots:
                            pe.wait_ge(gt_comb, u + 1)
                            for t in range(NT):
                                r = nc.tensor.transpose(bank[2 + u][0:E, t * 128:(t + 1) * 128], comb[u][:, t, :], ident)
                            r.then_inc(gt_tr, 1)

                        units = [(u, e, c) for u in slots for e in range(E + 1) for c in range(3)]

                        def down(m):
                            u, e, c = units[m]
                            pe.wait_ge(mo_hd, m + 1)
                            mm(bank[6 + u][:, :], MW("d")[0:CH[c], (3 * e + c) * 128:(3 * e + c + 1) * 128],
                               hd[m % 3][0:CH[c], :], start=(e == 0 and c == 0), stop=(e == E and c == 2)) \
                                .then_inc(mo_dn, 1)

                        pe.wait_ge(gt_row, SLOTS)
                        for m, (u, e, c) in enumerate(units):
                            p = 2 * (m % 3)
                            if m >= 3:
                                pe.wait_ge(mo_hd, m - 2)
                            a = e * HID + 128 * c
                            mm(bank[p][0:CH[c], :], MW("g")[:, a:a + CH[c]], Hh[u][:, :], start=True, stop=True) \
                                .then_inc(mo_g, 1)
                            if e and c == 0:
                                pe.wait_ge(hx_ready, u * E + e)
                            src = hx[(u * E + e - 1) % 3] if e else Hh[u][:, :]
                            mm(bank[p + 1][0:CH[c], :], MW("u")[:, a:a + CH[c]], src, start=True, stop=True) \
                                .then_inc(mo_u, 1)
                            if m >= 2:
                                down(m - 2)
                        down(len(units) - 2)
                        down(len(units) - 1)

                    def local_layer(d):
                        for u in slots:
                            pe.wait_ge(sh_ready, 2 * d * SLOTS + u + 1)
                            for i in range(8):
                                j = (d * SLOTS + u) * 8 + i
                                n, f = ("q", "k")[i // 4], i % 4
                                if u or i >= 2:
                                    pe.wait_ge(f_cp, j - 1)
                                    pe.wait_ge(f_t2, j - 1)
                                for w, dst, s in ((n, bank[2 * (i % 2)], f_main), (n + "r", bank[2 * (i % 2) + 1], f_rot)):
                                    mm(dst[:, :], FW(w, d)[:, f * 128:(f + 1) * 128], SH[u][:, :], start=True, stop=True) \
                                        .then_inc(s, 1)
                                if i:
                                    norm_sums(d, u, i - 1)
                                if i % 2:
                                    t = i // 2
                                    k = (d * SLOTS + u) * NT + t
                                    if u or t >= 2:
                                        pe.wait_ge(f_vc, k - 1)
                                    mm(bank[4 + t % 2][:, :], SH[u][:, t * 128:(t + 1) * 128], FW("v", d),
                                       start=True, stop=True).then_inc(f_v, 1)
                            norm_sums(d, u, 7)
                        for u in slots:
                            pe.wait_ge(f_rn, d * SLOTS + u + 1)
                            to_rows(bank[6 + u], st128[:, u, :], 16).then_inc(f_rt, 1)
                        for u in slots:
                            pe.wait_ge(f_rc, d * SLOTS + u + 1)
                            if u == 0:
                                pe.wait_ge(f_tt, (d + 1) * SLOTS * 8)
                                pe.wait_ge(f_cp, (d + 1) * SLOTS * 8)
                            for f in range(4):
                                if u:
                                    pe.wait_ge(f_kn, d * SLOTS * 4 + f + 1)
                                mm(bank[f][:, :], K("spread_n")[0:16, f * 128:(f + 1) * 128], XC[u][0:16, :],
                                   start=True, stop=True).then_inc(f_bc, 1)
                        NW = SLOTS * NT * 2
                        pe.wait_ge(f_kn, (d + 1) * SLOTS * 4)
                        pe.wait_ge(f_vc, (d + 1) * SLOTS * NT)

                        def scores(w):
                            u, t, hq = w // 8, w // 2 % 4, w % 2
                            lo = 0 if t else 64
                            if w >= 2:
                                pe.wait_ge(l_mk, 4 * (d * NW + w - 1))
                            for par in range(2):
                                for j in range(2):
                                    f, p = 2 * hq + j, 64 * par
                                    r = mm(bank[2 * (w % 2) + par][:, j * 192 + lo:j * 192 + 192],
                                           qk[u][p:p + 64, f, t * 128:(t + 1) * 128],
                                           qk[u][p:p + 64, 4 + f, t * 128 - 64 + lo:(t + 1) * 128], start=True, stop=True)
                                r.then_inc(l_s, 1)

                        def transposes(w):
                            t = w // 2 % 4
                            pe.wait_ge(l_p, d * NW + w + 1)
                            if w:
                                pe.wait_ge(l_ev, d * NW + w)
                            for par in range(2):
                                for j in range(2):
                                    a = (2 * par + j) * 128
                                    r = nc.tensor.transpose(bank[4][:, a:a + 128], pr[w % 3][:, par, j, 128:256], ident)
                                    if t:
                                        r = nc.tensor.transpose(bank[5][:, a:a + 128], pr[w % 3][:, par, j, 0:128], ident)
                            r.then_inc(l_tr, 1)

                        def values(w):
                            u, t, hq = w // 8, w // 2 % 4, w % 2
                            pe.wait_ge(l_ev, d * NW + w + 1)
                            if hq == 0 and w >= 4:
                                pe.wait_ge(l_o, (d * NW + w) // 2 - 1)
                            for par in range(2):
                                for j in range(2):
                                    h, f, a = 4 * hq + 2 * j + par, 2 * hq + j, (2 * par + j) * 128
                                    o = bank[6 + w // 2 % 2][64 * par:64 * par + 64, f * 128:(f + 1) * 128]
                                    r = mm(o, vv[u][:, t, h * LD:(h + 1) * LD], ptc[w % 2][:, a:a + 128],
                                           start=True, stop=(t == 0))
                                    if t:
                                        r = mm(o, vv[u][64:128, t - 1, h * LD:(h + 1) * LD],
                                               ptp[w % 2][64:128, a:a + 128], start=False, stop=True)
                            r.then_inc(l_pv, 1)

                        scores(0)
                        scores(1)
                        for w in range(NW):
                            transposes(w)
                            if w + 2 < NW:
                                scores(w + 2)
                            if w:
                                values(w - 1)
                        values(NW - 1)
                        for u in slots:
                            pe.wait_ge(l_o, (d * NW + (u + 1) * 8) // 2)
                            for f in range(4):
                                r = mm(bank[u][:, :], FW("wo", d)[:, f * 128:(f + 1) * 128], qk[u][:, f, :],
                                       start=(f == 0), stop=(f == 3))
                            r.then_inc(wo_mm, 1)
                        layer_norm(4 + d, SH, lambda u: pe.wait_ge(sh_ready, (2 * d + 1) * SLOTS + u + 1))
                        units = [(u, c) for u in slots for c in range(3)]

                        def down(m):
                            u, c = units[m]
                            pe.wait_ge(w1_hd, d * 6 + m + 1)
                            r = mm(bank[6 + u][:, :], FW("w2", d)[0:GC[c], c * 128:(c + 1) * 128],
                                   ghd[m % 2][0:GC[c], :], start=(c == 0), stop=(c == 2))
                            r.then_inc(w2_mm, 1)

                        pe.wait_ge(ln_xc, (5 + d) * SLOTS)
                        for m, (u, c) in enumerate(units):
                            if c == 0:
                                pe.wait_ge(ln_h, (4 + d) * SLOTS + u + 1)
                            if m >= 2:
                                pe.wait_ge(w1_hd, d * 6 + m - 1)
                            for k in range(2):
                                mm(bank[2 * (m % 2) + k][0:GC[c], :],
                                   FW("w1", d)[:, k * GH + 128 * c:k * GH + 128 * c + GC[c]], G[u][:, :],
                                   start=True, stop=True).then_inc(w1_mm, 1)
                            if m >= 1:
                                down(m - 1)
                        down(5)

                    def norm_sums(d, u, i):
                        pe.wait_ge(f_sq, (d * SLOTS + u) * 8 + i + 1)
                        for t in range(NT):
                            a = (t * 8 + i) * 2
                            r = mm(bank[6 + u][:, a:a + 2], sqr[i % 2][:, t * 128:(t + 1) * 128], K("blk2"),
                                   start=True, stop=True)
                        r.then_inc(f_stat, 1)

                    for u in slots:
                        pe.wait_ge(x_in, 16 * SLOTS)
                        for t in range(NT):
                            r = nc.tensor.transpose(bank[6 + u][:, t * 128:(t + 1) * 128], xin[u][:, 0, t, :], ident)
                        r.then_inc(x_tr, 1)
                    layer_norm(0, X, lambda u: pe.wait_ge(x_ready, u + 1))
                    attention(0)
                    layer_norm(1, X, lambda u: pe.wait_ge(x_att, u + 1))
                    moe()
                    layer_norm(2, X, lambda u: pe.wait_ge(x_moe, u + 1))
                    attention(1)
                    layer_norm(3, X, lambda u: pe.wait_ge(x_att, SLOTS + u + 1))
                    for d in range(DEPTH):
                        local_layer(d)
                    for u in slots:
                        pe.wait_ge(x_last, u + 1)
                        for t in range(NT):
                            r = nc.tensor.transpose(bank[u][:, t * 128:(t + 1) * 128], X[u][:, t * 128:(t + 1) * 128], ident)
                        r.then_inc(o_tr, 1)

                @block.scalar
                def _(act):
                    fn = nc.scalar.activation

                    def layer_norm(i):
                        for u in slots:
                            act.wait_ge(ln_cent, i * SLOTS + u + 1)
                            fn(SQ[u][:, :], bank[u][:, :], ACT.Square).then_inc(ln_sq, 1)
                            fn(XC[u][:, :], bank[u][:, :], ACT.Copy).then_inc(ln_xc, 1)

                    def attention(l):
                        per = 5 if l == 0 else 3
                        base = 5 * SLOTS * l
                        for u in slots:
                            if l == 1:
                                for i in range(2):
                                    act.wait_ge(at_prod, base + per * u + i + 1)
                                    fn((SQ[u], G[u])[i][:, :], bank[2 * u + i][:, :], ACT.Square).then_inc(at_sq, 1)
                                    fn((qf, kf)[i][u], bank[2 * u + i][:, :], ACT.Copy).then_inc(at_f, 1)
                            act.wait_ge(at_prod, base + per * (u + 1))
                            act.wait_ge(vaug_one, l * SLOTS + u + 1)
                            vb = bank[(4, 1)[u]] if l == 0 else bank[4 + u]
                            fn(vaug[u][:, :, :, 0:DH].rearrange("p t h c -> p (t h) c"),
                               vb[:, :].rearrange("p (a c) -> p a c", c=DH), ACT.Copy).then_inc(at_v, 1)
                        if l == 1:
                            for u in slots:
                                act.wait_ge(at_ve, u + 1)
                                fn(st128[:, u, :], st128[:, u, :], ACT.Sqrt).then_inc(at_sd, 1)
                            for u in slots:
                                act.wait_ge(at_rt, u + 1)
                                fn(XC[u][0:2 * H, :], bank[6 + u][0:2 * H, :], ACT.Copy).then_inc(at_rc, 1)
                        for u in slots:
                            for i in range(2):
                                k = (l * SLOTS + u) * 2 + i
                                act.wait_ge(sp_hi, k + 1)
                                fn(parts[u][i][:, 0, :], (qf, kf)[i][u], ACT.Copy).then_inc(sp_first, 1)
                                act.wait_ge(sp_r, k + 1)
                                fn(parts[u][i][:, 1, :], rem[u], ACT.Copy).then_inc(sp_mid, 1)
                        for n in range(NU):
                            for t in range(NT):
                                for hh in range(GRP):
                                    v = n * 16 + t * GRP + hh
                                    act.wait_ge(s_mm, l * NU * 16 + v + 1)
                                    if v >= PTB:
                                        act.wait_ge(pv_done, l * NU * NT + (v - PTB) // GRP + 1)
                                    fn(pt[v % PTB], bank[2 + v % 4][:, :], ACT.Exp, scale=float(DH) ** -0.5) \
                                        .then_inc(e_done, 1)
                                if t == 1 and n:
                                    evacuate(l, n - 1)
                        evacuate(l, NU - 1)
                        for u in slots:
                            act.wait_ge(den_tr, l * SLOTS + u + 1)
                            fn(XC[u][0:H, :], bank[2 + u][0:H, :], ACT.Copy).then_inc(den_cp, 1)
                        for u in slots:
                            act.wait_ge(y_att, l * SLOTS + u + 1)
                            fn(XC[u][:, :], bank[u][:, :], ACT.Identity, scale=MOD(l, 2, u), bias=MOD(l, 6, u)) \
                                .then_inc(t_att, 1)

                    def evacuate(l, n):
                        u, g = divmod(n, NG)
                        act.wait_ge(pv_done, (l * NU + n + 1) * NT)
                        fn(raw[u][g], bank[6][:, :], ACT.Copy).then_inc(o_raw, 1)

                    def moe():
                        for u in slots:
                            act.wait_ge(gt_sub, u + 1)
                            fn(lg[u][:, :, :], lg[u][:, :, :], ACT.Exp).then_inc(gt_exp, 1)
                        for u in slots:
                            act.wait_ge(gt_tr, u + 1)
                            fn(cbT[u][0:E, :], bank[2 + u][0:E, :], ACT.Copy).then_inc(gt_row, 1)
                        for m in range(SLOTS * (E + 1) * 3):
                            c = CH[m % 3]
                            act.wait_ge(mo_g, m + 1)
                            if m >= 3:
                                act.wait_ge(mo_hd, m - 2)
                            fn(sl[m % 3][0:c, :], bank[2 * (m % 3)][0:c, :], ACT.Silu).then_inc(mo_sl, 1)

                    def local_layer(d):
                        for u in slots:
                            for i in range(8):
                                j = (d * SLOTS + u) * 8 + i
                                act.wait_ge(f_main, j + 1)
                                if u or i >= 2:
                                    act.wait_ge(f_t1, j - 1)
                                    act.wait_ge(f_stat, j - 1)
                                fn(qs[i % 2], bank[2 * (i % 2)][:, :], ACT.Copy).then_inc(f_cp, 1)
                                act.wait_ge(f_cp, j + 1)
                                fn(sqr[i % 2], qs[i % 2], ACT.Square).then_inc(f_sq, 1)
                                if i % 2:
                                    t = i // 2
                                    act.wait_ge(f_v, (d * SLOTS + u) * NT + t + 1)
                                    fn(vv[u][:, t, :], bank[4 + t % 2][:, :], ACT.Copy).then_inc(f_vc, 1)
                        for u in slots:
                            act.wait_ge(f_n2, d * SLOTS + u + 1)
                            fn(st128[:, u, 0:64], st128[:, u, 0:64], ACT.Sqrt).then_inc(f_sd, 1)
                        for u in slots:
                            act.wait_ge(f_rt, d * SLOTS + u + 1)
                            fn(XC[u][0:16, :], bank[6 + u][0:16, :], ACT.Copy).then_inc(f_rc, 1)
                        NW = SLOTS * NT * 2

                        def transposed(w):
                            t = w // 2 % 4
                            act.wait_ge(l_tr, d * NW + w + 1)
                            if w >= 2:
                                act.wait_ge(l_pv, d * NW + w - 1)
                            if t:
                                fn(ptp[w % 2][64:128, :], bank[5][64:128, :], ACT.Copy).then_inc(l_evp, 1)
                            fn(ptc[w % 2], bank[4][:, :], ACT.Copy).then_inc(l_ev, 1)

                        def output(w):
                            u, t = w // 8, w // 2 % 4
                            act.wait_ge(l_pv, d * NW + w + 1)
                            fn(qk[u][:, 0:4, t * 128:(t + 1) * 128],
                               bank[6 + w // 2 % 2][:, :].rearrange("p (f t) -> p f t", f=4), ACT.Copy).then_inc(l_o, 1)

                        for w in range(NW):
                            t = w // 2 % 4
                            lo = 64 if t else 128
                            act.wait_ge(l_nm, d * NW + w + 1)
                            for par in range(2):
                                for j in range(2):
                                    p = pr[w % 3][:, par, j, lo:256]
                                    fn(p, p, ACT.Exp, scale=8.0, bias=lm[w % 3][:, par, j:j + 1],
                                       accum_out=lsum[w % 3][:, par, j:j + 1]).then_inc(l_ex, 1)
                            if w:
                                transposed(w - 1)
                            if w % 2 and w > 2:
                                output(w - 2)
                        transposed(NW - 1)
                        output(NW - 1)
                        layer_norm(4 + d)
                        for m in range(6):
                            c = m % 3
                            act.wait_ge(w1_mm, 2 * (d * 6 + m + 1))
                            if m >= 2:
                                act.wait_ge(w1_hd, d * 6 + m - 1)
                            fn(glu[m % 2][0:GC[c], :], bank[2 * (m % 2) + 1][0:GC[c], :], ACT.Gelu,
                               bias=V_(f"b1{d}")[0:GC[c], 3 + c:4 + c]).then_inc(w1_gl, 1)

                    for u in slots:
                        act.wait_ge(x_tr, u + 1)
                        fn(X[u][:, :], bank[6 + u][:, :], ACT.Copy).then_inc(x_ready, 1)
                    layer_norm(0)
                    attention(0)
                    layer_norm(1)
                    moe()
                    layer_norm(2)
                    attention(1)
                    layer_norm(3)
                    for d in range(DEPTH):
                        local_layer(d)
                    for u in slots:
                        act.wait_ge(o_tr, u + 1)
                        fn(G[u][:, :], bank[u][:, :], ACT.Copy).then_inc(o_ev, 1)

                @block.vector
                def _(dve):
                    tt, ts, stt = nc.vector.tensor_tensor, nc.vector.tensor_scalar, nc.vector.scalar_tensor_tensor
                    links = [0]

                    def link(ins):
                        links[0] += 1
                        ins.then_inc(dve_link, 1)
                        dve.wait_ge(dve_link, links[0])

                    def layer_norm(i, dst, scale, shift):
                        for u in slots:
                            dve.wait_ge(ln_stat, i * SLOTS + u + 1)
                            ts(ve[:, u, :], bank[2 + u][:, 0:NT], 1e-5, None, ALU.add).then_inc(ln_var, 1)
                        for u in slots:
                            dve.wait_ge(ln_xc, i * SLOTS + u + 1)
                            dve.wait_ge(ln_bc, i * SLOTS + u + 1)
                            link(tt(XC[u][:, :], XC[u][:, :], bank[4 + u][:, :], ALU.mult))
                            ts(dst[u][:, :], XC[u][:, :], scale(u), shift(u), ALU.mult, ALU.add).then_inc(ln_h, 1)

                    def attention(l):
                        for u in slots:
                            if l == 0:
                                base = 5 * u
                                for i in range(2):
                                    mb, rb = (bank[2 * i], bank[2 * i + 1]) if u == 0 else \
                                        ((bank[5], bank[6]), (bank[7], bank[0]))[i]
                                    f = (qf, kf)[i][u]
                                    dve.wait_ge(at_prod, base + 2 * i + 1)
                                    tt(f, mb[:, :], K("cos"), ALU.mult).then_inc(at_used, 1)
                                    dve.wait_ge(at_prod, base + 2 * i + 2)
                                    if i:
                                        dve.wait_ge(sp_hi, 2 * u + 1)
                                    tt(ropet[u], rb[:, :], K("sin"), ALU.mult).then_inc(at_used, 1)
                                    dve.wait_ge(at_used, (u * 2 + i) * 2 + 2)
                                    tt(f, f, ropet[u], ALU.add).then_inc(sp_hi, 1)
                            else:
                                dve.wait_ge(at_stat, u + 1)
                                ts(st128[:, u, :], bank[6 + u][:, 0:128], 1e-5, None, ALU.add).then_inc(at_ve, 1)
                        if l == 1:
                            for u in slots:
                                dve.wait_ge(at_sd, u + 1)
                                nc.vector.reciprocal(st128[:, u, :], st128[:, u, :]).then_inc(at_rs, 1)
                            for u in slots:
                                for i in range(2):
                                    dve.wait_ge(at_f, 2 * u + i + 1)
                                    dve.wait_ge(at_bc, 2 * u + i + 1)
                                    f = (qf, kf)[i][u]
                                    link(tt(f, f, bank[(4 + u, 6 + u)[i]][:, :], ALU.mult))
                                    ts(f, f, V_(("qg", "kg")[i]), V_(("qb", "kb")[i]), ALU.mult, ALU.add) \
                                        .then_inc(sp_hi, 1)
                        for u in slots:
                            for i in range(2):
                                k = (l * SLOTS + u) * 2 + i
                                f = (qf, kf)[i][u]
                                dve.wait_ge(sp_first, k + 1)
                                if i:
                                    dve.wait_ge(sp_done, k)
                                tt(rem[u], f, parts[u][i][:, 0, :], ALU.subtract).then_inc(sp_r, 1)
                                dve.wait_ge(sp_mid, k + 1)
                                tt(parts[u][i][:, 2, :], rem[u], parts[u][i][:, 1, :], ALU.subtract).then_inc(sp_done, 1)

                        def maxima(n, steps):
                            for s in steps:
                                i = l * NU * 16 + n * 16 + s
                                dve.wait_ge(a_mm, i + 1)
                                nc.vector.tensor_reduce(mx[n % 2][:, s:s + 1], bank[i % 2][:, :], axis=AX.X,
                                                        op=ALU.max).then_inc(a_mx, 1)

                        def split_max(n):
                            dve.wait_ge(m_tr, l * NU + n + 1)
                            k = l * NU + n
                            if k >= 2:
                                dve.wait_ge(m_row, 48 * (k - 1))
                            m, t = m3[n % 2], bank[7][0:16, 0:128]
                            link(ts(m[:, 0, :], t, -1.0, None, ALU.mult))
                            link(stt(mneg[:, :], t, -1.0, m[:, 0, :], ALU.mult, ALU.subtract))
                            link(nc.vector.tensor_copy(m[:, 1, :], mneg[:, :]))
                            tt(m[:, 2, :], mneg[:, :], m[:, 1, :], ALU.subtract).then_inc(m_spl, 1)

                        maxima(0, range(16))
                        split_max(0)
                        maxima(1, range(16))
                        for n in range(NU):
                            if n + 2 < NU:
                                maxima(n + 2, range(8))
                            if n + 1 < NU:
                                split_max(n + 1)
                            if n + 2 < NU:
                                maxima(n + 2, range(8, 16))
                        for u in slots:
                            dve.wait_ge(den_mm, l * SLOTS + u + 1)
                            nc.vector.reciprocal(rec[:, u, :], bank[u][:, 0:NG * NT * GRP]).then_inc(den_rec, 1)
                        for u in slots:
                            for g in range(NG):
                                dve.wait_ge(den_bc, l * NU + u * NG + g + 1)
                                tt(raw[u][g], raw[u][g], bank[4 + g][:, :], ALU.mult).then_inc(o_norm, 1)
                        for u in slots:
                            dve.wait_ge(t_att, l * SLOTS + u + 1)
                            tt(X[u][:, :], X[u][:, :], XC[u][:, :], ALU.add).then_inc(x_att, 1)

                    def moe():
                        one = lambda a, n: a.unsqueeze(2).to_broadcast([128, NT, n])
                        for u in slots:
                            dve.wait_ge(gt_mm, u + 1)
                            p = bank[u][:, 0:NT * E].rearrange("p (t e) -> p t e", t=NT)
                            link(nc.vector.tensor_reduce(s4[u], p, axis=AX.X, op=ALU.max))
                            tt(lg[u][:, :, :], p, one(s4[u], E), ALU.subtract).then_inc(gt_sub, 1)
                        for u in slots:
                            dve.wait_ge(gt_exp, u + 1)
                            l3 = lg[u][:, :, :]
                            link(nc.vector.tensor_reduce(s4[u], l3, axis=AX.X, op=ALU.add))
                            link(nc.vector.reciprocal(s4[u], s4[u]))
                            link(tt(l3, l3, one(s4[u], E), ALU.mult))
                            for t in range(NT):
                                link(nc.vector.max(top[u][:, t, :], lg[u][:, t, :]))
                            for t in range(NT):
                                link(nc.vector.max_index(topi[u][:, t, :], top[u][:, t, :], lg[u][:, t, :]))
                            link(nc.vector.tensor_copy(topf[u][:, :, :], topi[u][:, :, :]))
                            link(tt(s4[u], top[u][:, :, 0], top[u][:, :, 1], ALU.add))
                            link(ts(s4[u], s4[u], 1e-20, None, ALU.add))
                            link(nc.vector.reciprocal(s4[u], s4[u]))
                            link(tt(w2v[u][:, :, :], top[u][:, :, 0:2], one(s4[u], 2), ALU.mult))
                            io = K("iota8").unsqueeze(1).to_broadcast([128, NT, E])
                            for j, dst in enumerate((comb[u], c2[u])):
                                link(tt(dst[:, :, :], io, one(topf[u][:, :, j], E), ALU.is_equal))
                                link(tt(dst[:, :, :], dst[:, :, :], one(w2v[u][:, :, j], E), ALU.mult))
                            tt(comb[u][:, :, :], comb[u][:, :, :], c2[u][:, :, :], ALU.add).then_inc(gt_comb, 1)
                        for m in range(SLOTS * (E + 1) * 3):
                            c = CH[m % 3]
                            dve.wait_ge(mo_sl, m + 1)
                            dve.wait_ge(mo_u, m + 1)
                            if m >= 3:
                                dve.wait_ge(mo_dn, m - 2)
                            tt(hd[m % 3][0:c, :], sl[m % 3][0:c, :], bank[2 * (m % 3) + 1][0:c, :], ALU.mult) \
                                .then_inc(mo_hd, 1)
                            if m % 27 == 26:
                                u = m // 27
                                dve.wait_ge(mo_dn, m + 1)
                                stt(X[u][:, :], bank[6 + u][:, :], MOD(0, 5, u), X[u][:, :], ALU.mult, ALU.add) \
                                    .then_inc(x_moe, 1)

                    def shift(first_of_turn, ready):
                        for u in slots:
                            ready(u)
                            link(nc.vector.tensor_copy(SH[u][0:64, :], Hh[u][0:64, :]))
                            nc.vector.tensor_copy(SH[u][64:128, 1:S], Hh[u][64:128, 0:S - 1]).then_inc(sh_ready, 1)

                    def local_layer(d):
                        if d == 0:
                            shift(True, lambda u: dve.wait_ge(ln_h, 3 * SLOTS + u + 1))
                        else:
                            shift(False, lambda u: dve.wait_ge(z_ffn, (d - 1) * SLOTS + u + 1))
                        for i, (t, s) in enumerate((("xa", "qs"), ("xb", "qsr"), ("xai", "ks"), ("xbi", "ksr"))):
                            ts(tab[:, i, :], K(t), V_(f"{s}{d}"), None, ALU.mult).then_inc(tb_ready, 1)
                        dve.wait_ge(tb_ready, 4 * (d + 1))
                        for u in slots:
                            for i in range(8):
                                j = (d * SLOTS + u) * 8 + i
                                dve.wait_ge(f_rot, j + 1)
                                tt(qk[u][:, i, :], bank[2 * (i % 2) + 1][:, :], tab[:, 2 * (i // 4) + 1, :], ALU.mult) \
                                    .then_inc(f_t2, 1)
                                dve.wait_ge(f_t1, j + 1)
                                dve.wait_ge(f_t2, j + 1)
                                tt(qk[u][:, i, :], qk[u][:, i, :], xt[i % 2], ALU.add).then_inc(f_tt, 1)
                        for u in slots:
                            dve.wait_ge(f_stat, (d * SLOTS + u + 1) * 8)
                            ts(st128[:, u, 0:64], bank[6 + u][:, 0:64], 1e-24, None, ALU.max).then_inc(f_n2, 1)
                        for u in slots:
                            dve.wait_ge(f_sd, d * SLOTS + u + 1)
                            nc.vector.reciprocal(st128[:, u, 0:64], st128[:, u, 0:64]).then_inc(f_rn, 1)
                        for u in slots:
                            for f in range(4):
                                dve.wait_ge(f_bc, (d * SLOTS + u) * 4 + f + 1)
                                tt(qk[u][:, 4 + f, :], qk[u][:, 4 + f, :], bank[f][:, :], ALU.mult).then_inc(f_kn, 1)
                        NW = SLOTS * NT * 2

                        def masked(w):
                            u, t, hq = w // 8, w // 2 % 4, w % 2
                            lo = 0 if t else 64
                            dve.wait_ge(l_s, 2 * (d * NW + w + 1))
                            if w >= 3:
                                dve.wait_ge(l_tr, d * NW + w - 2)
                            for par in range(2):
                                for j in range(2):
                                    a = (t * 8 + 2 * hq + j) * 2 + par
                                    stt(pr[w % 3][:, par, j, 64 + lo:256],
                                        bank[2 * (w % 2) + par][:, j * 192 + lo:j * 192 + 192],
                                        st128[:, u, a:a + 1], K("mask")[:, lo:192], ALU.mult, ALU.add).then_inc(l_mk, 1)
                            dve.wait_ge(l_mk, 4 * (d * NW + w + 1))
                            link(nc.vector.tensor_reduce(lm[w % 3][:, :, :], pr[w % 3][:, :, :, 64 + lo:256],
                                                         axis=AX.X, op=ALU.max))
                            ts(lm[w % 3][:, :, :], lm[w % 3][:, :, :], -8.0, None, ALU.mult).then_inc(l_nm, 1)

                        def normalise(w):
                            t = w // 2 % 4
                            lo = 64 if t else 128
                            dve.wait_ge(l_ex, 4 * (d * NW + w + 1))
                            link(nc.vector.reciprocal(lrec[w % 3][:, :, :], lsum[w % 3][:, :, :]))
                            for par in range(2):
                                for j in range(2):
                                    p = pr[w % 3][:, par, j, lo:256]
                                    r = ts(p, p, lrec[w % 3][:, par, j:j + 1], None, ALU.mult)
                            r.then_inc(l_p, 1)

                        masked(0)
                        for w in range(NW):
                            if w + 1 < NW:
                                masked(w + 1)
                            normalise(w)
                        for u in slots:
                            dve.wait_ge(wo_mm, d * SLOTS + u + 1)
                            tt(Hh[u][:, :], Hh[u][:, :], bank[u][:, :], ALU.add).then_inc(z_att, 1)
                        shift(False, lambda u: dve.wait_ge(z_att, d * SLOTS + u + 1))
                        layer_norm(4 + d, G, lambda u: V_(f"lg{d}"), lambda u: V_(f"lb{d}"))
                        for m in range(6):
                            u, c = divmod(m, 3)
                            dve.wait_ge(w1_gl, d * 6 + m + 1)
                            if m >= 2:
                                dve.wait_ge(w2_mm, d * 6 + m - 1)
                            stt(ghd[m % 2][0:GC[c], :], bank[2 * (m % 2)][0:GC[c], :], V_(f"b1{d}")[0:GC[c], c:c + 1],
                                glu[m % 2][0:GC[c], :], ALU.add, ALU.mult).then_inc(w1_hd, 1)
                        for u in slots:
                            dve.wait_ge(w2_mm, d * 6 + 3 * (u + 1))
                            stt(Hh[u][:, :], bank[6 + u][:, :], V_(f"b2{d}"), Hh[u][:, :], ALU.add, ALU.add) \
                                .then_inc(z_ffn, 1)

                    nc.vector.tensor_copy(modu[:, :, :], mod[:, :, bass.ts(turn, SLOTS)]).then_inc(mod_ready, 1)
                    dve.wait_ge(mod_ready, 1)
                    layer_norm(0, Hh, lambda u: MOD(0, 1, u), lambda u: MOD(0, 0, u))
                    attention(0)
                    layer_norm(1, Hh, lambda u: MOD(0, 4, u), lambda u: MOD(0, 3, u))
                    moe()
                    layer_norm(2, Hh, lambda u: MOD(1, 1, u), lambda u: MOD(1, 0, u))
                    attention(1)
                    layer_norm(3, Hh, lambda u: MOD(1, 4, u), lambda u: MOD(1, 3, u))
                    for d in range(DEPTH):
                        local_layer(d)
                    for u in slots:
                        dve.wait_ge(z_ffn, (DEPTH - 1) * SLOTS + u + 1)
                        stt(X[u][:, :], Hh[u][:, :], MOD(1, 5, u), X[u][:, :], ALU.mult, ALU.add).then_inc(x_last, 1)

                @block.gpsimd
                def _(pool):
                    tt = nc.gpsimd.tensor_tensor

                    def layer_norm(i):
                        for u in slots:
                            pool.wait_ge(ln_var, i * SLOTS + u + 1)
                            tt(rs[:, u, :], ve[:, u, :], mhalf[:, :], ALU.pow).then_inc(ln_rstd, 1)

                    def value_tiles(l):
                        for u in slots:
                            nc.gpsimd.memset(vaug[u], 0.0).then_inc(zeroed, 1)
                            pool.wait_ge(zeroed, l * SLOTS + u + 1)
                            nc.gpsimd.memset(vaug[u][:, :, :, DH:DH + 1], 1.0).then_inc(vaug_one, 1)

                    layer_norm(0)
                    value_tiles(0)
                    layer_norm(1)
                    for m in range(SLOTS * E):
                        u, e = divmod(m, E)
                        pool.wait_ge(cb_rd[u], 16)
                        if m >= 3:
                            mu, me = divmod(m - 3, E)
                            pool.wait_ge(mo_u, mu * 27 + 3 * (me + 2))
                        tt(hx[m % 3], Hh[u][:, :], cb[u][:, e, :], ALU.mult).then_inc(hx_ready, 1)
                    layer_norm(2)
                    value_tiles(1)
                    layer_norm(3)
                    for d in range(DEPTH):
                        for u in slots:
                            for i in range(8):
                                j = (d * SLOTS + u) * 8 + i
                                pool.wait_ge(tb_ready, 4 * (d + 1))
                                pool.wait_ge(f_cp, j + 1)
                                if u or i >= 2:
                                    pool.wait_ge(f_tt, j - 1)
                                tt(xt[i % 2], qs[i % 2], tab[:, 2 * (i // 4), :], ALU.mult).then_inc(f_t1, 1)
                        layer_norm(4 + d)
            nc.gpsimd.sem_clear(range(first, last + 1))
            nc.all_engine_barrier()


def lay_out(v):
    f = {k: np.asarray(a) for k, a in v.items()}

    def pad(a, rows):
        out = np.zeros((rows,) + a.shape[1:], a.dtype)
        out[:a.shape[0]] = a
        return out

    def swapped(w, width):
        return np.roll(w.reshape(w.shape[0], -1, width), width // 2, axis=2).reshape(w.shape)

    att = {}
    w = f["L0_attn_w_qkv"]
    att["q0"], att["k0"], att["v0"] = w[:, :C], w[:, C:2 * C], w[:, 2 * C:]
    att["qr0"], att["kr0"] = swapped(att["q0"], DH), swapped(att["k0"], DH)
    w = f["L1_attn_w_qkv"]
    att["qT1"], att["kT1"], att["v1"] = w[:, :C].T, w[:, C:2 * C].T, w[:, 2 * C:]
    for l in range(2):
        wp = f[f"L{l}_attn_w_proj"].reshape(NG, GRP, DH, C)
        out = np.zeros((GRP, 32, NG, C), wp.dtype)
        out[:, :DH] = wp.transpose(1, 2, 0, 3)
        att[f"p{l}"] = out.reshape(128, NG * C)
    att_w = np.concatenate([att[n] for n, _ in ATT_SIZES], axis=1)

    moe = {"gate": f["L0_ffn_gate_w"].T}
    for n, s_, e_ in (("g", "shared_gate", "expert_gate"), ("u", "shared_up", "expert_up")):
        w = np.concatenate([f["L0_ffn_" + s_][None], f["L0_ffn_" + e_]])
        moe[n] = w.transpose(2, 0, 1).reshape(C, -1)
    w = np.concatenate([f["L0_ffn_shared_down"][None], f["L0_ffn_expert_down"]]).transpose(2, 0, 1)
    moe["d"] = pad(w, 384).reshape(3, 128, E + 1, C).transpose(1, 2, 0, 3).reshape(128, -1)
    moe_w = np.concatenate([moe[n] for n, _ in MOE_SIZES], axis=1)

    ffn, vec = {}, {}
    twice = lambda a: np.concatenate([a, a])
    col = lambda a: a.reshape(-1, 1)
    for d in range(DEPTH):
        w = f["L1_ffn_wqkv"][d]
        q, k, ffn[f"v{d}"] = w[:, :QKV], w[:, QKV:2 * QKV], w[:, 2 * QKV:]
        ffn[f"q{d}"], ffn[f"qr{d}"] = q, swapped(q, LD)
        ffn[f"k{d}"], ffn[f"kr{d}"] = k, swapped(k, LD)
        ffn[f"wo{d}"] = f["L1_ffn_wo"][d].reshape(4, 128, C).transpose(1, 0, 2).reshape(128, -1)
        ffn[f"w1{d}"] = f["L1_ffn_w1"][d]
        ffn[f"w2{d}"] = pad(f["L1_ffn_w2"][d], 384).reshape(3, 128, C).transpose(1, 0, 2).reshape(128, -1)
        for n, src in (("qs", "q_scale"), ("ks", "k_scale")):
            a = f["L1_ffn_" + src][d]
            vec[f"{n}{d}"] = col(twice(a))
            vec[f"{n}r{d}"] = col(twice(np.roll(a, LD // 2)))
        vec[f"lg{d}"], vec[f"lb{d}"] = col(f["L1_ffn_ln_g"][d]), col(f["L1_ffn_ln_b"][d])
        b1 = f["L1_ffn_b1"][d]
        vec[f"b1{d}"] = np.concatenate([pad(b1[k * GH:(k + 1) * GH], 384).reshape(3, 128) for k in range(2)]).T
        vec[f"b2{d}"] = col(f["L1_ffn_b2"][d])
    vec["bproj"] = col(f["L0_attn_b_proj"])
    for n, src in (("qg", "q_gamma"), ("qb", "q_beta"), ("kg", "k_gamma"), ("kb", "k_beta")):
        vec[n] = col(np.tile(f["L1_attn_" + src], H))
    ffn_w = np.concatenate([ffn[n] for n, _ in FFN_SIZES], axis=1)
    vec = np.concatenate([vec[n] for n, _ in VEC_SIZES], axis=1)
    cT = np.concatenate([f["L0_c"].T, f["L1_c"].T], axis=1)
    wmod = np.stack([f["L0_wmod"], f["L1_wmod"]])
    ones = np.full((3, H * S // 2), 0x3F803F80, np.uint32).view(np.float32)
    return {"x": f["L0_attn_x"], "consts": constants(), "ones": ones, "att_w": att_w, "moe_w": moe_w,
            "ffn_w": ffn_w, "vec": vec, "cT": cT, "wmod": wmod}


def kernel(**inputs):
    import concourse.bacc as bacc
    from concourse.bass_utils import run_bass_kernel_spmd

    nc = bacc.Bacc("TRN2", target_bir_lowering=False, num_devices=1)
    arrays, args = {}, []
    for name, a in lay_out(inputs).items():
        a = np.ascontiguousarray(a)
        arrays[f"in_{name}"] = a
        args.append(nc.dram_tensor(f"in_{name}", a.shape, mybir.dt.from_np(a.dtype), kind="ExternalInput").ap())
    args.append(nc.dram_tensor("out", (B, S, C), F32, kind="ExternalOutput").ap())
    adaln_kernel(nc, *args)
    return run_bass_kernel_spmd(nc, [arrays], core_ids=[0]).results[0]["out"]
```

```python
import numpy as np
import concourse.bass as bass
from concourse import mybir
from contextlib import ExitStack

F32 = mybir.dt.float32
BF16 = mybir.dt.bfloat16
U32 = mybir.dt.uint32
ALU = mybir.AluOpType
ACT = mybir.ActivationFunctionType
AX = mybir.AxisListType

B, S, C = 8, 512, 128
SLOTS = 2
NT = S // 128
H, DH = 16, 8
GRP = 4
NG = H // GRP
E, HID = 8, 352
CH = [128, 128, 96]
LH, LD, WIN = 8, 64, 64
DEPTH = 2
GH = 341
GC = [128, 128, 85]
MASKED = -1e30
TERMS = 6
KR = TERMS * DH
MR = 96
RING = 4


def columns(sizes):
    at, out = 0, {}
    for name, n in sizes:
        out[name] = (at, at + n)
        at += n
    return out, at


CONST_SIZES = [("ident", 128), ("center", 128), ("center8", 128), ("inv", 1), ("blk16", H), ("blk2", 2),
               ("sel4", GRP), ("iota8", E), ("cos", S), ("sin", S), ("xa", S), ("xb", S), ("xai", S),
               ("xbi", S), ("mask", 192)]
SEL_SIZES = [("o", NG * 128), ("h", 2 * 128), ("n", 4 * 128), ("ident", 128)]
ATT_SIZES = [("q0", 128), ("qr0", 128), ("k0", 128), ("kr0", 128), ("v0", 128), ("qT1", 128),
             ("kT1", 128), ("v1", 128), ("p0", NG * 128), ("p1", NG * 128)]
MOE_SIZES = [("gate", E), ("g", (E + 1) * HID), ("u", (E + 1) * HID), ("d", (E + 1) * 3 * 128)]
QKV = 4 * 128
FFN_ONE = [("q", QKV), ("qr", QKV), ("k", QKV), ("kr", QKV), ("v", QKV), ("wo", 4 * 128),
           ("w1", 2 * GH), ("w2", 3 * 128)]
VEC_SIZES = [("bproj", 1), ("qg", 1), ("qb", 1), ("kg", 1), ("kb", 1)] + [
    (f"{n}{d}", w) for d in range(DEPTH)
    for n, w in (("qs", 1), ("qsr", 1), ("ks", 1), ("ksr", 1), ("lg", 1), ("lb", 1), ("b1", 6), ("b2", 1))]
FFN_SIZES = [(f"{n}{d}", w) for d in range(DEPTH) for n, w in FFN_ONE]
CC, NC_ = columns(CONST_SIZES)
AC, NA_ = columns(ATT_SIZES)
MC, NM_ = columns(MOE_SIZES)
FC, NF_ = columns(FFN_SIZES)
VC, NV_ = columns(VEC_SIZES)
SC, NS_ = columns(SEL_SIZES)


def constants():
    t = {}
    t["ident"] = np.eye(128)
    t["center"] = np.eye(128) - 1.0 / 128
    blk = np.kron(np.eye(H), np.ones((DH, DH))) / DH
    t["center8"] = np.eye(128) - blk
    t["inv"] = np.full((128, 1), 1.0 / 128)
    t["blk16"] = np.kron(np.eye(H), np.ones((DH, 1))) / DH
    t["blk2"] = np.kron(np.eye(2), np.ones((LD, 1)))
    sel = np.zeros((128, GRP))
    for j in range(GRP):
        sel[32 * j + DH, j] = 1.0
    t["sel4"] = sel
    t["iota8"] = np.tile(np.arange(E), (128, 1))
    f4 = np.float32
    tok = np.arange(S, dtype=f4)
    inv = (f4(1.0) / f4(10000.0) ** (np.arange(0, DH, 2, dtype=f4) / f4(DH))).astype(f4)
    fr = tok[None, :] * inv[:, None]
    cos, sin = np.cos(fr), np.sin(fr)
    t["cos"] = np.tile(np.concatenate([cos, cos]), (H, 1))
    t["sin"] = np.tile(np.concatenate([-sin, sin]), (H, 1))
    half = np.arange(0, LD, 2, dtype=f4)
    inv = (f4(1.0) / f4(10000.0) ** (half / f4(LD))).astype(f4)
    fr = tok[None, :] * inv[:, None]
    base = (half + f4(0.4 * LD)) / f4(1.4 * LD)
    scale = base[:, None] ** ((tok - S // 2) / f4(WIN // 2))[None, :]
    cos, sin = np.cos(fr), np.sin(fr)
    two = lambda a, b: np.tile(np.concatenate([a, b]), (2, 1))
    t["xa"] = two(cos * scale, cos * scale)
    t["xb"] = two(-sin * scale, sin * scale)
    t["xai"] = two(cos / scale, cos / scale)
    t["xbi"] = two(-sin / scale, sin / scale)
    i, j = np.arange(128)[:, None], np.arange(192)[None, :] - 64
    t["mask"] = np.where((i < j) | (i > j + WIN), MASKED, 0.0)
    return np.concatenate([t[n].astype(np.float32) for n, _ in CONST_SIZES], axis=1)


def selectors():
    o, h, n = np.zeros((3, H, NG, GRP, 32)), np.zeros((3, 2 * H, 2, H, DH)), np.zeros((3, 16, 4, 2, LD))
    for g in range(NG):
        for k in range(GRP):
            o[:, GRP * g + k, g, k] = 1.0
    for k in range(2):
        for head in range(H):
            h[:, k * H + head, k, head] = 1.0
    for f in range(4):
        for k in range(2):
            n[:, (4 + f) * 2 + k, f, k] = 1.0
    out = np.zeros((128, NS_), np.float32)
    for name, a in (("o", o), ("h", h), ("n", n)):
        a = a.reshape(a.shape[0] * a.shape[1], -1)
        out[:a.shape[0], SC[name][0]:SC[name][1]] = a
    out[:, SC["ident"][0]:] = np.eye(128)
    return out


def schedule():
    start = [("x", 0), ("x", 1)] + [(k, 0, u) for k in ("lc", "ls", "lb") for u in range(2)]
    start += [("p", 0, 0, i) for i in range(4)] + [("v", 0, 0)]
    att = [{}, {}]
    att[0].update({(0, 0): [("p", 0, 1, 0), ("p", 0, 1, 1)], (0, 1): [("p", 0, 1, 2), ("p", 0, 1, 3)],
                   (0, 2): [("v", 0, 1)]})
    att[1].update({(0, 0): [("lc", 2, 1)], (0, 1): [("ls", 2, 1)], (0, 2): [("lb", 2, 1)],
                   (0, 3): [("p", 1, 1, 0), ("p", 1, 1, 1), ("hs", 1)], (1, 0): [("v", 1, 1)],
                   (1, 1): [("hr", 1)], (1, 2): [("hb", 1, 0), ("hb", 1, 1)]})

    def way_out(l, u):
        return [[("dn", l, u)], [("dr", l, u)], [("db", l, u, 0), ("db", l, u, 1)],
                [("db", l, u, 2), ("db", l, u, 3)], [("y", l, u)], [("lc", 2 * l + 1, u)],
                [("ls", 2 * l + 1, u)], [("lb", 2 * l + 1, u)]]

    for l in range(2):
        for k, steps in enumerate(way_out(l, 0)):
            att[l][divmod(4 * NG + 2 + k, NT)] = steps
    att[0][(6, 3)] = [("g", 0)]
    att[0][(7, 1)] = [("c", 0)]
    moe = {k + 1: steps for k, steps in enumerate(way_out(0, 1))}
    moe.update({10: [("g", 1)], 13: [("c", 1)], 30: [("lc", 2, 0)], 31: [("ls", 2, 0)], 32: [("lb", 2, 0)],
                33: [("p", 1, 0, 0), ("p", 1, 0, 1), ("hs", 0)], 34: [("v", 1, 0)], 35: [("hr", 0)],
                36: [("hb", 0, 0), ("hb", 0, 1)]})
    for k in range(32):
        moe.setdefault(45 + k // 4, []).append(("a", 1, k // 16, k % 16))
    moe[53] = [("m", 1, 0)]
    local = dict(enumerate(way_out(1, 1)))
    order = list(start)
    for l in range(2):
        if l == 0:
            order.append(("m", 0, 0))
        for n in range(2 * NG):
            for t in range(NT):
                if t == 1 and n + 1 < 2 * NG:
                    order.append(("m", l, n + 1))
                order += att[l].get((n, t), [])
        if l == 0:
            for m in range(54):
                order += moe.get(m, [])
    for i in range(8):
        order += local[i]
    return start, att, moe, local, {step: k for k, step in enumerate(order)}


def adaln_kernel(nc, x, consts, sel, ones, att_w, moe_w, ffn_w, vec, cT, wmod, out):
    ctx = ExitStack()
    with ctx:
        def sb(name, shape, dt=F32):
            return ctx.enter_context(nc.sbuf_tensor(name, shape, dt))

        sems = []

        def sem(name):
            s = ctx.enter_context(nc.semaphore(name))
            sems.append(s)
            return s

        bank = [ctx.enter_context(nc.psum_tensor(f"bank{i}", [128, 512], F32)) for i in range(8)]

        cst = sb("cst", [128, NC_])
        selb = sb("selb", [128, NS_], BF16)
        aw = sb("aw", [128, NA_])
        mw = sb("mw", [128, NM_])
        fw = sb("fw", [128, NF_])
        vc = sb("vc", [128, NV_])
        wqc = sb("wqc", [128, 2, 128])
        mod = sb("mod", [128, 14, B])
        modu = sb("modu", [128, 14, SLOTS])

        def K(n):
            return cst[:, CC[n][0]:CC[n][1]]

        def AW(n):
            return aw[:, AC[n][0]:AC[n][1]]

        def MW(n):
            return mw[:, MC[n][0]:MC[n][1]]

        def FW(n, d):
            return fw[:, FC[f"{n}{d}"][0]:FC[f"{n}{d}"][1]]

        def V_(n):
            return vc[:, VC[n][0]:VC[n][1]]

        def MOD(l, j, u):
            return modu[:, 7 * l + j, u:u + 1]

        def SEL(n):
            return selb[:, SC[n][0]:SC[n][1]]

        ident = K("ident")
        identb = SEL("ident")
        X = [sb(f"X{u}", [128, S]) for u in range(SLOTS)]
        Hh = [sb(f"H{u}", [128, S]) for u in range(SLOTS)]
        G = [sb(f"G{u}", [128, S]) for u in range(SLOTS)]
        SH = [sb(f"SH{u}", [128, S]) for u in range(SLOTS)]
        XC = [sb(f"XC{u}", [128, S]) for u in range(SLOTS)]
        SQ = [sb(f"SQ{u}", [128, S]) for u in range(SLOTS)]
        ve = sb("ve", [128, SLOTS, NT])
        rs = sb("rs", [128, SLOTS, NT])
        mhalf = sb("mhalf", [128, NT])
        st128 = sb("st128", [128, SLOTS, 128])
        ARENA = 20480
        ar = sb("stage_memory", [128, ARENA])
        cur = [0]

        def part(n):
            a = cur[0]
            cur[0] += n
            assert cur[0] <= ARENA, cur[0]
            return ar[:, a:a + n]

        stacks = ar[:, 0:2 * RING * GRP * S // 2]
        qst = part(RING * GRP * S // 2).bitcast(BF16).rearrange("p (r h t) -> p r h t", r=RING, h=GRP)
        kst32 = part(RING * GRP * S // 2)
        kst = kst32.bitcast(BF16).rearrange("p (r h t) -> p r h t", r=RING, h=GRP)
        vaug = [part(NT * H * 16).rearrange("p (t h c) -> p t h c", t=NT, h=H) for u in range(SLOTS)]
        PTB = 8
        pt = [part(S) for _ in range(PTB)]
        raw = [None, None]
        raw[1] = [part(S) for g in range(NG)]
        raw[0] = [part(S) for g in range(NG)]
        qf = [raw[u][0] for u in range(SLOTS)]
        kf = [raw[u][1] for u in range(SLOTS)]
        rem = [raw[u][2] for u in range(SLOTS)]
        ropet = [raw[u][3] for u in range(SLOTS)]
        free_at = cur[0]
        cur[0] = 0
        off = 2 * H * S // 2 + SLOTS * NT * H * 16
        parts = [[ar[:, a + 768 * i:a + 768 * (i + 1)].bitcast(BF16).rearrange("p (j t) -> p j t", j=3)
                  for i in range(2)] for a in (off, free_at)]
        cur[0] = free_at
        cb = [part(S) for _ in range(4)]
        moe_at = (0, off + 2 * 1536)
        hx, sl, hd = ([[ar[:, moe_at[u] + S * (2 * k + i):moe_at[u] + S * (2 * k + i + 1)] for i in range(2)]
                       for u in range(SLOTS)] for k in range(3))
        cbT = SQ
        g_at = [0]

        def small(n):
            a = g_at[0]
            g_at[0] += NT * n
            return [G[u][:, a:a + NT * n].rearrange("p (t e) -> p t e", t=NT) for u in range(SLOTS)]

        lg, top, topf, comb, c2, w2v = (small(n) for n in (E, 8, 8, E, E, 2))
        topi = [a.bitcast(U32) for a in small(8)]
        s4 = [a.rearrange("p t e -> p (t e)") for a in small(1)]
        cur[0] = 0
        qk = [part(8 * S).rearrange("p (i t) -> p i t", i=8) for u in range(SLOTS)]
        vv = [part(NT * S).rearrange("p (t f) -> p t f", t=NT) for u in range(SLOTS)]
        pr_at = cur[0]
        qs = [part(S) for _ in range(2)]
        sqr = [part(S) for _ in range(2)]
        cur[0] = pr_at
        prf = [part(4 * 256) for _ in range(3)]
        pr = [p.rearrange("p (a j k) -> p a j k", a=2, j=2) for p in prf]
        ptc = [part(512) for _ in range(2)]
        xt = [part(S) for _ in range(2)]
        tab = part(4 * S).rearrange("p (i t) -> p i t", i=4)
        ptp = [part(512) for _ in range(2)]
        glu = [prf[0][:, 0:S], prf[1][:, 0:S]]
        ghd = [ptc[0], ptc[1]]
        cur[0] = 0
        stp = [sb(f"stp{u}", [128, NT, 3, 2 * H], BF16) for u in range(SLOTS)]
        strem = sb("strem", [128, SLOTS, 128])
        rows = [XC[u][:, :].bitcast(BF16)[:, 0:S] for u in range(SLOTS)]

        mx = [sb(f"mx{i}", [128, 16]) for i in range(2)]
        mneg = sb("mneg", [16, 128])
        m3 = [sb(f"m3_{i}", [16, 3, 128], BF16) for i in range(2)]
        rec = st128
        lm = [sb(f"lm{i}", [128, 2, 2]) for i in range(3)]
        lsum = [sb(f"lsum{i}", [128, 2, 2]) for i in range(3)]
        lrec = [sb(f"lrec{i}", [128, 2, 2]) for i in range(3)]

        scr = nc.dram_tensor("scr_parts", (2, SLOTS, 2, 3, 128, S), BF16, kind="Internal").ap()
        scr_c = nc.dram_tensor("scr_comb", (SLOTS, E, S), F32, kind="Internal").ap()

        s_load = sem("s_load")
        s_pe0 = sem("s_pe0")
        s_act0 = sem("s_act0")
        s_dve0 = sem("s_dve0")
        s_pool0 = sem("s_pool0")
        ct = ar[:, 0:2 * B]
        wm = ar[:, 1024:1024 + 2 * 6 * C].rearrange("p (l n) -> p l n", l=2)
        selt = ar[:, 8192:8192 + NS_]
        mtmp = ar[:, 4096:4096 + 2 * 4 * B].rearrange("p (l j b) -> p l j b", l=2, j=4)
        with nc.Block() as block:
            @block.sync
            def _(sp):
                for dst, src in ((selt, sel), (ct, cT), (wm, wmod.rearrange("l p n -> p l n")), (vc[:, :], vec),
                                 (cst[:, :], consts), (aw[:, :], att_w), (mw[:, :], moe_w), (fw[:, :], ffn_w)):
                    sp.dma_start(dst, src).then_inc(s_load, 16)
                sp.wait_ge(s_load, 16 * 8)

            @block.gpsimd
            def _(pool):
                nc.gpsimd.memset(mhalf[:, :], -0.5).then_inc(s_pool0, 1)
                for u in range(SLOTS):
                    nc.gpsimd.memset(SH[u][:, :], 0.0).then_inc(s_pool0, 1)

            @block.scalar
            def _(act):
                act.wait_ge(s_load, 16 * 8)
                nc.scalar.activation(ct, ct, ACT.Silu).then_inc(s_act0, 1)

            @block.tensor
            def _(pe):
                pe.wait_ge(s_load, 16 * 8)
                pe.wait_ge(s_act0, 1)
                for l in range(2):
                    for j in range(6):
                        nc.tensor.matmul(bank[0][:, (6 * l + j) * B:(6 * l + j + 1) * B],
                                         wm[:, l, j * C:(j + 1) * C], ct[:, l * B:(l + 1) * B],
                                         start=True, stop=True).then_inc(s_pe0, 1)
                for i, n in enumerate(("qT1", "kT1")):
                    nc.tensor.matmul(bank[1][:, i * 128:(i + 1) * 128], AW(n), K("center8"),
                                     start=True, stop=True).then_inc(s_pe0, 1)

            @block.vector
            def _(dve):
                done = [0]

                def step(ins):
                    done[0] += 1
                    ins.then_inc(s_dve0, 1)
                    dve.wait_ge(s_dve0, done[0])

                dve.wait_ge(s_pe0, 14)
                step(nc.vector.tensor_copy(selb[:, :], selt))
                step(nc.vector.tensor_copy(wqc[:, :, :], bank[1][:, 0:256].rearrange("p (i c) -> p i c", i=2)))
                m = mod[:, :, :].rearrange("p (l j) b -> p l j b", l=2)
                step(nc.vector.tensor_copy(m[:, :, 0:6, :],
                                           bank[0][:, 0:12 * B].rearrange("p (l j b) -> p l j b", l=2, j=6)))
                for j in (1, 4):
                    step(nc.vector.tensor_scalar(m[:, :, j, :], m[:, :, j, :], 1.0, None, ALU.add))
                for j in (2, 5):
                    g, a, s = m[:, :, j, :], mtmp[:, :, 0, :], mtmp[:, :, 1, :]
                    step(nc.vector.tensor_scalar(a, g, -1.0, None, ALU.mult))
                    step(nc.vector.tensor_tensor(a, a, g, ALU.max))
                    step(nc.vector.tensor_scalar(s, g, 0.0, 2.0, ALU.is_ge, ALU.mult))
                    step(nc.vector.tensor_scalar(s, s, 1.0, None, ALU.subtract))
                    step(nc.vector.tensor_scalar(a, a, 0.25, None, ALU.max))
                    step(nc.vector.tensor_tensor(g, a, s, ALU.mult))
                step(nc.vector.tensor_scalar(m[:, :, 6, :], m[:, :, 2, :], V_("bproj"), None, ALU.mult))
                step(nc.vector.tensor_scalar(m[:, 1, 6, :], m[:, 1, 2, :], 0.0, None, ALU.mult))

        x_in = sem("x_in"); step_mm = sem("step_mm"); step_read = [sem(f"step_read{i}") for i in range(2)]; f_r1 = sem("f_r1")
        mod_ready = sem("mod_ready")
        dve_link = sem("dve_link"); zeroed = sem("zeroed"); sp_first = sem("sp_first"); l_evp = sem("l_evp")
        ln_cent = sem("ln_cent"); ln_xc = sem("ln_xc"); ln_sq = sem("ln_sq"); ln_stat = sem("ln_stat")
        ln_var = sem("ln_var"); ln_rstd = sem("ln_rstd"); ln_bc = sem("ln_bc"); ln_h = sem("ln_h")

        at_sq = sem("at_sq"); at_sd = sem("at_sd")
        at_rs = sem("at_rs")
        f_rt = sem("f_rt"); f_rc = sem("f_rc")
        sp_hi = sem("sp_hi"); sp_r = sem("sp_r"); sp_mid = sem("sp_mid"); sp_done = sem("sp_done")
        vaug_one = sem("vaug_one")
        st_wr = [sem(f"st_wr{u}") for u in range(SLOTS)]
        st_rd = [sem(f"st_rd{i}") for i in range(RING)]
        ring_clear = sem("ring_clear"); ones_rd = sem("ones_rd")
        a_mm = sem("a_mm"); a_mx = sem("a_mx"); m_spl = sem("m_spl"); m_row = sem("m_row")
        s_mm = sem("s_mm"); e_done = sem("e_done"); pv_done = sem("pv_done"); o_raw = sem("o_raw"); o_clear = sem("o_clear")
        den_rec = sem("den_rec")
        x_att = sem("x_att")
        gt_exp = sem("gt_exp"); gt_comb = sem("gt_comb")
        cb_wr = sem("cb_wr")
        cb_rd = [sem(f"cb_rd{u}") for u in range(4)]
        hx_ready = sem("hx_ready"); mo_g = sem("mo_g"); mo_u = sem("mo_u"); mo_sl = sem("mo_sl")
        mo_hd = sem("mo_hd"); mo_dn = sem("mo_dn"); x_moe = sem("x_moe")
        sh_ready = sem("sh_ready"); tb_ready = sem("tb_ready")
        f_main = sem("f_main"); f_rot = sem("f_rot"); f_cp = sem("f_cp"); f_sq = sem("f_sq")
        f_t1 = sem("f_t1"); f_t2 = sem("f_t2"); f_tt = sem("f_tt"); f_stat = sem("f_stat")
        f_v = sem("f_v"); f_vc = sem("f_vc"); f_n2 = sem("f_n2"); f_sd = sem("f_sd"); f_rn = sem("f_rn")
        f_bc = sem("f_bc"); f_kn = sem("f_kn")
        l_s = sem("l_s"); l_mk = sem("l_mk"); l_nm = sem("l_nm"); l_ex = sem("l_ex"); l_p = sem("l_p")
        l_tr = sem("l_tr"); l_ev = sem("l_ev"); l_pv = sem("l_pv"); l_o = sem("l_o")
        wo_mm = sem("wo_mm"); z_att = sem("z_att")
        w1_mm = sem("w1_mm"); w1_gl = sem("w1_gl"); w1_hd = sem("w1_hd"); w2_mm = sem("w2_mm"); z_ffn = sem("z_ffn")
        x_last = sem("x_last"); o_tr = sem("o_tr"); o_ev = sem("o_ev"); o_dma = sem("o_dma")
        turn_sems = sems[5:]
        first, last = turn_sems[0].num, turn_sems[-1].num
        assert last - first == len(turn_sems) - 1

        xv = x.rearrange("(w u) (t p) c -> u p w t c", p=128, u=SLOTS)
        ov = out.rearrange("(w u) (t p) c -> u p w t c", p=128, u=SLOTS)
        xin = [G[u][:, :].rearrange("p (o t c) -> p o t c", o=1, t=NT) for u in range(SLOTS)]
        slots = range(SLOTS)
        NU = SLOTS * NG
        CLEARS = 4

        start, att_steps, moe_steps, local_steps, STEP = schedule()

        def read(engine, *name):
            k = STEP[name]
            engine.wait_ge(step_read[k % 2], k // 2 + 1)

        def a_count(l, n, s):
            return l * NU * 16 + (n - 2 * l) * 16 + s

        with nc.Fori(0, B // SLOTS) as turn:
            with nc.Block() as block:
                @block.sync
                def _(sp):
                    for u in slots:
                        sp.dma_start(xin[u], xv[u, :, bass.ds(turn, 1), :, :]).then_inc(x_in, 16)

                    def parts_out(l, u):
                        for i in range(2):
                            sp.wait_ge(sp_done, (l * SLOTS + u) * 2 + i + 1)
                            sp.dma_start(scr[l, u, i, :, :, :].rearrange("j p t -> p j t"),
                                         parts[u][i]).then_inc(st_wr[u], 16)

                    def rows_of_ones(l):
                        sp.wait_ge(ring_clear, CLEARS * (l + 1))
                        sp.dma_start(kst32[MR:MR + 3, :], ones).then_inc(ones_rd, 16)

                    def stack(l, n):
                        u, g = divmod(n, NG)
                        if g == 0:
                            sp.wait_ge(st_wr[u], 32 * (l + 1))
                        if n >= RING:
                            sp.wait_ge(s_mm, (l * NU + n - RING + 1) * 16)
                        group = scr[l, u, :, :, GRP * DH * g:GRP * DH * (g + 1), :] \
                            .rearrange("i j (h d) t -> i j d h t", h=GRP)
                        for r, (jq, jk) in enumerate(zip((0, 0, 0, 1, 1, 2), (0, 1, 2, 0, 1, 0))):
                            sp.dma_start(qst[8 * r:8 * r + 8, n % RING, :, :],
                                         group[0, jq, :, :, :]).then_inc(st_rd[n % RING], 16)
                            sp.dma_start(kst[8 * r:8 * r + 8, n % RING, :, :],
                                         group[1, jk, :, :, :]).then_inc(st_rd[n % RING], 16)

                    def maximum_rows(l, n):
                        sp.wait_ge(m_spl, l * NU + n + 1)
                        for j in range(3):
                            sp.dma_start(qst[MR + j:MR + j + 1, n % RING, :, :].rearrange("o h (t c) -> o (h t) c", t=NT),
                                         m3[n % 2][:, j, :]).then_inc(m_row, 16)

                    def expert_weights(u, es):
                        for e in es:
                            m = u * E + e
                            if m >= 4:
                                sp.wait_ge(hx_ready, m - 3)
                            sp.dma_start(cb[m % 4], scr_c[u, e, :].partition_broadcast(128)).then_inc(cb_rd[m % 4], 16)

                    def weights_out(u):
                        read(sp, "c", u)
                        sp.dma_start(scr_c[u, :, :], cbT[u][0:E, :]).then_inc(cb_wr, 16)
                        sp.wait_ge(cb_wr, 16 * (u + 1))

                    def attention(l):
                        parts_out(l, 0)
                        rows_of_ones(l)
                        for n in range(RING):
                            stack(l, n)
                        if l:
                            expert_weights(1, range(5, E))
                        for n in range(NU):
                            if 2 + l <= n and n + 2 - l < NU:
                                stack(l, n + 2 - l)
                            maximum_rows(l, n)
                            if n == 1 + l:
                                parts_out(l, 1)

                    attention(0)
                    weights_out(0)
                    expert_weights(0, range(6))
                    weights_out(1)
                    expert_weights(0, range(6, E))
                    expert_weights(1, range(5))
                    attention(1)
                    for u in slots:
                        sp.wait_ge(o_ev, u + 1)
                        sp.dma_start(ov[u, :, bass.ds(turn, 1), :, :],
                                     G[u][:, :].rearrange("p (o t c) -> p o t c", o=1, t=NT)).then_inc(o_dma, 16)
                    sp.wait_ge(o_dma, 16 * SLOTS)

                @block.tensor
                def _(pe):
                    mm = nc.tensor.matmul

                    def to_rows(dst, u, k):
                        src = stp[u][:, :, :, :].rearrange("p t j k -> p (t j k)")
                        d = dst[0:3 * k, :].bitcast(BF16)
                        for t in range(NT):
                            r = nc.tensor.transpose(d[:, t * 128:(t + 1) * 128], src[:, t * 3 * k:(t + 1) * 3 * k], identb)
                        return r

                    def stack_loaded(l, n):
                        pe.wait_ge(st_rd[n % RING], 12 * 16 * (l * NU // RING + n // RING + 1))

                    def step(kind, *a):
                        k = STEP[(kind, *a)]
                        if k >= 2:
                            pe.wait_ge(step_read[k % 2], k // 2)
                        o = bank[6 + k % 2]
                        u = a[-1] if kind not in ("p", "hb", "db", "a", "m") else a[1] if kind in ("p", "db") else a[0]
                        cols = lambda t: slice(t * 128, (t + 1) * 128)
                        if kind == "x":
                            pe.wait_ge(x_in, 16 * SLOTS)
                            for t in range(NT):
                                r = nc.tensor.transpose(o[:, cols(t)], xin[u][:, 0, t, :], ident)
                        elif kind == "lc":
                            if a[0] == 0:
                                read(pe, "x", u)
                            else:
                                pe.wait_ge(*((x_att, u + 1), (x_moe, u + 1), (x_att, SLOTS + u + 1))[a[0] - 1])
                            r = mm(o[:, :], K("center"), X[u][:, :], start=True, stop=True)
                        elif kind == "ls":
                            pe.wait_ge(ln_sq, a[0] * SLOTS + u + 1)
                            for t in range(NT):
                                r = mm(o[:, t:t + 1], SQ[u][:, cols(t)], K("inv"), start=True, stop=True)
                        elif kind == "lb":
                            pe.wait_ge(ln_rstd, a[0] * SLOTS + u + 1)
                            for t in range(NT):
                                r = mm(o[:, cols(t)], rs[:, u, t:t + 1].to_broadcast([128, 128]), ident,
                                       start=True, stop=True)
                        elif kind == "p":
                            l, _, i = a
                            pe.wait_ge(ln_h, 2 * l * SLOTS + u + 1)
                            w = (AW("q0"), AW("qr0"), AW("k0"), AW("kr0"))[i] if l == 0 else wqc[:, i, :]
                            r = mm(o[:, :], w, Hh[u][:, :], start=True, stop=True)
                        elif kind == "v":
                            for t in range(NT):
                                r = mm(o[:, cols(t)], Hh[u][:, cols(t)], AW(f"v{a[0]}"), start=True, stop=True)
                        elif kind == "hs":
                            for i in range(2):
                                pe.wait_ge(at_sq, 2 * u + i + 1)
                                for t in range(NT):
                                    r = mm(o[:, (2 * t + i) * H:(2 * t + i + 1) * H], (SQ[u], G[u])[i][:, cols(t)],
                                           K("blk16"), start=True, stop=True)
                        elif kind == "hr":
                            pe.wait_ge(at_rs, u + 1)
                            r = to_rows(o, u, 2 * H)
                        elif kind == "hb":
                            read(pe, "hr", u)
                            r = mm(o[:, :], SEL("h")[0:6 * H, a[1] * 128:(a[1] + 1) * 128], rows[u][0:6 * H, :],
                                   start=True, stop=True)
                        elif kind == "a":
                            l, n, s = a
                            if s == 0:
                                stack_loaded(l, n)
                            r = mm(o[:, :], qst[0:MR, n, s // NT, cols(s % NT)], kst[0:MR, n, s // NT, :],
                                   start=True, stop=True)
                        elif kind == "m":
                            l, n = a
                            if l and n < 2:
                                read(pe, "a", l, n, 15)
                            else:
                                pe.wait_ge(a_mx, a_count(l, n, 16))
                            r = nc.tensor.transpose(o[0:16, 0:128], mx[n % 2][:, :], ident)
                        elif kind == "dn":
                            pe.wait_ge(o_raw, a[0] * NU + (u + 1) * NG)
                            for g in range(NG):
                                for t in range(NT):
                                    c = (t * NG + g) * GRP
                                    r = mm(o[:, c:c + GRP], raw[u][g][:, cols(t)], K("sel4"), start=True, stop=True)
                        elif kind == "dr":
                            pe.wait_ge(den_rec, a[0] * SLOTS + u + 1)
                            r = to_rows(o, u, H)
                        elif kind == "db":
                            read(pe, "dr", a[0], u)
                            r = mm(o[:, :], SEL("o")[0:3 * H, a[2] * 128:(a[2] + 1) * 128], rows[u][0:3 * H, :],
                                   start=True, stop=True)
                        elif kind == "y":
                            for g in range(NG):
                                read(pe, "db", a[0], u, g)
                                r = mm(o[:, :], AW(f"p{a[0]}")[:, g * 128:(g + 1) * 128], raw[u][g],
                                       start=(g == 0), stop=(g == NG - 1))
                        elif kind == "g":
                            pe.wait_ge(ln_h, SLOTS + u + 1)
                            for t in range(NT):
                                r = mm(o[:, t * E:(t + 1) * E], Hh[u][:, cols(t)], MW("gate"), start=True, stop=True)
                        elif kind == "c":
                            pe.wait_ge(gt_comb, u + 1)
                            for t in range(NT):
                                r = nc.tensor.transpose(o[0:E, cols(t)], comb[u][:, t, :], ident)
                        r.then_inc(step_mm, 1)

                    def layer_norm(i, src, ready):
                        for u in slots:
                            ready(u)
                            mm(bank[u][:, :], K("center"), src[u][:, :], start=True, stop=True).then_inc(ln_cent, 1)
                        for u in slots:
                            k = i * SLOTS + u + 1
                            pe.wait_ge(ln_sq, k)
                            for t in range(NT):
                                r = mm(bank[2 + u][:, t:t + 1], SQ[u][:, t * 128:(t + 1) * 128], K("inv"),
                                       start=True, stop=True)
                            r.then_inc(ln_stat, 1)
                        for u in slots:
                            pe.wait_ge(ln_rstd, i * SLOTS + u + 1)
                            for t in range(NT):
                                r = mm(bank[4 + u][:, t * 128:(t + 1) * 128],
                                       rs[:, u, t:t + 1].to_broadcast([128, 128]), ident, start=True, stop=True)
                            r.then_inc(ln_bc, 1)

                    def attention(l):
                        def score_for_max(n, s):
                            hh, t = divmod(s, NT)
                            i = a_count(l, n, s)
                            if s == 0:
                                stack_loaded(l, n)
                            if i >= 2:
                                pe.wait_ge(a_mx, i - 1)
                            mm(bank[i % 2][:, :], qst[0:MR, n % RING, hh, t * 128:(t + 1) * 128],
                               kst[0:MR, n % RING, hh, :], start=True, stop=True).then_inc(a_mm, 1)

                        def score_minus_max(n, t, hh):
                            v = l * NU * 16 + n * 16 + t * GRP + hh
                            if n == 0 and t == 0 and hh == 0:
                                pe.wait_ge(ones_rd, 16 * (l + 1))
                            if t == 0 and hh == 0:
                                pe.wait_ge(m_row, 48 * (l * NU + n + 1))
                            if v >= 3:
                                pe.wait_ge(e_done, v - 2)
                            mm(bank[2 + v % 3][:, :], kst[:, n % RING, hh, t * 128:(t + 1) * 128],
                               qst[:, n % RING, hh, :], start=True, stop=True).then_inc(s_mm, 1)

                        def weigh_values(n, t):
                            u, g = divmod(n, NG)
                            v = n * 16 + t * GRP
                            pe.wait_ge(e_done, l * NU * 16 + v + GRP)
                            if t == 0:
                                read(pe, "v", l, u)
                                if n == 0:
                                    pe.wait_ge(o_clear, l + 1)
                                else:
                                    pe.wait_ge(o_raw, l * NU + n)
                            for hh in range(GRP):
                                r = mm(bank[5][32 * hh:32 * hh + 16, :], vaug[u][:, t, GRP * g + hh, :],
                                       pt[(v + hh) % PTB], start=(t == 0), stop=(t == NT - 1))
                            r.then_inc(pv_done, 1)

                        if l == 0:
                            for s in range(16):
                                score_for_max(0, s)
                            step("m", 0, 0)
                            for s in range(16):
                                score_for_max(1, s)
                        else:
                            pe.wait_ge(mo_hd, 54)
                            pe.wait_ge(x_moe, SLOTS)
                        for n in range(NU):
                            for t in range(NT):
                                for hh in range(GRP):
                                    score_minus_max(n, t, hh)
                                    if n + 2 < NU:
                                        score_for_max(n + 2, t * GRP + hh)
                                if t == 1 and n + 1 < NU:
                                    step("m", l, n + 1)
                                if t:
                                    weigh_values(n, t - 1)
                                elif n:
                                    weigh_values(n - 1, NT - 1)
                                for st in att_steps[l].get((n, t), []):
                                    step(*st)
                        weigh_values(NU - 1, NT - 1)

                    def moe():
                        units = [(u, e, c) for u in slots for e in range(E + 1) for c in range(3)]

                        def down(m):
                            u, e, c = units[m]
                            pe.wait_ge(mo_hd, m + 1)
                            mm(bank[4 + u][:, :], MW("d")[0:CH[c], (3 * e + c) * 128:(3 * e + c + 1) * 128],
                               hd[u][m % 2][0:CH[c], :], start=(e == 0 and c == 0), stop=(e == E and c == 2)) \
                                .then_inc(mo_dn, 1)

                        pe.wait_ge(e_done, NU * 16)
                        pe.wait_ge(o_raw, NU)
                        pe.wait_ge(a_mx, NU * 16)
                        for m, (u, e, c) in enumerate(units):
                            p = 2 * (m % 2)
                            if m >= 2:
                                pe.wait_ge(mo_hd, m - 1)
                            w = e * HID + 128 * c
                            mm(bank[p][0:CH[c], :], MW("g")[:, w:w + CH[c]], Hh[u][:, :], start=True, stop=True) \
                                .then_inc(mo_g, 1)
                            if e and c == 0:
                                pe.wait_ge(hx_ready, u * E + e)
                            src = hx[u][(e - 1) % 2] if e else Hh[u][:, :]
                            mm(bank[p + 1][0:CH[c], :], MW("u")[:, w:w + CH[c]], src, start=True, stop=True) \
                                .then_inc(mo_u, 1)
                            if m:
                                down(m - 1)
                            for st in moe_steps.get(m, []):
                                step(*st)
                        down(53)

                    def local_layer(d):
                        for u in slots:
                            pe.wait_ge(sh_ready, 2 * d * SLOTS + u + 1)
                            for i in range(8):
                                j = (d * SLOTS + u) * 8 + i
                                n, f = ("q", "k")[i // 4], i % 4
                                if u or i >= 2:
                                    pe.wait_ge(f_cp, j - 1)
                                    pe.wait_ge(f_t2, j - 1)
                                for w, dst, s in ((n, bank[2 * (i % 2)], f_main), (n + "r", bank[2 * (i % 2) + 1], f_rot)):
                                    mm(dst[:, :], FW(w, d)[:, f * 128:(f + 1) * 128], SH[u][:, :], start=True, stop=True) \
                                        .then_inc(s, 1)
                                if i:
                                    norm_sums(d, u, i - 1)
                                if i % 2:
                                    t = i // 2
                                    k = (d * SLOTS + u) * NT + t
                                    if u or t:
                                        pe.wait_ge(f_vc, k)
                                    mm(bank[5][:, :], SH[u][:, t * 128:(t + 1) * 128], FW("v", d),
                                       start=True, stop=True).then_inc(f_v, 1)
                                if d == 0 and u == 0:
                                    for st in local_steps[i]:
                                        step(*st)
                            norm_sums(d, u, 7)
                        if d == 0:
                            for i in range(2):
                                pe.wait_ge(step_read[i], (len(STEP) + 1 - i) // 2)
                        for u in slots:
                            pe.wait_ge(f_rn, d * SLOTS + u + 1)
                            to_rows(bank[6 + u], u, 16).then_inc(f_rt, 1)
                        for u in slots:
                            pe.wait_ge(f_rc, d * SLOTS + u + 1)
                            if u == 0:
                                pe.wait_ge(f_tt, (d + 1) * SLOTS * 8)
                                pe.wait_ge(f_cp, (d + 1) * SLOTS * 8)
                            for f in range(4):
                                if u:
                                    pe.wait_ge(f_kn, d * SLOTS * 4 + f + 1)
                                mm(bank[f][:, :], SEL("n")[0:48, f * 128:(f + 1) * 128], rows[u][0:48, :],
                                   start=True, stop=True).then_inc(f_bc, 1)
                        NW = SLOTS * NT * 2
                        pe.wait_ge(f_kn, (d + 1) * SLOTS * 4)
                        pe.wait_ge(f_vc, (d + 1) * SLOTS * NT)

                        def scores(w):
                            u, t, hq = w // 8, w // 2 % 4, w % 2
                            lo = 0 if t else 64
                            if w >= 2:
                                pe.wait_ge(l_mk, 4 * (d * NW + w - 1))
                            for j in range(2):
                                for par in range(2):
                                    f, p = 2 * hq + j, 64 * par
                                    r = mm(bank[2 * (w % 2) + par][:, j * 192 + lo:j * 192 + 192],
                                           qk[u][p:p + 64, f, t * 128:(t + 1) * 128],
                                           qk[u][p:p + 64, 4 + f, t * 128 - 64 + lo:(t + 1) * 128], start=True, stop=True)
                            r.then_inc(l_s, 1)

                        def transposes(w):
                            t = w // 2 % 4
                            pe.wait_ge(l_p, d * NW + w + 1)
                            if w:
                                pe.wait_ge(l_ev, d * NW + w)
                            for par in range(2):
                                for j in range(2):
                                    a = (2 * par + j) * 128
                                    r = nc.tensor.transpose(bank[4][:, a:a + 128], pr[w % 3][:, par, j, 128:256], ident)
                                    if t:
                                        r = nc.tensor.transpose(bank[5][:, a:a + 128], pr[w % 3][:, par, j, 0:128], ident)
                            r.then_inc(l_tr, 1)

                        def values(w):
                            u, t, hq = w // 8, w // 2 % 4, w % 2
                            pe.wait_ge(l_ev, d * NW + w + 1)
                            if hq == 0 and w >= 4:
                                pe.wait_ge(l_o, (d * NW + w) // 2 - 1)
                            for j in range(2):
                                for first in ((True, False) if t else (True,)):
                                    for par in range(2):
                                        h, f, a = 4 * hq + 2 * j + par, 2 * hq + j, (2 * par + j) * 128
                                        o = bank[6 + w // 2 % 2][64 * par:64 * par + 64, f * 128:(f + 1) * 128]
                                        if first:
                                            r = mm(o, vv[u][:, t, h * LD:(h + 1) * LD], ptc[w % 2][:, a:a + 128],
                                                   start=True, stop=(t == 0))
                                        else:
                                            r = mm(o, vv[u][64:128, t - 1, h * LD:(h + 1) * LD],
                                                   ptp[w % 2][64:128, a:a + 128], start=False, stop=True)
                            r.then_inc(l_pv, 1)

                        scores(0)
                        scores(1)
                        for w in range(NW):
                            transposes(w)
                            if w + 2 < NW:
                                scores(w + 2)
                            if w:
                                values(w - 1)
                        values(NW - 1)
                        for u in slots:
                            pe.wait_ge(l_o, (d * NW + (u + 1) * 8) // 2)
                            for f in range(4):
                                r = mm(bank[u][:, :], FW("wo", d)[:, f * 128:(f + 1) * 128], qk[u][:, f, :],
                                       start=(f == 0), stop=(f == 3))
                            r.then_inc(wo_mm, 1)
                        layer_norm(4 + d, SH, lambda u: pe.wait_ge(sh_ready, (2 * d + 1) * SLOTS + u + 1))
                        units = [(u, c) for u in slots for c in range(3)]

                        def down(m):
                            u, c = units[m]
                            pe.wait_ge(w1_hd, d * 6 + m + 1)
                            r = mm(bank[6 + u][:, :], FW("w2", d)[0:GC[c], c * 128:(c + 1) * 128],
                                   ghd[m % 2][0:GC[c], :], start=(c == 0), stop=(c == 2))
                            r.then_inc(w2_mm, 1)

                        pe.wait_ge(ln_xc, (d + 1) * SLOTS)
                        for m, (u, c) in enumerate(units):
                            if c == 0:
                                pe.wait_ge(ln_h, (4 + d) * SLOTS + u + 1)
                            if m >= 2:
                                pe.wait_ge(w1_hd, d * 6 + m - 1)
                            for k in range(2):
                                mm(bank[2 * (m % 2) + k][0:GC[c], :],
                                   FW("w1", d)[:, k * GH + 128 * c:k * GH + 128 * c + GC[c]], G[u][:, :],
                                   start=True, stop=True).then_inc(w1_mm, 1)
                            if m >= 1:
                                down(m - 1)
                        down(5)

                    def norm_sums(d, u, i):
                        pe.wait_ge(f_sq, (d * SLOTS + u) * 8 + i + 1)
                        if u and i == 0:
                            pe.wait_ge(f_n2, d * SLOTS + 1)
                        for t in range(NT):
                            a = (t * 8 + i) * 2
                            r = mm(bank[4][:, a:a + 2], sqr[i % 2][:, t * 128:(t + 1) * 128], K("blk2"),
                                   start=True, stop=True)
                        r.then_inc(f_stat, 1)

                    for st in start:
                        step(*st)
                    attention(0)
                    moe()
                    attention(1)
                    for d in range(DEPTH):
                        local_layer(d)
                    for u in slots:
                        pe.wait_ge(x_last, u + 1)
                        for t in range(NT):
                            r = nc.tensor.transpose(bank[u][:, t * 128:(t + 1) * 128], X[u][:, t * 128:(t + 1) * 128], ident)
                        r.then_inc(o_tr, 1)

                @block.scalar
                def _(act):
                    fn = nc.scalar.activation

                    def step(kind, *a):
                        k = STEP[(kind, *a)]
                        o = bank[6 + k % 2]
                        u = a[-1]
                        if kind == "x":
                            act.wait_ge(step_mm, k + 1)
                            fn(X[u][:, :], o[:, :], ACT.Copy).then_inc(step_read[k % 2], 1)
                        elif kind == "lc":
                            act.wait_ge(step_mm, k + 1)
                            fn(SQ[u][:, :], o[:, :], ACT.Square).then_inc(ln_sq, 1)
                            fn(XC[u][:, :], o[:, :], ACT.Copy).then_inc(step_read[k % 2], 1)
                        elif kind == "p" and a[0] == 1:
                            _, u, i = a
                            act.wait_ge(step_mm, k + 1)
                            fn((SQ[u], G[u])[i][:, :], o[:, :], ACT.Square).then_inc(at_sq, 1)
                            fn((qf, kf)[i][u], o[:, :], ACT.Copy).then_inc(step_read[k % 2], 1)
                        elif kind == "v":
                            act.wait_ge(step_mm, k + 1)
                            act.wait_ge(vaug_one, a[0] * SLOTS + u + 1)
                            fn(vaug[u][:, :, :, 0:DH].rearrange("p t h c -> p (t h) c"),
                               o[:, :].rearrange("p (a c) -> p a c", c=DH), ACT.Copy).then_inc(step_read[k % 2], 1)
                            if a[0] == 0:
                                split(0, u)
                        elif kind == "hs":
                            read(act, "hs", u)
                            fn(st128[:, u, :], st128[:, u, :], ACT.Sqrt).then_inc(at_sd, 1)
                        elif kind in ("hr", "dr"):
                            n = 3 * H * (2 if kind == "hr" else 1)
                            act.wait_ge(step_mm, k + 1)
                            fn(rows[u][0:n, :], o[0:n, :].bitcast(BF16)[:, 0:S], ACT.Copy).then_inc(step_read[k % 2], 1)
                        elif kind == "hb" and a[1] == 1:
                            split(1, a[0])
                        elif kind == "y":
                            act.wait_ge(step_mm, k + 1)
                            fn(XC[u][:, :], o[:, :], ACT.Identity, scale=MOD(a[0], 2, u), bias=MOD(a[0], 6, u)) \
                                .then_inc(step_read[k % 2], 1)
                        elif kind == "g":
                            read(act, "g", u)
                            fn(lg[u], lg[u], ACT.Exp).then_inc(gt_exp, 1)
                        elif kind == "c":
                            act.wait_ge(step_mm, k + 1)
                            fn(cbT[u][0:E, :], o[0:E, :], ACT.Copy).then_inc(step_read[k % 2], 1)

                    def split(l, u):
                        for i in range(2):
                            k = (l * SLOTS + u) * 2 + i
                            act.wait_ge(sp_hi, k + 1)
                            fn(parts[u][i][:, 0, :], (qf, kf)[i][u], ACT.Copy).then_inc(sp_first, 1)
                            act.wait_ge(sp_r, k + 1)
                            fn(parts[u][i][:, 1, :], rem[u], ACT.Copy).then_inc(sp_mid, 1)

                    def layer_norm(i):
                        for u in slots:
                            act.wait_ge(ln_cent, (i - 4) * SLOTS + u + 1)
                            fn(SQ[u][:, :], bank[u][:, :], ACT.Square).then_inc(ln_sq, 1)
                            fn(XC[u][:, :], bank[u][:, :], ACT.Copy).then_inc(ln_xc, 1)

                    def attention(l):
                        for n in range(NU):
                            for t in range(NT):
                                for hh in range(GRP):
                                    v = l * NU * 16 + n * 16 + t * GRP + hh
                                    act.wait_ge(s_mm, v + 1)
                                    if n * 16 + t * GRP + hh >= PTB:
                                        act.wait_ge(pv_done, (v - PTB) // GRP + 1)
                                    fn(pt[v % PTB], bank[2 + v % 3][:, :], ACT.Exp, scale=float(DH) ** -0.5) \
                                        .then_inc(e_done, 1)
                                if t == 1 and n:
                                    evacuate(l, n - 1)
                                for st in att_steps[l].get((n, t), []):
                                    step(*st)
                        evacuate(l, NU - 1)

                    def evacuate(l, n):
                        u, g = divmod(n, NG)
                        act.wait_ge(pv_done, (l * NU + n + 1) * NT)
                        fn(raw[u][g], bank[5][:, :], ACT.Copy).then_inc(o_raw, 1)

                    def moe():
                        for m in range(SLOTS * (E + 1) * 3):
                            c, u = CH[m % 3], m // 27
                            act.wait_ge(mo_g, m + 1)
                            if m >= 2:
                                act.wait_ge(mo_hd, m - 1)
                            fn(sl[u][m % 2][0:c, :], bank[2 * (m % 2)][0:c, :], ACT.Silu).then_inc(mo_sl, 1)
                            for st in moe_steps.get(m, []):
                                step(*st)

                    def local_layer(d):
                        for u in slots:
                            for i in range(8):
                                j = (d * SLOTS + u) * 8 + i
                                act.wait_ge(f_main, j + 1)
                                if u or i >= 2:
                                    act.wait_ge(f_t1, j - 1)
                                    act.wait_ge(f_stat, j - 1)
                                fn(qs[i % 2], bank[2 * (i % 2)][:, :], ACT.Copy).then_inc(f_cp, 1)
                                act.wait_ge(f_cp, j + 1)
                                fn(sqr[i % 2], qs[i % 2], ACT.Square).then_inc(f_sq, 1)
                                if i % 2:
                                    t = i // 2
                                    act.wait_ge(f_v, (d * SLOTS + u) * NT + t + 1)
                                    fn(vv[u][:, t, :], bank[5][:, :], ACT.Copy).then_inc(f_vc, 1)
                                if d == 0 and u == 0:
                                    for st in local_steps[i]:
                                        step(*st)
                        for u in slots:
                            act.wait_ge(f_n2, d * SLOTS + u + 1)
                            fn(st128[:, u, 0:64], st128[:, u, 0:64], ACT.Sqrt).then_inc(f_sd, 1)
                        for u in slots:
                            act.wait_ge(f_rt, d * SLOTS + u + 1)
                            fn(rows[u][0:48, :], bank[6 + u][0:48, :].bitcast(BF16)[:, 0:S], ACT.Copy).then_inc(f_rc, 1)
                        NW = SLOTS * NT * 2

                        def transposed(w):
                            t = w // 2 % 4
                            act.wait_ge(l_tr, d * NW + w + 1)
                            if w >= 2:
                                act.wait_ge(l_pv, d * NW + w - 1)
                            if t:
                                fn(ptp[w % 2][64:128, :], bank[5][64:128, :], ACT.Copy).then_inc(l_evp, 1)
                            fn(ptc[w % 2], bank[4][:, :], ACT.Copy).then_inc(l_ev, 1)

                        def output(w):
                            u, t = w // 8, w // 2 % 4
                            act.wait_ge(l_pv, d * NW + w + 1)
                            fn(qk[u][:, 0:4, t * 128:(t + 1) * 128],
                               bank[6 + w // 2 % 2][:, :].rearrange("p (f t) -> p f t", f=4), ACT.Copy).then_inc(l_o, 1)

                        for w in range(NW):
                            t = w // 2 % 4
                            lo = 64 if t else 128
                            act.wait_ge(l_nm, d * NW + w + 1)
                            for par in range(2):
                                for j in range(2):
                                    p = pr[w % 3][:, par, j, lo:256]
                                    fn(p, p, ACT.Exp, scale=8.0, bias=lm[w % 3][:, par, j:j + 1],
                                       accum_out=lsum[w % 3][:, par, j:j + 1]).then_inc(l_ex, 1)
                            if w:
                                transposed(w - 1)
                            if w % 2 and w > 2:
                                output(w - 2)
                        transposed(NW - 1)
                        output(NW - 1)
                        layer_norm(4 + d)
                        for m in range(6):
                            c = m % 3
                            act.wait_ge(w1_mm, 2 * (d * 6 + m + 1))
                            if m >= 2:
                                act.wait_ge(w1_hd, d * 6 + m - 1)
                            fn(glu[m % 2][0:GC[c], :], bank[2 * (m % 2) + 1][0:GC[c], :], ACT.Gelu,
                               bias=V_(f"b1{d}")[0:GC[c], 3 + c:4 + c]).then_inc(w1_gl, 1)

                    for st in start:
                        step(*st)
                    attention(0)
                    moe()
                    attention(1)
                    for d in range(DEPTH):
                        local_layer(d)
                    for u in slots:
                        act.wait_ge(o_tr, u + 1)
                        fn(G[u][:, :], bank[u][:, :], ACT.Copy).then_inc(o_ev, 1)

                @block.vector
                def _(dve):
                    tt, ts, stt = nc.vector.tensor_tensor, nc.vector.tensor_scalar, nc.vector.scalar_tensor_tensor
                    links = [0]

                    def link(ins):
                        links[0] += 1
                        ins.then_inc(dve_link, 1)
                        dve.wait_ge(dve_link, links[0])

                    def three_parts(u, k, done):
                        src = st128[:, u, 0:NT * k].rearrange("p (t k) -> p t k", t=NT)
                        r = strem[:, u, 0:NT * k].rearrange("p (t k) -> p t k", t=NT)
                        q = stp[u][:, :, :, :].rearrange("p t j k -> p (t j k)")[:, 0:NT * 3 * k] \
                            .rearrange("p (t j k) -> p t j k", t=NT, j=3)
                        link(nc.vector.tensor_copy(q[:, :, 0, :], src))
                        link(tt(r, src, q[:, :, 0, :], ALU.subtract))
                        link(nc.vector.tensor_copy(q[:, :, 1, :], r))
                        tt(q[:, :, 2, :], r, q[:, :, 1, :], ALU.subtract).then_inc(done, 1)

                    def split(l, u):
                        for i in range(2):
                            k = (l * SLOTS + u) * 2 + i
                            f = (qf, kf)[i][u]
                            dve.wait_ge(sp_first, k + 1)
                            if i:
                                dve.wait_ge(sp_done, k)
                            tt(rem[u], f, parts[u][i][:, 0, :], ALU.subtract).then_inc(sp_r, 1)
                            dve.wait_ge(sp_mid, k + 1)
                            tt(parts[u][i][:, 2, :], rem[u], parts[u][i][:, 1, :], ALU.subtract).then_inc(sp_done, 1)

                    def step(kind, *a):
                        k = STEP[(kind, *a)]
                        o = bank[6 + k % 2]
                        u = a[-1]
                        if kind == "ls":
                            dve.wait_ge(step_mm, k + 1)
                            ts(ve[:, u, :], o[:, 0:NT], 1e-5, None, ALU.add).then_inc(step_read[k % 2], 1)
                        elif kind == "lb":
                            i = a[0]
                            dve.wait_ge(step_mm, k + 1)
                            read(dve, "lc", i, u)
                            tt(XC[u][:, :], XC[u][:, :], o[:, :], ALU.mult).then_inc(step_read[k % 2], 1)
                            read(dve, kind, *a)
                            ts(Hh[u][:, :], XC[u][:, :], MOD(i // 2, 3 * (i % 2) + 1, u), MOD(i // 2, 3 * (i % 2), u),
                               ALU.mult, ALU.add).then_inc(ln_h, 1)
                        elif kind == "p" and a[0] == 0:
                            _, u, i = a
                            f = (qf, kf)[i // 2][u]
                            dve.wait_ge(step_mm, k + 1)
                            if i % 2 == 0:
                                tt(f, o[:, :], K("cos"), ALU.mult).then_inc(step_read[k % 2], 1)
                            else:
                                if i == 3:
                                    dve.wait_ge(sp_hi, 2 * u + 1)
                                tt(ropet[u], o[:, :], K("sin"), ALU.mult).then_inc(step_read[k % 2], 1)
                                read(dve, kind, *a)
                                tt(f, f, ropet[u], ALU.add).then_inc(sp_hi, 1)
                        elif kind == "v" and a[0] == 0:
                            split(0, u)
                        elif kind == "hs":
                            dve.wait_ge(step_mm, k + 1)
                            ts(st128[:, u, :], o[:, 0:128], 1e-5, None, ALU.add).then_inc(step_read[k % 2], 1)
                            dve.wait_ge(at_sd, u + 1)
                            link(nc.vector.reciprocal(st128[:, u, :], st128[:, u, :]))
                            three_parts(u, 2 * H, at_rs)
                        elif kind == "hb":
                            u, i = a
                            f = (qf, kf)[i][u]
                            dve.wait_ge(step_mm, k + 1)
                            read(dve, "p", 1, u, i)
                            tt(f, f, o[:, :], ALU.mult).then_inc(step_read[k % 2], 1)
                            read(dve, kind, *a)
                            ts(f, f, V_(("qg", "kg")[i]), V_(("qb", "kb")[i]), ALU.mult, ALU.add).then_inc(sp_hi, 1)
                            if i:
                                split(1, u)
                        elif kind == "a":
                            dve.wait_ge(step_mm, k + 1)
                            nc.vector.tensor_reduce(mx[a[1] % 2][:, a[2]:a[2] + 1], o[:, :], axis=AX.X,
                                                    op=ALU.max).then_inc(step_read[k % 2], 1)
                        elif kind == "m":
                            l, n = a
                            dve.wait_ge(step_mm, k + 1)
                            if l * NU + n >= 2:
                                dve.wait_ge(m_row, 48 * (l * NU + n - 1))
                            m = m3[n % 2]
                            link(ts(m[:, 0, :], o[0:16, 0:128], -1.0, None, ALU.mult))
                            stt(mneg[:, :], o[0:16, 0:128], -1.0, m[:, 0, :], ALU.mult, ALU.subtract) \
                                .then_inc(step_read[k % 2], 1)
                            read(dve, kind, *a)
                            link(nc.vector.tensor_copy(m[:, 1, :], mneg[:, :]))
                            tt(m[:, 2, :], mneg[:, :], m[:, 1, :], ALU.subtract).then_inc(m_spl, 1)
                            dve.wait_ge(m_spl, l * NU + n + 1)
                        elif kind == "dn":
                            dve.wait_ge(step_mm, k + 1)
                            nc.vector.reciprocal(st128[:, u, 0:64], o[:, 0:64]).then_inc(step_read[k % 2], 1)
                            read(dve, kind, *a)
                            three_parts(u, H, den_rec)
                        elif kind == "db":
                            l, u, g = a
                            dve.wait_ge(step_mm, k + 1)
                            tt(raw[u][g], raw[u][g], o[:, :], ALU.mult).then_inc(step_read[k % 2], 1)
                        elif kind == "y":
                            read(dve, kind, *a)
                            tt(X[u][:, :], X[u][:, :], XC[u][:, :], ALU.add).then_inc(x_att, 1)
                        elif kind == "g":
                            one = lambda v, n: v.unsqueeze(2).to_broadcast([128, NT, n])
                            dve.wait_ge(step_mm, k + 1)
                            p = o[:, 0:NT * E].rearrange("p (t e) -> p t e", t=NT)
                            link(nc.vector.tensor_reduce(s4[u], p, axis=AX.X, op=ALU.max))
                            tt(lg[u], p, one(s4[u], E), ALU.subtract).then_inc(step_read[k % 2], 1)
                            dve.wait_ge(gt_exp, u + 1)
                            l3 = lg[u]
                            link(nc.vector.tensor_reduce(s4[u], l3, axis=AX.X, op=ALU.add))
                            link(nc.vector.reciprocal(s4[u], s4[u]))
                            link(tt(l3, l3, one(s4[u], E), ALU.mult))
                            for t in range(NT):
                                link(nc.vector.max(top[u][:, t, :], lg[u][:, t, :]))
                            for t in range(NT):
                                link(nc.vector.max_index(topi[u][:, t, :], top[u][:, t, :], lg[u][:, t, :]))
                            link(nc.vector.tensor_copy(topf[u], topi[u]))
                            link(tt(s4[u], top[u][:, :, 0], top[u][:, :, 1], ALU.add))
                            link(ts(s4[u], s4[u], 1e-20, None, ALU.add))
                            link(nc.vector.reciprocal(s4[u], s4[u]))
                            link(tt(w2v[u], top[u][:, :, 0:2], one(s4[u], 2), ALU.mult))
                            io = K("iota8").unsqueeze(1).to_broadcast([128, NT, E])
                            for j, dst in enumerate((comb[u], c2[u])):
                                link(tt(dst, io, one(topf[u][:, :, j], E), ALU.is_equal))
                                link(tt(dst, dst, one(w2v[u][:, :, j], E), ALU.mult))
                            tt(comb[u], comb[u], c2[u], ALU.add).then_inc(gt_comb, 1)
                    def attention(l):
                        def maxima(n, steps):
                            for s in steps:
                                i = a_count(l, n, s)
                                dve.wait_ge(a_mm, i + 1)
                                nc.vector.tensor_reduce(mx[n % 2][:, s:s + 1], bank[i % 2][:, :], axis=AX.X,
                                                        op=ALU.max).then_inc(a_mx, 1)

                        if l:
                            dve.wait_ge(x_moe, SLOTS)
                        nc.vector.memset(bank[5][:, :], 0.0).then_inc(o_clear, 1)
                        if l == 0:
                            maxima(0, range(16))
                            step("m", 0, 0)
                            maxima(1, range(16))
                        for n in range(NU):
                            for t in range(NT):
                                if n + 2 < NU:
                                    maxima(n + 2, range(NT * t, NT * t + NT))
                                if t == 1 and n + 1 < NU:
                                    step("m", l, n + 1)
                                for st in att_steps[l].get((n, t), []):
                                    step(*st)

                    def moe():
                        def residual(u):
                            dve.wait_ge(mo_dn, 27 * (u + 1))
                            stt(X[u][:, :], bank[4 + u][:, :], MOD(0, 5, u), X[u][:, :], ALU.mult, ALU.add) \
                                .then_inc(x_moe, 1)

                        for m in range(SLOTS * (E + 1) * 3):
                            c, u = CH[m % 3], m // 27
                            dve.wait_ge(mo_sl, m + 1)
                            dve.wait_ge(mo_u, m + 1)
                            if m >= 2:
                                dve.wait_ge(mo_dn, m - 1)
                            tt(hd[u][m % 2][0:c, :], sl[u][m % 2][0:c, :], bank[2 * (m % 2) + 1][0:c, :], ALU.mult) \
                                .then_inc(mo_hd, 1)
                            if m == 28:
                                residual(0)
                            for st in moe_steps.get(m, []):
                                step(*st)
                        residual(1)

                    def layer_norm(i, dst, scale, shift):
                        for u in slots:
                            dve.wait_ge(ln_stat, (i - 4) * SLOTS + u + 1)
                            ts(ve[:, u, :], bank[2 + u][:, 0:NT], 1e-5, None, ALU.add).then_inc(ln_var, 1)
                        for u in slots:
                            dve.wait_ge(ln_xc, (i - 4) * SLOTS + u + 1)
                            dve.wait_ge(ln_bc, (i - 4) * SLOTS + u + 1)
                            link(tt(XC[u][:, :], XC[u][:, :], bank[4 + u][:, :], ALU.mult))
                            ts(dst[u][:, :], XC[u][:, :], scale(u), shift(u), ALU.mult, ALU.add).then_inc(ln_h, 1)

                    def shift(u):
                        nc.vector.tensor_copy(SH[u][0:64, :], Hh[u][0:64, :])
                        nc.vector.tensor_copy(SH[u][64:128, 1:S], Hh[u][64:128, 0:S - 1]).then_inc(sh_ready, 1)

                    def local_layer(d):
                        if d == 0:
                            dve.wait_ge(ln_h, 3 * SLOTS + 1)
                            shift(0)
                        else:
                            for u in slots:
                                dve.wait_ge(z_ffn, (d - 1) * SLOTS + u + 1)
                                shift(u)
                        for i, (t, s) in enumerate((("xa", "qs"), ("xb", "qsr"), ("xai", "ks"), ("xbi", "ksr"))):
                            ts(tab[:, i, :], K(t), V_(f"{s}{d}"), None, ALU.mult).then_inc(tb_ready, 1)
                        dve.wait_ge(tb_ready, 4 * (d + 1))

                        def rotated(u, i):
                            j = (d * SLOTS + u) * 8 + i
                            dve.wait_ge(f_rot, j + 1)
                            tt(qk[u][:, i, :], bank[2 * (i % 2) + 1][:, :], tab[:, 2 * (i // 4) + 1, :], ALU.mult) \
                                .then_inc(f_t2, 1)

                        def squared_norms(u):
                            dve.wait_ge(f_stat, (d * SLOTS + u + 1) * 8)
                            ts(st128[:, u, 0:64], bank[4][:, 0:64], 1e-24, None, ALU.max).then_inc(f_n2, 1)

                        for u in slots:
                            rotated(u, 0)
                            for i in range(8):
                                j = (d * SLOTS + u) * 8 + i
                                if i < 7:
                                    rotated(u, i + 1)
                                dve.wait_ge(f_t1, j + 1)
                                dve.wait_ge(f_t2, j + 1)
                                tt(qk[u][:, i, :], qk[u][:, i, :], xt[i % 2], ALU.add).then_inc(f_tt, 1)
                                if d == 0 and u == 0:
                                    for st in local_steps[i]:
                                        step(*st)
                            squared_norms(u)
                            if d == 0 and u == 0:
                                dve.wait_ge(ln_h, 3 * SLOTS + 2)
                                shift(1)
                        for u in slots:
                            dve.wait_ge(f_sd, d * SLOTS + u + 1)
                            nc.vector.reciprocal(st128[:, u, 0:64], st128[:, u, 0:64]).then_inc(f_r1, 1)
                            dve.wait_ge(f_r1, d * SLOTS + u + 1)
                            three_parts(u, 16, f_rn)
                        for u in slots:
                            for f in range(4):
                                dve.wait_ge(f_bc, (d * SLOTS + u) * 4 + f + 1)
                                tt(qk[u][:, 4 + f, :], qk[u][:, 4 + f, :], bank[f][:, :], ALU.mult).then_inc(f_kn, 1)
                        NW = SLOTS * NT * 2

                        def masked(w):
                            u, t, hq = w // 8, w // 2 % 4, w % 2
                            lo = 0 if t else 64
                            dve.wait_ge(l_s, d * NW + w + 1)
                            if w >= 3:
                                dve.wait_ge(l_tr, d * NW + w - 2)
                            for par in range(2):
                                for j in range(2):
                                    a = (t * 8 + 2 * hq + j) * 2 + par
                                    stt(pr[w % 3][:, par, j, 64 + lo:256],
                                        bank[2 * (w % 2) + par][:, j * 192 + lo:j * 192 + 192],
                                        st128[:, u, a:a + 1], K("mask")[:, lo:192], ALU.mult, ALU.add).then_inc(l_mk, 1)
                            dve.wait_ge(l_mk, 4 * (d * NW + w + 1))
                            link(nc.vector.tensor_reduce(lm[w % 3][:, :, :], pr[w % 3][:, :, :, 64 + lo:256],
                                                         axis=AX.X, op=ALU.max))
                            ts(lm[w % 3][:, :, :], lm[w % 3][:, :, :], -8.0, None, ALU.mult).then_inc(l_nm, 1)

                        def normalise(w):
                            t = w // 2 % 4
                            lo = 64 if t else 128
                            dve.wait_ge(l_ex, 4 * (d * NW + w + 1))
                            link(nc.vector.reciprocal(lrec[w % 3][:, :, :], lsum[w % 3][:, :, :]))
                            for par in range(2):
                                for j in range(2):
                                    p = pr[w % 3][:, par, j, lo:256]
                                    r = ts(p, p, lrec[w % 3][:, par, j:j + 1], None, ALU.mult)
                            r.then_inc(l_p, 1)

                        masked(0)
                        masked(1)
                        for w in range(NW):
                            normalise(w)
                            if 0 < w < NW - 1:
                                masked(w + 1)
                        for u in slots:
                            dve.wait_ge(wo_mm, d * SLOTS + u + 1)
                            tt(Hh[u][:, :], Hh[u][:, :], bank[u][:, :], ALU.add).then_inc(z_att, 1)
                        for u in slots:
                            dve.wait_ge(z_att, d * SLOTS + u + 1)
                            shift(u)
                        layer_norm(4 + d, G, lambda u: V_(f"lg{d}"), lambda u: V_(f"lb{d}"))
                        for m in range(6):
                            u, c = divmod(m, 3)
                            dve.wait_ge(w1_gl, d * 6 + m + 1)
                            if m >= 2:
                                dve.wait_ge(w2_mm, d * 6 + m - 1)
                            stt(ghd[m % 2][0:GC[c], :], bank[2 * (m % 2)][0:GC[c], :], V_(f"b1{d}")[0:GC[c], c:c + 1],
                                glu[m % 2][0:GC[c], :], ALU.add, ALU.mult).then_inc(w1_hd, 1)
                        for u in slots:
                            dve.wait_ge(w2_mm, d * 6 + 3 * (u + 1))
                            stt(Hh[u][:, :], bank[6 + u][:, :], V_(f"b2{d}"), Hh[u][:, :], ALU.add, ALU.add) \
                                .then_inc(z_ffn, 1)

                    nc.vector.tensor_copy(modu[:, :, :], mod[:, :, bass.ts(turn, SLOTS)]).then_inc(mod_ready, 1)
                    dve.wait_ge(mod_ready, 1)
                    for st in start:
                        step(*st)
                    attention(0)
                    moe()
                    attention(1)
                    for d in range(DEPTH):
                        local_layer(d)
                    for u in slots:
                        dve.wait_ge(z_ffn, (DEPTH - 1) * SLOTS + u + 1)
                        stt(X[u][:, :], Hh[u][:, :], MOD(1, 5, u), X[u][:, :], ALU.mult, ALU.add).then_inc(x_last, 1)

                @block.gpsimd
                def _(pool):
                    tt = nc.gpsimd.tensor_tensor

                    def power(ready, n, u):
                        pool.wait_ge(ready, n)
                        tt(rs[:, u, :], ve[:, u, :], mhalf[:, :], ALU.pow).then_inc(ln_rstd, 1)

                    def norm_step(i, u):
                        read(pool, "ls", i, u)
                        tt(rs[:, u, :], ve[:, u, :], mhalf[:, :], ALU.pow).then_inc(ln_rstd, 1)

                    def value_tile(l, u):
                        nc.gpsimd.memset(vaug[u], 0.0).then_inc(zeroed, 1)
                        pool.wait_ge(zeroed, l * SLOTS + u + 1)
                        nc.gpsimd.memset(vaug[u][:, :, :, DH:DH + 1], 1.0).then_inc(vaug_one, 1)

                    def scaled(m):
                        u, e = divmod(m, E)
                        pool.wait_ge(cb_rd[m % 4], 16 * (m // 4 + 1))
                        if e >= 2:
                            pool.wait_ge(mo_u, u * 27 + 3 * e)
                        tt(hx[u][e % 2], Hh[u][:, :], cb[m % 4], ALU.mult).then_inc(hx_ready, 1)

                    def clear_stacks(pieces):
                        for k in pieces:
                            w = 2 * RING * GRP * S // 2 // CLEARS
                            nc.gpsimd.memset(stacks[:, w * k:w * (k + 1)], 0.0).then_inc(ring_clear, 1)

                    clear_stacks(range(CLEARS))
                    norm_step(0, 0)
                    norm_step(0, 1)
                    value_tile(0, 0)
                    value_tile(0, 1)
                    norm_step(1, 0)
                    pool.wait_ge(pv_done, NU * NT)
                    for e in range(2):
                        scaled(e)
                    norm_step(1, 1)
                    for e in range(2, E):
                        scaled(e)
                    scaled(E)
                    norm_step(2, 0)
                    value_tile(1, 0)
                    for e in range(1, E):
                        scaled(E + e)
                        if e == 1:
                            pool.wait_ge(mo_dn, 27)
                        if e <= CLEARS:
                            clear_stacks(range(e - 1, e))
                    norm_step(2, 1)
                    value_tile(1, 1)
                    norm_step(3, 0)
                    for d in range(DEPTH):
                        for u in slots:
                            for i in range(8):
                                j = (d * SLOTS + u) * 8 + i
                                pool.wait_ge(tb_ready, 4 * (d + 1))
                                pool.wait_ge(f_cp, j + 1)
                                if u or i >= 2:
                                    pool.wait_ge(f_tt, j - 1)
                                tt(xt[i % 2], qs[i % 2], tab[:, 2 * (i // 4), :], ALU.mult).then_inc(f_t1, 1)
                                if d == 0 and u == 0 and i == 6:
                                    norm_step(3, 1)
                        for u in slots:
                            power(ln_var, d * SLOTS + u + 1, u)
            nc.gpsimd.sem_clear(range(first, last + 1))
            nc.all_engine_barrier()


def lay_out(v):
    f = {k: np.asarray(a) for k, a in v.items()}

    def pad(a, rows):
        out = np.zeros((rows,) + a.shape[1:], a.dtype)
        out[:a.shape[0]] = a
        return out

    def swapped(w, width):
        return np.roll(w.reshape(w.shape[0], -1, width), width // 2, axis=2).reshape(w.shape)

    att = {}
    w = f["L0_attn_w_qkv"]
    att["q0"], att["k0"], att["v0"] = w[:, :C], w[:, C:2 * C], w[:, 2 * C:]
    att["qr0"], att["kr0"] = swapped(att["q0"], DH), swapped(att["k0"], DH)
    w = f["L1_attn_w_qkv"]
    att["qT1"], att["kT1"], att["v1"] = w[:, :C].T, w[:, C:2 * C].T, w[:, 2 * C:]
    for l in range(2):
        wp = f[f"L{l}_attn_w_proj"].reshape(NG, GRP, DH, C)
        out = np.zeros((GRP, 32, NG, C), wp.dtype)
        out[:, :DH] = wp.transpose(1, 2, 0, 3)
        att[f"p{l}"] = out.reshape(128, NG * C)
    att_w = np.concatenate([att[n] for n, _ in ATT_SIZES], axis=1)

    moe = {"gate": f["L0_ffn_gate_w"].T}
    for n, s_, e_ in (("g", "shared_gate", "expert_gate"), ("u", "shared_up", "expert_up")):
        w = np.concatenate([f["L0_ffn_" + s_][None], f["L0_ffn_" + e_]])
        moe[n] = w.transpose(2, 0, 1).reshape(C, -1)
    w = np.concatenate([f["L0_ffn_shared_down"][None], f["L0_ffn_expert_down"]]).transpose(2, 0, 1)
    moe["d"] = pad(w, 384).reshape(3, 128, E + 1, C).transpose(1, 2, 0, 3).reshape(128, -1)
    moe_w = np.concatenate([moe[n] for n, _ in MOE_SIZES], axis=1)

    ffn, vec = {}, {}
    twice = lambda a: np.concatenate([a, a])
    col = lambda a: a.reshape(-1, 1)
    for d in range(DEPTH):
        w = f["L1_ffn_wqkv"][d]
        q, k, ffn[f"v{d}"] = w[:, :QKV], w[:, QKV:2 * QKV], w[:, 2 * QKV:]
        ffn[f"q{d}"], ffn[f"qr{d}"] = q, swapped(q, LD)
        ffn[f"k{d}"], ffn[f"kr{d}"] = k, swapped(k, LD)
        ffn[f"wo{d}"] = f["L1_ffn_wo"][d].reshape(4, 128, C).transpose(1, 0, 2).reshape(128, -1)
        ffn[f"w1{d}"] = f["L1_ffn_w1"][d]
        ffn[f"w2{d}"] = pad(f["L1_ffn_w2"][d], 384).reshape(3, 128, C).transpose(1, 0, 2).reshape(128, -1)
        for n, src in (("qs", "q_scale"), ("ks", "k_scale")):
            a = f["L1_ffn_" + src][d]
            vec[f"{n}{d}"] = col(twice(a))
            vec[f"{n}r{d}"] = col(twice(np.roll(a, LD // 2)))
        vec[f"lg{d}"], vec[f"lb{d}"] = col(f["L1_ffn_ln_g"][d]), col(f["L1_ffn_ln_b"][d])
        b1 = f["L1_ffn_b1"][d]
        vec[f"b1{d}"] = np.concatenate([pad(b1[k * GH:(k + 1) * GH], 384).reshape(3, 128) for k in range(2)]).T
        vec[f"b2{d}"] = col(f["L1_ffn_b2"][d])
    vec["bproj"] = col(f["L0_attn_b_proj"])
    for n, src in (("qg", "q_gamma"), ("qb", "q_beta"), ("kg", "k_gamma"), ("kb", "k_beta")):
        vec[n] = col(np.tile(f["L1_attn_" + src], H))
    ffn_w = np.concatenate([ffn[n] for n, _ in FFN_SIZES], axis=1)
    vec = np.concatenate([vec[n] for n, _ in VEC_SIZES], axis=1)
    cT = np.concatenate([f["L0_c"].T, f["L1_c"].T], axis=1)
    wmod = np.stack([f["L0_wmod"], f["L1_wmod"]])
    ones = np.full((3, H * S // 2), 0x3F803F80, np.uint32).view(np.float32)
    return {"x": f["L0_attn_x"], "consts": constants(), "sel": selectors(), "ones": ones, "att_w": att_w, "moe_w": moe_w,
            "ffn_w": ffn_w, "vec": vec, "cT": cT, "wmod": wmod}


def kernel(**inputs):
    import concourse.bacc as bacc
    from concourse.bass_utils import run_bass_kernel_spmd

    nc = bacc.Bacc("TRN2", target_bir_lowering=False, num_devices=1)
    arrays, args = {}, []
    for name, a in lay_out(inputs).items():
        a = np.ascontiguousarray(a)
        arrays[f"in_{name}"] = a
        args.append(nc.dram_tensor(f"in_{name}", a.shape, mybir.dt.from_np(a.dtype), kind="ExternalInput").ap())
    args.append(nc.dram_tensor("out", (B, S, C), F32, kind="ExternalOutput").ap())
    adaln_kernel(nc, *args)
    return run_bass_kernel_spmd(nc, [arrays], core_ids=[0]).results[0]["out"]
```

```python
import numpy as np
import concourse.bass as bass
from concourse import mybir
from contextlib import ExitStack

F32 = mybir.dt.float32
BF16 = mybir.dt.bfloat16
U32 = mybir.dt.uint32
ALU = mybir.AluOpType
ACT = mybir.ActivationFunctionType
AX = mybir.AxisListType

B, S, C = 8, 512, 128
SLOTS = 2
NT = S // 128
H, DH = 16, 8
GRP = 4
NG = H // GRP
E, HID = 8, 352
CH = [128, 128, 96]
LH, LD, WIN = 8, 64, 64
DEPTH = 2
GH = 341
GC = [128, 128, 85]
MASKED = -1e30
TERMS = 6
KR = TERMS * DH
MR = 96
RING = 4


def columns(sizes):
    at, out = 0, {}
    for name, n in sizes:
        out[name] = (at, at + n)
        at += n
    return out, at


CONST_SIZES = [("ident", 128), ("center", 128), ("center8", 128), ("inv", 1), ("blk16", H), ("blk2", 2),
               ("sel4", GRP), ("iota8", E), ("cos", S), ("sin", S), ("xa", S), ("xb", S), ("xai", S),
               ("xbi", S), ("mask", 192)]
SEL_SIZES = [("o", NG * 128), ("h", 2 * 128), ("n", 4 * 128), ("ident", 128)]
ATT_SIZES = [("q0", 128), ("qr0", 128), ("k0", 128), ("kr0", 128), ("v0", 128), ("qT1", 128),
             ("kT1", 128), ("v1", 128), ("p0", NG * 128), ("p1", NG * 128)]
MOE_SIZES = [("gate", E), ("g", (E + 1) * HID), ("u", (E + 1) * HID), ("d", (E + 1) * 3 * 128)]
QKV = 4 * 128
FFN_ONE = [("q", QKV), ("qr", QKV), ("k", QKV), ("kr", QKV), ("v", QKV), ("wo", 4 * 128),
           ("w1", 2 * GH), ("w2", 3 * 128)]
VEC_SIZES = [("bproj", 1), ("qg", 1), ("qb", 1), ("kg", 1), ("kb", 1)] + [
    (f"{n}{d}", w) for d in range(DEPTH)
    for n, w in (("qs", 1), ("qsr", 1), ("ks", 1), ("ksr", 1), ("lg", 1), ("lb", 1), ("b1", 6), ("b2", 1))]
FFN_SIZES = [(f"{n}{d}", w) for d in range(DEPTH) for n, w in FFN_ONE]
CC, NC_ = columns(CONST_SIZES)
AC, NA_ = columns(ATT_SIZES)
MC, NM_ = columns(MOE_SIZES)
FC, NF_ = columns(FFN_SIZES)
VC, NV_ = columns(VEC_SIZES)
SC, NS_ = columns(SEL_SIZES)


def constants():
    t = {}
    t["ident"] = np.eye(128)
    t["center"] = np.eye(128) - 1.0 / 128
    blk = np.kron(np.eye(H), np.ones((DH, DH))) / DH
    t["center8"] = np.eye(128) - blk
    t["inv"] = np.full((128, 1), 1.0 / 128)
    t["blk16"] = np.kron(np.eye(H), np.ones((DH, 1))) / DH
    t["blk2"] = np.kron(np.eye(2), np.ones((LD, 1)))
    sel = np.zeros((128, GRP))
    for j in range(GRP):
        sel[32 * j + DH, j] = 1.0
    t["sel4"] = sel
    t["iota8"] = np.tile(np.arange(E), (128, 1))
    f4 = np.float32
    tok = np.arange(S, dtype=f4)
    inv = (f4(1.0) / f4(10000.0) ** (np.arange(0, DH, 2, dtype=f4) / f4(DH))).astype(f4)
    fr = tok[None, :] * inv[:, None]
    cos, sin = np.cos(fr), np.sin(fr)
    t["cos"] = np.tile(np.concatenate([cos, cos]), (H, 1))
    t["sin"] = np.tile(np.concatenate([-sin, sin]), (H, 1))
    half = np.arange(0, LD, 2, dtype=f4)
    inv = (f4(1.0) / f4(10000.0) ** (half / f4(LD))).astype(f4)
    fr = tok[None, :] * inv[:, None]
    base = (half + f4(0.4 * LD)) / f4(1.4 * LD)
    scale = base[:, None] ** ((tok - S // 2) / f4(WIN // 2))[None, :]
    cos, sin = np.cos(fr), np.sin(fr)
    two = lambda a, b: np.tile(np.concatenate([a, b]), (2, 1))
    t["xa"] = two(cos * scale, cos * scale)
    t["xb"] = two(-sin * scale, sin * scale)
    t["xai"] = two(cos / scale, cos / scale)
    t["xbi"] = two(-sin / scale, sin / scale)
    i, j = np.arange(128)[:, None], np.arange(192)[None, :] - 64
    t["mask"] = np.where((i < j) | (i > j + WIN), MASKED, 0.0)
    return np.concatenate([t[n].astype(np.float32) for n, _ in CONST_SIZES], axis=1)


def selectors():
    o, h, n = np.zeros((3, H, NG, GRP, 32)), np.zeros((3, 2 * H, 2, H, DH)), np.zeros((3, 16, 4, 2, LD))
    for g in range(NG):
        for k in range(GRP):
            o[:, GRP * g + k, g, k] = 1.0
    for k in range(2):
        for head in range(H):
            h[:, k * H + head, k, head] = 1.0
    for f in range(4):
        for k in range(2):
            n[:, (4 + f) * 2 + k, f, k] = 1.0
    out = np.zeros((128, NS_), np.float32)
    for name, a in (("o", o), ("h", h), ("n", n)):
        a = a.reshape(a.shape[0] * a.shape[1], -1)
        out[:a.shape[0], SC[name][0]:SC[name][1]] = a
    out[:, SC["ident"][0]:] = np.eye(128)
    return out


def schedule(only_head):
    head = [("x", 0)] + [(k, 0, 0) for k in ("lc", "ls", "lb")] + [("p", 0, 0, i) for i in range(4)] + \
        [("v", 0, 0), ("s", 0, 0, 0), ("s", 0, 0, 1)]
    start = [("x", 1)] + [(k, 0, 1) for k in ("lc", "ls", "lb")]
    att = [{}, {}]
    att[0].update({(0, 0): [("p", 0, 1, 0), ("p", 0, 1, 1)], (0, 1): [("p", 0, 1, 2), ("p", 0, 1, 3)],
                   (0, 2): [("v", 0, 1)]})
    att[1].update({(0, 0): [("lc", 2, 1), ("ls", 2, 1)], (0, 1): [("lb", 2, 1)],
                   (0, 2): [("p", 1, 1, 0), ("p", 1, 1, 1)], (0, 3): [("hs", 1), ("v", 1, 1)],
                   (1, 0): [("hr", 1)], (1, 1): [("hb", 1, 0), ("hb", 1, 1)]})

    def way_out(l, u):
        return [[("dn", l, u)], [("dr", l, u)], [("db", l, u, 0), ("db", l, u, 1)],
                [("db", l, u, 2), ("db", l, u, 3)], [("y", l, u)], [("lc", 2 * l + 1, u)],
                [("ls", 2 * l + 1, u)], [("lb", 2 * l + 1, u)]]

    for l in range(2):
        for k, steps in enumerate(way_out(l, 0)):
            att[l][divmod(4 * NG + 2 + k, NT)] = steps
    att[0][(6, 3)] = [("g", 0)]
    att[0][(7, 2)] = [("c", 0)]
    moe = {k + 1: steps for k, steps in enumerate(way_out(0, 1))}
    moe.update({10: [("g", 1)], 13: [("c", 1)], 29: [("lc", 2, 0)], 30: [("ls", 2, 0)], 31: [("lb", 2, 0)],
                32: [("p", 1, 0, 0), ("p", 1, 0, 1), ("hs", 0)], 33: [("v", 1, 0)], 34: [("hr", 0)],
                35: [("hb", 0, 0), ("hb", 0, 1)]})
    for k in range(32):
        moe.setdefault(41 + k // 3, []).append(("a", 1, k // 16, k % 16))
    moe[53] = [("m", 1, 0)]

    def norms(d, u):
        return [("nr", d, u)] + [("nb", d, u, f) for f in range(4)]

    def feed_forward(d, u):
        return [("wo", d, u)] + [(k, 4 + d, u) for k in ("lc", "ls", "lb")] + \
            [(k, d, u, c) for k in ("fg", "fa") for c in range(3)] + [("f2", d, u)]

    lp = [[{}, {}], [{}, {}]]
    lp[0][0] = dict(enumerate(way_out(1, 1)))
    for d in range(DEPTH):
        n = norms(d, 0)
        lp[d][1] = {3: n[0:1], 4: n[1:3], 6: n[3:5]}
    f = feed_forward(0, 1)
    lp[1][0] = {0: f[0:1], 1: f[1:2], 2: f[2:3], 3: f[3:4], 4: f[4:6], 5: f[6:7], 6: f[7:9], 7: f[9:11]}
    lw = [{}, {}]
    for d in range(DEPTH):
        lw[d].update(zip(((3, 0), (4, 0), (4, 1), (5, 0), (5, 1)), ([st] for st in norms(d, 1))))
        lw[d].update(zip(((9, 1), (10, 0), (10, 1), (11, 0), (11, 1), (12, 0), (12, 1), (13, 0), (13, 1), (14, 0),
                          (14, 1)), ([st] for st in feed_forward(d, 0))))
    f = feed_forward(1, 1)
    end = [("o", 0), f[0], head[0], f[1], head[1], f[2], head[2], f[3], head[3], f[4], f[5], *head[4:6], f[6],
           *head[6:8], f[7], head[8], head[9], *f[8:10], head[10], f[10], ("o", 1)]
    order = [("one bank", "attention", 0)] + start
    for l in range(2):
        if l == 0:
            order.append(("m", 0, 0))
        else:
            order.append(("one bank", "attention", 1))
        for n in range(2 * NG):
            for t in range(NT):
                steps = att[l].get((n, t), [])
                order += steps[0:1]
                if t == 1 and n + 1 < 2 * NG:
                    order.append(("m", l, n + 1))
                order += steps[1:]
        order.append(("two banks",))
        if l == 0:
            for m in range(54):
                order += moe.get(m, [])
    for d in range(DEPTH):
        for u in range(2):
            for i in range(8):
                order += lp[d][u].get(i, [])
        order.append(("one bank", "local", d))
        for w in range(16):
            for k in range(2):
                order += lw[d].get((w, k), [])
        order.append(("two banks",))
    order += end
    if only_head:
        end = order = head
    where, count, turn, k, both = {}, [0, 0], 0, 0, True
    before = {}
    for step in order:
        if step[0] == "s":
            continue
        if step[0] in ("one bank", "two banks"):
            both = step[0] == "two banks"
            before[step[1:]] = count[0]
            continue
        b = turn if both else 1
        turn = 1 - b
        where[step] = (k, b, count[b])
        count[b] += 1
        k += 1
    return start, att, moe, lp, lw, end, where, before


def adaln_kernel(nc, x, consts, sel, ones, att_w, moe_w, ffn_w, vec, cT, wmod, out):
    ctx = ExitStack()
    with ctx:
        def sb(name, shape, dt=F32):
            return ctx.enter_context(nc.sbuf_tensor(name, shape, dt))

        sems = []

        def sem(name):
            s = ctx.enter_context(nc.semaphore(name))
            sems.append(s)
            return s

        bank = [ctx.enter_context(nc.psum_tensor(f"bank{i}", [128, 512], F32)) for i in range(8)]

        cst = sb("cst", [128, NC_])
        selb = sb("selb", [128, NS_], BF16)
        aw = sb("aw", [128, NA_])
        mw = sb("mw", [128, NM_])
        fw = sb("fw", [128, NF_])
        vc = sb("vc", [128, NV_])
        wqc = sb("wqc", [128, 2, 128])
        mod = sb("mod", [128, 14, B + SLOTS])
        modu = sb("modu", [128, 14, SLOTS])

        def K(n):
            return cst[:, CC[n][0]:CC[n][1]]

        def AW(n):
            return aw[:, AC[n][0]:AC[n][1]]

        def MW(n):
            return mw[:, MC[n][0]:MC[n][1]]

        def FW(n, d):
            return fw[:, FC[f"{n}{d}"][0]:FC[f"{n}{d}"][1]]

        def V_(n):
            return vc[:, VC[n][0]:VC[n][1]]

        def MOD(l, j, u):
            return modu[:, 7 * l + j, u:u + 1]

        def SEL(n):
            return selb[:, SC[n][0]:SC[n][1]]

        ident = K("ident")
        identb = SEL("ident")
        X = [sb(f"X{u}", [128, S]) for u in range(SLOTS)]
        Hh = [sb(f"H{u}", [128, S]) for u in range(SLOTS)]
        G = [sb(f"G{u}", [128, S]) for u in range(SLOTS)]
        SH = [sb(f"SH{u}", [128, S]) for u in range(SLOTS)]
        XC = [sb(f"XC{u}", [128, S]) for u in range(SLOTS)]
        SQ = [sb(f"SQ{u}", [128, S]) for u in range(SLOTS)]
        ve = sb("ve", [128, SLOTS, NT])
        rs = sb("rs", [128, SLOTS, NT])
        mhalf = sb("mhalf", [128, NT])
        st128 = sb("st128", [128, SLOTS, 128])
        ARENA = 20480
        ar = sb("stage_memory", [128, ARENA])
        cur = [0]

        def part(n):
            a = cur[0]
            cur[0] += n
            assert cur[0] <= ARENA, cur[0]
            return ar[:, a:a + n]

        stacks = ar[:, 0:2 * RING * GRP * S // 2]
        qst = part(RING * GRP * S // 2).bitcast(BF16).rearrange("p (r h t) -> p r h t", r=RING, h=GRP)
        kst32 = part(RING * GRP * S // 2)
        kst = kst32.bitcast(BF16).rearrange("p (r h t) -> p r h t", r=RING, h=GRP)
        vaug = [part(NT * H * 16).rearrange("p (t h c) -> p t h c", t=NT, h=H) for u in range(SLOTS)]
        PTB = 8
        pt = [part(S) for _ in range(PTB)]
        raw = [None, None]
        raw[1] = [part(S) for g in range(NG)]
        raw[0] = [part(S) for g in range(NG)]
        qf = [raw[u][0] for u in range(SLOTS)]
        kf = [raw[u][1] for u in range(SLOTS)]
        rem = [raw[u][2] for u in range(SLOTS)]
        ropet = [raw[u][3] for u in range(SLOTS)]
        free_at = cur[0]
        cur[0] = 0
        off = 2 * H * S // 2 + SLOTS * NT * H * 16
        parts = [[ar[:, a + 768 * i:a + 768 * (i + 1)].bitcast(BF16).rearrange("p (j t) -> p j t", j=3)
                  for i in range(2)] for a in (off, free_at)]
        cur[0] = free_at
        cb = [part(S) for _ in range(4)]
        moe_at = (0, off + 2 * 1536)
        hx, sl, hd = ([[ar[:, moe_at[u] + S * (2 * k + i):moe_at[u] + S * (2 * k + i + 1)] for i in range(2)]
                       for u in range(SLOTS)] for k in range(3))
        cbT = SQ
        g_at = [0]

        def small(n):
            a = g_at[0]
            g_at[0] += NT * n
            return [G[u][:, a:a + NT * n].rearrange("p (t e) -> p t e", t=NT) for u in range(SLOTS)]

        lg, top, topf, comb, c2, w2v = (small(n) for n in (E, 8, 8, E, E, 2))
        topi = [a.bitcast(U32) for a in small(8)]
        s4 = [a.rearrange("p t e -> p (t e)") for a in small(1)]
        cur[0] = 0
        qk = [part(8 * S).rearrange("p (i t) -> p i t", i=8) for u in range(SLOTS)]
        vv = [part(NT * S).rearrange("p (t f) -> p t f", t=NT) for u in range(SLOTS)]
        pr_at = cur[0]
        qs = [part(S) for _ in range(2)]
        sqr = [part(S) for _ in range(2)]
        cur[0] = pr_at
        prf = [part(4 * 256) for _ in range(3)]
        pr = [p.rearrange("p (a j k) -> p a j k", a=2, j=2) for p in prf]
        ptc = [part(512) for _ in range(2)]
        xt = [part(S) for _ in range(2)]
        tab = part(4 * S).rearrange("p (i t) -> p i t", i=4)
        ptp = [part(512) for _ in range(2)]
        sqr.append(ptp[1])
        gated = [[tab[:, c, :] for c in range(3)], [ptc[0], ptc[1], ptp[0]]]
        cur[0] = 0
        stp = [sb(f"stp{u}", [128, NT, 3, 2 * H], BF16) for u in range(SLOTS)]
        strem = sb("strem", [128, SLOTS, 128])
        rows = [XC[u][:, :].bitcast(BF16)[:, 0:S] for u in range(SLOTS)]

        mx = [sb(f"mx{i}", [128, 16]) for i in range(2)]
        mneg = sb("mneg", [16, 128])
        m3 = [sb(f"m3_{i}", [16, 3, 128], BF16) for i in range(2)]
        rec = st128
        lm = [sb(f"lm{i}", [128, 2, 2]) for i in range(3)]
        lsum = [sb(f"lsum{i}", [128, 2, 2]) for i in range(3)]
        lrec = [sb(f"lrec{i}", [128, 2, 2]) for i in range(3)]

        scr = nc.dram_tensor("scr_parts", (2, SLOTS, 2, 3, DH, H * S), BF16, kind="Internal").ap()
        scr_c = nc.dram_tensor("scr_comb", (SLOTS, E, S), F32, kind="Internal").ap()

        s_load = sem("s_load")
        s_pe0 = sem("s_pe0")
        s_act0 = sem("s_act0")
        s_dve0 = sem("s_dve0")
        s_pool0 = sem("s_pool0")
        ct = ar[:, 0:2 * B]
        wm = ar[:, 1024:1024 + 2 * 6 * C].rearrange("p (l n) -> p l n", l=2)
        selt = ar[:, 8192:8192 + NS_]
        mtmp = ar[:, 4096:4096 + 2 * 4 * B].rearrange("p (l j b) -> p l j b", l=2, j=4)
        with nc.Block() as block:
            @block.sync
            def _(sp):
                for dst, src in ((selt, sel), (ct, cT), (wm, wmod.rearrange("l p n -> p l n")), (vc[:, :], vec),
                                 (cst[:, :], consts), (aw[:, :], att_w), (mw[:, :], moe_w), (fw[:, :], ffn_w)):
                    sp.dma_start(dst, src).then_inc(s_load, 16)
                sp.wait_ge(s_load, 16 * 8)

            @block.gpsimd
            def _(pool):
                nc.gpsimd.memset(mhalf[:, :], -0.5).then_inc(s_pool0, 1)
                nc.gpsimd.memset(mod[:, :, B:], 0.0).then_inc(s_pool0, 1)
                for u in range(SLOTS):
                    nc.gpsimd.memset(SH[u][:, :], 0.0).then_inc(s_pool0, 1)

            @block.scalar
            def _(act):
                act.wait_ge(s_load, 16 * 8)
                nc.scalar.activation(ct, ct, ACT.Silu).then_inc(s_act0, 1)

            @block.tensor
            def _(pe):
                pe.wait_ge(s_load, 16 * 8)
                pe.wait_ge(s_act0, 1)
                for l in range(2):
                    for j in range(6):
                        nc.tensor.matmul(bank[0][:, (6 * l + j) * B:(6 * l + j + 1) * B],
                                         wm[:, l, j * C:(j + 1) * C], ct[:, l * B:(l + 1) * B],
                                         start=True, stop=True).then_inc(s_pe0, 1)
                for i, n in enumerate(("qT1", "kT1")):
                    nc.tensor.matmul(bank[1][:, i * 128:(i + 1) * 128], AW(n), K("center8"),
                                     start=True, stop=True).then_inc(s_pe0, 1)

            @block.vector
            def _(dve):
                done = [0]

                def step(ins):
                    done[0] += 1
                    ins.then_inc(s_dve0, 1)
                    dve.wait_ge(s_dve0, done[0])

                dve.wait_ge(s_pe0, 14)
                step(nc.vector.tensor_copy(selb[:, :], selt))
                step(nc.vector.tensor_copy(wqc[:, :, :], bank[1][:, 0:256].rearrange("p (i c) -> p i c", i=2)))
                m = mod[:, :, 0:B].rearrange("p (l j) b -> p l j b", l=2)
                step(nc.vector.tensor_copy(m[:, :, 0:6, :],
                                           bank[0][:, 0:12 * B].rearrange("p (l j b) -> p l j b", l=2, j=6)))
                for j in (1, 4):
                    step(nc.vector.tensor_scalar(m[:, :, j, :], m[:, :, j, :], 1.0, None, ALU.add))
                for j in (2, 5):
                    g, a, s = m[:, :, j, :], mtmp[:, :, 0, :], mtmp[:, :, 1, :]
                    step(nc.vector.tensor_scalar(a, g, -1.0, None, ALU.mult))
                    step(nc.vector.tensor_tensor(a, a, g, ALU.max))
                    step(nc.vector.tensor_scalar(s, g, 0.0, 2.0, ALU.is_ge, ALU.mult))
                    step(nc.vector.tensor_scalar(s, s, 1.0, None, ALU.subtract))
                    step(nc.vector.tensor_scalar(a, a, 0.25, None, ALU.max))
                    step(nc.vector.tensor_tensor(g, a, s, ALU.mult))
                step(nc.vector.tensor_scalar(m[:, :, 6, :], m[:, :, 2, :], V_("bproj"), None, ALU.mult))
                step(nc.vector.tensor_scalar(m[:, 1, 6, :], m[:, 1, 2, :], 0.0, None, ALU.mult))

        x_in = [sem(f"x_in{u}") for u in range(SLOTS)]; step_mm = sem("step_mm"); step_read = [sem(f"step_read{i}") for i in range(2)]; f_r1 = sem("f_r1")
        mod_ready = sem("mod_ready")
        dve_link = sem("dve_link"); zeroed = sem("zeroed"); sp_first = sem("sp_first"); l_evp = sem("l_evp")
        ln_sq = sem("ln_sq")
        ln_rstd = sem("ln_rstd"); ln_h = sem("ln_h")

        at_sq = sem("at_sq"); at_sd = sem("at_sd")
        at_rs = sem("at_rs")
        sp_hi = sem("sp_hi"); sp_r = sem("sp_r"); sp_pool = sem("sp_pool"); sp_mid = sem("sp_mid"); sp_done = sem("sp_done")
        vaug_one = sem("vaug_one")
        st_wr = [sem(f"st_wr{u}") for u in range(SLOTS)]
        st_rd = [sem(f"st_rd{i}") for i in range(RING)]
        ring_clear = sem("ring_clear"); ones_rd = sem("ones_rd")
        a_mm = sem("a_mm"); a_mx = sem("a_mx"); m_spl = sem("m_spl"); m_row = sem("m_row")
        s_mm = sem("s_mm"); e_done = sem("e_done"); pv_done = sem("pv_done"); o_raw = sem("o_raw"); o_clear = sem("o_clear")
        den_rec = sem("den_rec")
        x_att = sem("x_att")
        gt_exp = sem("gt_exp"); gt_comb = sem("gt_comb")
        cb_wr = sem("cb_wr")
        cb_rd = [sem(f"cb_rd{u}") for u in range(4)]
        hx_ready = sem("hx_ready"); mo_g = sem("mo_g"); mo_u = sem("mo_u"); mo_sl = sem("mo_sl")
        mo_hd = sem("mo_hd"); mo_dn = sem("mo_dn"); x_moe = sem("x_moe")
        sh_ready = [sem(f"sh_ready{u}") for u in range(SLOTS)]; tb_ready = sem("tb_ready")
        f_main = sem("f_main"); f_rot = sem("f_rot"); f_cp = sem("f_cp"); f_sq = sem("f_sq")
        f_t1 = sem("f_t1"); f_t2 = sem("f_t2"); f_tt = sem("f_tt"); f_stat = sem("f_stat")
        f_v = sem("f_v"); f_vc = sem("f_vc"); f_n2 = sem("f_n2"); f_sd = sem("f_sd"); f_rn = sem("f_rn")
        l_s = sem("l_s"); l_mk = sem("l_mk"); l_nm = sem("l_nm"); l_ex = sem("l_ex"); l_p = sem("l_p")
        l_tr = sem("l_tr"); l_ev = sem("l_ev"); l_pv = sem("l_pv"); l_o = sem("l_o")
        w1_gl = sem("w1_gl")
        x_last = sem("x_last"); o_dma = sem("o_dma")
        turn_sems = sems[5:]
        first, last = turn_sems[0].num, turn_sems[-1].num
        assert last - first == len(turn_sems) - 1

        xv = x.rearrange("(w u) (t p) c -> u p w t c", p=128, u=SLOTS)
        ov = out.rearrange("(w u) (t p) c -> u p w t c", p=128, u=SLOTS)
        xin = [XC[u][:, :].rearrange("p (o t c) -> p o t c", o=1, t=NT) for u in range(SLOTS)]
        modv = mod[:, :, :].rearrange("p k (w u) -> p w k u", u=SLOTS)
        slots = range(SLOTS)
        NU = SLOTS * NG
        LNS = 6
        NW = SLOTS * NT * 2
        CLEARS = 4

        def early(steps, k):
            n = 2 if steps and steps[0][0] == "a" else 0
            return steps[n:] if k == 2 else steps[k:k + 1] if n else []

        def a_count(l, n, s):
            return l * NU * 16 + (n - 2 * l) * 16 + s

        def program(turn, only_head):
            start, att_steps, moe_steps, lp_steps, lw_steps, end_steps, STEP, bank6_steps = schedule(only_head)

            def read(engine, *name):
                _, b, n = STEP[name]
                engine.wait_ge(step_read[b], n + 1)

            def ln_n(i, u):
                return 0 if only_head else (i * SLOTS + u - 1) % (LNS * SLOTS)

            def at_n(l, u):
                return 0 if only_head else (l * SLOTS + u - 1) % (2 * SLOTS)

            def split_n(l, u):
                return 0 if only_head else at_n(l, u) - 1

            def of_turn(a, ahead):
                return a[:, 0:1] if only_head else a[:, ahead:][:, bass.ds(turn, 1)]

            with nc.Block() as block:
                @block.sync
                def _(sp):
                    def tokens_in(u, ahead):
                        sp.dma_start(xin[u], of_turn(xv[u], ahead)).then_inc(x_in[u], 16)

                    def parts_out(l, u):
                        for i in range(2):
                            sp.wait_ge(sp_done, at_n(l, u) * 2 + i + 1)
                            for j in range(3):
                                sp.dma_start(scr[l, u, i, j, :, :].rearrange("d (h t) -> h d t", h=H),
                                             parts[u][i][:, j, :]).then_inc(st_wr[u], 16)

                    def rows_of_ones(l):
                        if l:
                            sp.wait_ge(ring_clear, CLEARS)
                        sp.dma_start(kst32[MR:MR + 3, :], ones).then_inc(ones_rd, 16)

                    def stack(l, n):
                        u, g = divmod(n, NG)
                        if g == 0 and (l or u):
                            sp.wait_ge(st_wr[u], 96 * (l + u))
                        if n >= RING:
                            sp.wait_ge(s_mm, (l * NU + n - RING + 1) * 16)
                        group = scr[l, u, :, :, :, GRP * S * g:GRP * S * (g + 1)]
                        for r, j, copies in ((0, 0, 3), (3, 1, 2), (5, 2, 1)):
                            to = lambda st: st[DH * r:DH * (r + copies), n % RING, :, :].rearrange("p h t -> p (h t)")
                            sp.dma_start(to(qst), group[0, j:j + 1, :, :].to_broadcast([copies, DH, GRP * S])) \
                                .then_inc(st_rd[n % RING], 16)
                            sp.dma_start(to(kst), group[1, 0:copies, :, :]).then_inc(st_rd[n % RING], 16)

                    def maximum_rows(l, n):
                        sp.wait_ge(m_spl, l * NU + n + 1)
                        for j in range(3):
                            sp.dma_start(qst[MR + j:MR + j + 1, n % RING, :, :].rearrange("o h (t c) -> o (h t) c", t=NT),
                                         m3[n % 2][:, j, :]).then_inc(m_row, 16)

                    def expert_weights(u, es):
                        for e in es:
                            m = u * E + e
                            if m >= 4:
                                sp.wait_ge(hx_ready, m - 3)
                            sp.dma_start(cb[m % 4], scr_c[u, e, :].partition_broadcast(128)).then_inc(cb_rd[m % 4], 16)

                    def weights_out(u):
                        read(sp, "c", u)
                        sp.dma_start(scr_c[u, :, :], cbT[u][0:E, :]).then_inc(cb_wr, 16)
                        sp.wait_ge(cb_wr, 16 * (u + 1))

                    def attention(l):
                        if l:
                            parts_out(l, 0)
                        rows_of_ones(l)
                        for n in range(RING):
                            stack(l, n)
                            if l and n < E - 5:
                                expert_weights(1, range(5 + n, 6 + n))
                        for n in range(NU):
                            if 2 + l <= n and n + 2 - l < NU:
                                stack(l, n + 2 - l)
                            maximum_rows(l, n)
                            if n == 1 + l:
                                parts_out(l, 1)

                    def tokens_out(u):
                        read(sp, "o", u)
                        sp.dma_start(ov[u, :, bass.ds(turn, 1), :, :],
                                     G[u][:, :].rearrange("p (o t c) -> p o t c", o=1, t=NT)).then_inc(o_dma, 16)

                    if only_head:
                        tokens_in(0, 0)
                        parts_out(0, 0)
                        sp.wait_ge(st_wr[0], 96)
                        return
                    tokens_in(1, 0)
                    attention(0)
                    weights_out(0)
                    expert_weights(0, range(6))
                    weights_out(1)
                    expert_weights(0, range(6, E))
                    expert_weights(1, range(5))
                    attention(1)
                    sp.wait_ge(ln_h, ln_n(5, 0) + 1)
                    tokens_in(0, 1)
                    tokens_out(0)
                    parts_out(0, 0)
                    tokens_out(1)
                    sp.wait_ge(st_wr[0], 96 * 2)
                    sp.wait_ge(o_dma, 16 * SLOTS)

                @block.tensor
                def _(pe):
                    mm = nc.tensor.matmul

                    def to_rows(dst, u, k):
                        src = stp[u][:, :, :, :].rearrange("p t j k -> p (t j k)")
                        d = dst[0:3 * k, :].bitcast(BF16)
                        for t in range(NT):
                            r = nc.tensor.transpose(d[:, t * 128:(t + 1) * 128], src[:, t * 3 * k:(t + 1) * 3 * k], identb)
                        return r

                    def stack_loaded(l, n):
                        pe.wait_ge(st_rd[n % RING], 6 * 16 * (l * NU // RING + n // RING + 1))

                    def step(kind, *a):
                        if kind == "s":
                            return
                        _, b, n = STEP[(kind, *a)]
                        if n:
                            pe.wait_ge(step_read[b], n)
                        o = bank[6 + b]
                        u = a[0] if kind in ("hb", "a", "m") else a[1] if kind in ("p", "db", "nb", "fg", "fa") else a[-1]
                        cols = lambda t: slice(t * 128, (t + 1) * 128)
                        if kind == "x":
                            pe.wait_ge(x_in[u], 16)
                            for t in range(NT):
                                r = nc.tensor.transpose(o[:, cols(t)], xin[u][:, 0, t, :], ident)
                        elif kind == "lc":
                            if a[0] == 0:
                                read(pe, "x", u)
                            elif a[0] < 4:
                                pe.wait_ge(*((x_att, u + 1), (x_moe, u + 1), (x_att, SLOTS + u + 1))[a[0] - 1])
                            else:
                                pe.wait_ge(sh_ready[u], 2 * (a[0] - 4) + 2)
                            r = mm(o[:, :], K("center"), (X if a[0] < 4 else SH)[u][:, :], start=True, stop=True)
                        elif kind == "ls":
                            pe.wait_ge(ln_sq, ln_n(a[0], u) + 1)
                            for t in range(NT):
                                r = mm(o[:, t:t + 1], SQ[u][:, cols(t)], K("inv"), start=True, stop=True)
                        elif kind == "lb":
                            pe.wait_ge(ln_rstd, ln_n(a[0], u) + 1)
                            for t in range(NT):
                                r = mm(o[:, cols(t)], rs[:, u, t:t + 1].to_broadcast([128, 128]), ident,
                                       start=True, stop=True)
                        elif kind == "p":
                            l, _, i = a
                            pe.wait_ge(ln_h, ln_n(2 * l, u) + 1)
                            w = (AW("q0"), AW("qr0"), AW("k0"), AW("kr0"))[i] if l == 0 else wqc[:, i, :]
                            r = mm(o[:, :], w, Hh[u][:, :], start=True, stop=True)
                        elif kind == "v":
                            for t in range(NT):
                                r = mm(o[:, cols(t)], Hh[u][:, cols(t)], AW(f"v{a[0]}"), start=True, stop=True)
                        elif kind == "hs":
                            for i in range(2):
                                pe.wait_ge(at_sq, 2 * u + i + 1)
                                for t in range(NT):
                                    r = mm(o[:, (2 * t + i) * H:(2 * t + i + 1) * H], (SQ[u], G[u])[i][:, cols(t)],
                                           K("blk16"), start=True, stop=True)
                        elif kind == "hr":
                            pe.wait_ge(at_rs, u + 1)
                            r = to_rows(o, u, 2 * H)
                        elif kind == "hb":
                            read(pe, "hr", u)
                            r = mm(o[:, :], SEL("h")[0:6 * H, a[1] * 128:(a[1] + 1) * 128], rows[u][0:6 * H, :],
                                   start=True, stop=True)
                        elif kind == "a":
                            l, n, s = a
                            if s == 0:
                                stack_loaded(l, n)
                            r = mm(o[:, :], qst[0:MR, n, s // NT, cols(s % NT)], kst[0:MR, n, s // NT, :],
                                   start=True, stop=True)
                        elif kind == "m":
                            l, n = a
                            if l and n < 2:
                                read(pe, "a", l, n, 15)
                            else:
                                pe.wait_ge(a_mx, a_count(l, n, 16))
                            r = nc.tensor.transpose(o[0:16, 0:128], mx[n % 2][:, :], ident)
                        elif kind == "dn":
                            pe.wait_ge(o_raw, a[0] * NU + (u + 1) * NG)
                            for g in range(NG):
                                for t in range(NT):
                                    c = (t * NG + g) * GRP
                                    r = mm(o[:, c:c + GRP], raw[u][g][:, cols(t)], K("sel4"), start=True, stop=True)
                        elif kind == "dr":
                            pe.wait_ge(den_rec, a[0] * SLOTS + u + 1)
                            r = to_rows(o, u, H)
                        elif kind == "db":
                            read(pe, "dr", a[0], u)
                            r = mm(o[:, :], SEL("o")[0:3 * H, a[2] * 128:(a[2] + 1) * 128], rows[u][0:3 * H, :],
                                   start=True, stop=True)
                        elif kind == "y":
                            for g in range(NG):
                                read(pe, "db", a[0], u, g)
                                r = mm(o[:, :], AW(f"p{a[0]}")[:, g * 128:(g + 1) * 128], raw[u][g],
                                       start=(g == 0), stop=(g == NG - 1))
                        elif kind == "g":
                            pe.wait_ge(ln_h, ln_n(1, u) + 1)
                            for t in range(NT):
                                r = mm(o[:, t * E:(t + 1) * E], Hh[u][:, cols(t)], MW("gate"), start=True, stop=True)
                        elif kind == "c":
                            pe.wait_ge(gt_comb, u + 1)
                            for t in range(NT):
                                r = nc.tensor.transpose(o[0:E, cols(t)], comb[u][:, t, :], ident)
                        elif kind == "nr":
                            pe.wait_ge(f_rn, a[0] * SLOTS + u + 1)
                            r = to_rows(o, u, 16)
                        elif kind == "nb":
                            read(pe, "nr", a[0], u)
                            r = mm(o[:, :], SEL("n")[0:48, a[2] * 128:(a[2] + 1) * 128], rows[u][0:48, :],
                                   start=True, stop=True)
                        elif kind == "wo":
                            pe.wait_ge(l_o, (a[0] * NW + (u + 1) * 8) // 2)
                            for f in range(4):
                                r = mm(o[:, :], FW("wo", a[0])[:, f * 128:(f + 1) * 128], qk[u][:, f, :],
                                       start=(f == 0), stop=(f == 3))
                        elif kind in ("fg", "fa"):
                            d, _, c = a
                            pe.wait_ge(ln_h, ln_n(4 + d, u) + 1)
                            w = (kind == "fg") * GH + 128 * c
                            r = mm(o[0:GC[c], :], FW("w1", d)[:, w:w + GC[c]], G[u][:, :], start=True, stop=True)
                        elif kind == "f2":
                            for c in range(3):
                                read(pe, "fa", a[0], u, c)
                                r = mm(o[:, :], FW("w2", a[0])[0:GC[c], c * 128:(c + 1) * 128], gated[u][c][0:GC[c], :],
                                       start=(c == 0), stop=(c == 2))
                        elif kind == "o":
                            pe.wait_ge(x_last, u + 1)
                            for t in range(NT):
                                r = nc.tensor.transpose(o[:, cols(t)], X[u][:, cols(t)], ident)
                        r.then_inc(step_mm, 1)

                    def attention(l):
                        def score_for_max(n, s):
                            hh, t = divmod(s, NT)
                            i = a_count(l, n, s)
                            if s == 0:
                                stack_loaded(l, n)
                            if i >= 3:
                                pe.wait_ge(a_mx, i - 2)
                            mm(bank[i % 3][:, :], qst[0:MR, n % RING, hh, t * 128:(t + 1) * 128],
                               kst[0:MR, n % RING, hh, :], start=True, stop=True).then_inc(a_mm, 1)

                        def score_minus_max(n, t, hh):
                            v = l * NU * 16 + n * 16 + t * GRP + hh
                            if n == 0 and t == 0 and hh == 0:
                                pe.wait_ge(ones_rd, 16 * (l + 1))
                            if t == 0 and hh == 0:
                                pe.wait_ge(m_row, 48 * (l * NU + n + 1))
                            if v >= 3:
                                pe.wait_ge(e_done, v - 2)
                            mm(bank[(3, 4, 6)[v % 3]][:, :], kst[:, n % RING, hh, t * 128:(t + 1) * 128],
                               qst[:, n % RING, hh, :], start=True, stop=True).then_inc(s_mm, 1)

                        def weigh_values(n, t):
                            u, g = divmod(n, NG)
                            v = n * 16 + t * GRP
                            pe.wait_ge(e_done, l * NU * 16 + v + GRP)
                            if t == 0:
                                if l or u:
                                    read(pe, "v", l, u)
                                if n == 0:
                                    pe.wait_ge(o_clear, l + 1)
                                else:
                                    pe.wait_ge(o_raw, l * NU + n)
                            for hh in range(GRP):
                                r = mm(bank[5][32 * hh:32 * hh + 16, :], vaug[u][:, t, GRP * g + hh, :],
                                       pt[(v + hh) % PTB], start=(t == 0), stop=(t == NT - 1))
                            r.then_inc(pv_done, 1)

                        if l == 0:
                            step(*start[0])
                            for s in range(16):
                                score_for_max(0, s)
                                if s in (3, 7, 11):
                                    step(*start[s // 4 + 1])
                            step("m", 0, 0)
                            for s in range(16):
                                score_for_max(1, s)
                        else:
                            pe.wait_ge(mo_hd, 54)
                            pe.wait_ge(x_moe, SLOTS)
                            pe.wait_ge(step_read[0], bank6_steps["attention", 1])
                        for n in range(NU):
                            for t in range(NT):
                                for hh in range(GRP):
                                    if n + 2 < NU:
                                        score_for_max(n + 2, t * GRP + hh)
                                    score_minus_max(n, t, hh)
                                    if hh == 1:
                                        for st in att_steps[l].get((n, t), [])[0:1]:
                                            step(*st)
                                if t == 1 and n + 1 < NU:
                                    step("m", l, n + 1)
                                if t:
                                    weigh_values(n, t - 1)
                                elif n:
                                    weigh_values(n - 1, NT - 1)
                                for st in att_steps[l].get((n, t), [])[1:]:
                                    step(*st)
                        weigh_values(NU - 1, NT - 1)

                    def moe():
                        units = [(u, e, c) for u in slots for e in range(E + 1) for c in range(3)]

                        def down(m):
                            u, e, c = units[m]
                            pe.wait_ge(mo_hd, m + 1)
                            mm(bank[4 + u][:, :], MW("d")[0:CH[c], (3 * e + c) * 128:(3 * e + c + 1) * 128],
                               hd[u][m % 2][0:CH[c], :], start=(e == 0 and c == 0), stop=(e == E and c == 2)) \
                                .then_inc(mo_dn, 1)

                        pe.wait_ge(e_done, NU * 16)
                        pe.wait_ge(o_raw, NU)
                        pe.wait_ge(a_mx, NU * 16)
                        for m, (u, e, c) in enumerate(units):
                            p = 2 * (m % 2)
                            if m >= 2:
                                pe.wait_ge(mo_hd, m - 1)
                            w = e * HID + 128 * c
                            mm(bank[p][0:CH[c], :], MW("g")[:, w:w + CH[c]], Hh[u][:, :], start=True, stop=True) \
                                .then_inc(mo_g, 1)
                            for st in early(moe_steps.get(m, []), 0):
                                step(*st)
                            if e and c == 0:
                                pe.wait_ge(hx_ready, u * E + e)
                            src = hx[u][(e - 1) % 2] if e else Hh[u][:, :]
                            mm(bank[p + 1][0:CH[c], :], MW("u")[:, w:w + CH[c]], src, start=True, stop=True) \
                                .then_inc(mo_u, 1)
                            for st in early(moe_steps.get(m, []), 1):
                                step(*st)
                            if m:
                                down(m - 1)
                            for st in early(moe_steps.get(m, []), 2):
                                step(*st)
                        down(53)

                    def local_layer(d):
                        for u in slots:
                            pe.wait_ge(sh_ready[u], 2 * d + 1)
                            if (d, u) == (0, 0):
                                pe.wait_ge(e_done, 2 * NU * 16)
                            if d and u == 0:
                                pe.wait_ge(l_mk, 4 * d * NW)
                                pe.wait_ge(l_ev, d * NW)
                                pe.wait_ge(l_o, d * NW // 2)
                            for i in range(8):
                                j = (d * SLOTS + u) * 8 + i
                                n, f = ("q", "k")[i // 4], i % 4
                                if u or i >= 2:
                                    pe.wait_ge(f_cp, j - 1)
                                    pe.wait_ge(f_t2, j - 1)
                                for w, dst, s in ((n, bank[2 * (i % 2)], f_main), (n + "r", bank[2 * (i % 2) + 1], f_rot)):
                                    mm(dst[:, :], FW(w, d)[:, f * 128:(f + 1) * 128], SH[u][:, :], start=True, stop=True) \
                                        .then_inc(s, 1)
                                if i >= 2:
                                    norm_sums(d, u, i - 2)
                                if i % 2:
                                    t = i // 2
                                    k = (d * SLOTS + u) * NT + t
                                    if u or t:
                                        pe.wait_ge(f_vc, k)
                                    mm(bank[5][:, :], SH[u][:, t * 128:(t + 1) * 128], FW("v", d),
                                       start=True, stop=True).then_inc(f_v, 1)
                                for st in lp_steps[d][u].get(i, []):
                                    step(*st)
                            if u == 0:
                                norm_sums(d, u, 6)
                                norm_sums(d, u, 7)

                        def scores(w):
                            u, t, hq = w // 8, w // 2 % 4, w % 2
                            lo = 0 if t else 64
                            if w < 2:
                                pe.wait_ge(f_cp, (d + 1) * SLOTS * 8 - 1 + w)
                                pe.wait_ge(f_t2, (d + 1) * SLOTS * 8 - 1 + w)
                            if w % 8 == 0:
                                pe.wait_ge(f_tt, (d * SLOTS + w // 8 + 1) * 8)
                                for f in range(4):
                                    read(pe, "nb", d, u, f)
                            if w >= 2:
                                pe.wait_ge(l_mk, 4 * (d * NW + w - 1))
                            for j in range(2):
                                for par in range(2):
                                    f, p = 2 * hq + j, 64 * par
                                    r = mm(bank[2 * (w % 2) + par][:, j * 192 + lo:j * 192 + 192],
                                           qk[u][p:p + 64, f, t * 128:(t + 1) * 128],
                                           qk[u][p:p + 64, 4 + f, t * 128 - 64 + lo:(t + 1) * 128], start=True, stop=True)
                            r.then_inc(l_s, 1)

                        def transposes(w):
                            t = w // 2 % 4
                            pe.wait_ge(l_p, d * NW + w + 1)
                            if w:
                                pe.wait_ge(l_ev, d * NW + w)
                            else:
                                pe.wait_ge(f_n2, (d + 1) * SLOTS)
                                pe.wait_ge(f_vc, (d + 1) * SLOTS * NT)
                            for par in range(2):
                                for j in range(2):
                                    a = (2 * par + j) * 128
                                    r = nc.tensor.transpose(bank[4][:, a:a + 128], pr[w % 3][:, par, j, 128:256], ident)
                                    if t:
                                        r = nc.tensor.transpose(bank[5][:, a:a + 128], pr[w % 3][:, par, j, 0:128], ident)
                            r.then_inc(l_tr, 1)

                        def values(w):
                            u, t, hq = w // 8, w // 2 % 4, w % 2
                            pe.wait_ge(l_ev, d * NW + w + 1)
                            if w == 0:
                                pe.wait_ge(step_read[0], bank6_steps["local", d])
                            elif hq == 0:
                                pe.wait_ge(l_o, (d * NW + w) // 2)
                            for j in range(2):
                                for first in ((True, False) if t else (True,)):
                                    for par in range(2):
                                        h, f, a = 4 * hq + 2 * j + par, 2 * hq + j, (2 * par + j) * 128
                                        o = bank[6][64 * par:64 * par + 64, f * 128:(f + 1) * 128]
                                        if first:
                                            r = mm(o, vv[u][:, t, h * LD:(h + 1) * LD], ptc[w % 2][:, a:a + 128],
                                                   start=True, stop=(t == 0))
                                        else:
                                            r = mm(o, vv[u][64:128, t - 1, h * LD:(h + 1) * LD],
                                                   ptp[w % 2][64:128, a:a + 128], start=False, stop=True)
                            r.then_inc(l_pv, 1)

                        scores(0)
                        norm_sums(d, 1, 6)
                        scores(1)
                        norm_sums(d, 1, 7)
                        for w in range(NW):
                            transposes(w)
                            for st in lw_steps[d].get((w, 0), []):
                                step(*st)
                            if w + 2 < NW:
                                scores(w + 2)
                            if w:
                                values(w - 1)
                            for st in lw_steps[d].get((w, 1), []):
                                step(*st)
                        values(NW - 1)

                    def norm_sums(d, u, i):
                        pe.wait_ge(f_sq, (d * SLOTS + u) * 8 + i + 1)
                        if u and i == 0:
                            pe.wait_ge(f_n2, d * SLOTS + 1)
                        for t in range(NT):
                            a = (t * 8 + i) * 2
                            r = mm(bank[4][:, a:a + 2], sqr[i % 3][:, t * 128:(t + 1) * 128], K("blk2"),
                                   start=True, stop=True)
                        r.then_inc(f_stat, 1)

                    if not only_head:
                        attention(0)
                        moe()
                        attention(1)
                        for d in range(DEPTH):
                            local_layer(d)
                        pe.wait_ge(l_o, DEPTH * NW // 2)
                    for st in end_steps:
                        step(*st)

                @block.scalar
                def _(act):
                    fn = nc.scalar.activation

                    def step(kind, *a):
                        if kind == "s":
                            return split(*a)
                        k, b, _ = STEP[(kind, *a)]
                        o = bank[6 + b]
                        u = a[-1]
                        if kind == "x":
                            act.wait_ge(step_mm, k + 1)
                            fn(X[u][:, :], o[:, :], ACT.Copy).then_inc(step_read[b], 1)
                        elif kind == "lc":
                            act.wait_ge(step_mm, k + 1)
                            fn(SQ[u][:, :], o[:, :], ACT.Square).then_inc(ln_sq, 1)
                            fn(XC[u][:, :], o[:, :], ACT.Copy).then_inc(step_read[b], 1)
                        elif kind == "p" and a[0] == 1:
                            _, u, i = a
                            act.wait_ge(step_mm, k + 1)
                            fn((SQ[u], G[u])[i][:, :], o[:, :], ACT.Square).then_inc(at_sq, 1)
                            fn((qf, kf)[i][u], o[:, :], ACT.Copy).then_inc(step_read[b], 1)
                        elif kind == "v":
                            act.wait_ge(step_mm, k + 1)
                            act.wait_ge(vaug_one, at_n(a[0], u) + 1)
                            fn(vaug[u][:, :, :, 0:DH].rearrange("p t h c -> p (t h) c"),
                               o[:, :].rearrange("p (a c) -> p a c", c=DH), ACT.Copy).then_inc(step_read[b], 1)
                        elif kind == "hs":
                            read(act, "hs", u)
                            fn(st128[:, u, :], st128[:, u, :], ACT.Sqrt).then_inc(at_sd, 1)
                        elif kind in ("hr", "dr", "nr"):
                            n = 3 * H * (2 if kind == "hr" else 1)
                            act.wait_ge(step_mm, k + 1)
                            fn(rows[u][0:n, :], o[0:n, :].bitcast(BF16)[:, 0:S], ACT.Copy).then_inc(step_read[b], 1)
                        elif kind == "hb" and a[1] == 1:
                            split(1, a[0])
                        elif kind == "y":
                            act.wait_ge(step_mm, k + 1)
                            fn(XC[u][:, :], o[:, :], ACT.Identity, scale=MOD(a[0], 2, u), bias=MOD(a[0], 6, u)) \
                                .then_inc(step_read[b], 1)
                        elif kind == "g":
                            read(act, "g", u)
                            fn(lg[u], lg[u], ACT.Exp).then_inc(gt_exp, 1)
                        elif kind == "c":
                            act.wait_ge(step_mm, k + 1)
                            fn(cbT[u][0:E, :], o[0:E, :], ACT.Copy).then_inc(step_read[b], 1)
                        elif kind == "fg":
                            d, u, c = a
                            act.wait_ge(step_mm, k + 1)
                            fn(gated[u][c][0:GC[c], :], o[0:GC[c], :], ACT.Identity,
                               bias=V_(f"b1{d}")[0:GC[c], 3 + c:4 + c]).then_inc(step_read[b], 1)
                            if c == 2:
                                for c in range(3):
                                    read(act, "fg", d, u, c)
                                    fn(gated[u][c][0:GC[c], :], gated[u][c][0:GC[c], :], ACT.Gelu).then_inc(w1_gl, 1)
                        elif kind == "o":
                            act.wait_ge(step_mm, k + 1)
                            fn(G[u][:, :], o[:, :], ACT.Copy).then_inc(step_read[b], 1)

                    def split(l, u, only=None):
                        for i in range(2) if only is None else (only,):
                            act.wait_ge(sp_hi, at_n(l, u) * 2 + i + 1)
                            fn(parts[u][i][:, 0, :], (qf, kf)[i][u], ACT.Copy).then_inc(sp_first, 1)
                            k = split_n(l, u) * 2 + i
                            act.wait_ge(sp_r, k + 1)
                            fn(parts[u][i][:, 1, :], rem[u], ACT.Copy).then_inc(sp_mid, 1)

                    def attention(l):
                        for n in range(NU):
                            for t in range(NT):
                                for hh in range(GRP):
                                    v = l * NU * 16 + n * 16 + t * GRP + hh
                                    act.wait_ge(s_mm, v + 1)
                                    if n * 16 + t * GRP + hh >= PTB:
                                        act.wait_ge(pv_done, (v - PTB) // GRP + 1)
                                    fn(pt[v % PTB], bank[(3, 4, 6)[v % 3]][:, :], ACT.Exp, scale=float(DH) ** -0.5) \
                                        .then_inc(e_done, 1)
                                    if hh == 1:
                                        for st in att_steps[l].get((n, t), [])[0:1]:
                                            step(*st)
                                if t == 1 and n:
                                    evacuate(l, n - 1)
                                for st in att_steps[l].get((n, t), [])[1:]:
                                    step(*st)
                        evacuate(l, NU - 1)

                    def evacuate(l, n):
                        u, g = divmod(n, NG)
                        act.wait_ge(pv_done, (l * NU + n + 1) * NT)
                        fn(raw[u][g], bank[5][:, :], ACT.Copy).then_inc(o_raw, 1)

                    def moe():
                        for m in range(SLOTS * (E + 1) * 3):
                            c, u = CH[m % 3], m // 27
                            act.wait_ge(mo_g, m + 1)
                            if m >= 2:
                                act.wait_ge(mo_hd, m - 1)
                            fn(sl[u][m % 2][0:c, :], bank[2 * (m % 2)][0:c, :], ACT.Silu).then_inc(mo_sl, 1)
                            for st in moe_steps.get(m, []):
                                step(*st)

                    def local_layer(d):
                        for u in slots:
                            for i in range(8):
                                j = (d * SLOTS + u) * 8 + i
                                act.wait_ge(f_main, j + 1)
                                if u or i >= 2:
                                    act.wait_ge(f_t1, j - 1)
                                fn(qs[i % 2], bank[2 * (i % 2)][:, :], ACT.Copy).then_inc(f_cp, 1)
                                act.wait_ge(f_cp, j + 1)
                                if u or i >= 3:
                                    act.wait_ge(f_stat, j if i < 3 else j - 2)
                                fn(sqr[i % 3], qs[i % 2], ACT.Square).then_inc(f_sq, 1)
                                if i % 2:
                                    t = i // 2
                                    act.wait_ge(f_v, (d * SLOTS + u) * NT + t + 1)
                                    fn(vv[u][:, t, :], bank[5][:, :], ACT.Copy).then_inc(f_vc, 1)
                                if u and i == 0:
                                    act.wait_ge(f_n2, d * SLOTS + 1)
                                    fn(st128[:, 0, 0:64], st128[:, 0, 0:64], ACT.Sqrt).then_inc(f_sd, 1)
                                for st in lp_steps[d][u].get(i, []):
                                    step(*st)

                        def transposed(w):
                            t = w // 2 % 4
                            act.wait_ge(l_tr, d * NW + w + 1)
                            if w >= 2:
                                act.wait_ge(l_pv, d * NW + w - 1)
                            if t:
                                fn(ptp[w % 2][64:128, :], bank[5][64:128, :], ACT.Copy).then_inc(l_evp, 1)
                            fn(ptc[w % 2], bank[4][:, :], ACT.Copy).then_inc(l_ev, 1)

                        def output(w):
                            u, t = w // 8, w // 2 % 4
                            act.wait_ge(l_pv, d * NW + w + 1)
                            fn(qk[u][:, 0:4, t * 128:(t + 1) * 128],
                               bank[6][:, :].rearrange("p (f t) -> p f t", f=4), ACT.Copy).then_inc(l_o, 1)

                        for w in range(NW):
                            t = w // 2 % 4
                            lo = 64 if t else 128
                            act.wait_ge(l_nm, d * NW + w + 1)
                            for par in range(2):
                                for j in range(2):
                                    p = pr[w % 3][:, par, j, lo:256]
                                    fn(p, p, ACT.Exp, scale=8.0, bias=lm[w % 3][:, par, j:j + 1],
                                       accum_out=lsum[w % 3][:, par, j:j + 1]).then_inc(l_ex, 1)
                            if w:
                                transposed(w - 1)
                            for st in lw_steps[d].get((w - 1, 0), []):
                                step(*st)
                            if w % 2 and w > 2:
                                output(w - 2)
                            for st in lw_steps[d].get((w - 1, 1), []):
                                step(*st)
                        transposed(NW - 1)
                        output(NW - 1)

                    if not only_head:
                        for st in start:
                            step(*st)
                        attention(0)
                        moe()
                        attention(1)
                        for d in range(DEPTH):
                            local_layer(d)
                    for st in end_steps:
                        step(*st)

                @block.vector
                def _(dve):
                    tt, ts, stt = nc.vector.tensor_tensor, nc.vector.tensor_scalar, nc.vector.scalar_tensor_tensor
                    links = [0]

                    def link(ins):
                        links[0] += 1
                        ins.then_inc(dve_link, 1)
                        dve.wait_ge(dve_link, links[0])

                    def three_parts(u, k, done):
                        src = st128[:, u, 0:NT * k].rearrange("p (t k) -> p t k", t=NT)
                        r = strem[:, u, 0:NT * k].rearrange("p (t k) -> p t k", t=NT)
                        q = stp[u][:, :, :, :].rearrange("p t j k -> p (t j k)")[:, 0:NT * 3 * k] \
                            .rearrange("p (t j k) -> p t j k", t=NT, j=3)
                        link(nc.vector.tensor_copy(q[:, :, 0, :], src))
                        link(tt(r, src, q[:, :, 0, :], ALU.subtract))
                        link(nc.vector.tensor_copy(q[:, :, 1, :], r))
                        tt(q[:, :, 2, :], r, q[:, :, 1, :], ALU.subtract).then_inc(done, 1)

                    def split(l, u, only=None):
                        for i in range(2) if only is None else (only,):
                            k = at_n(l, u) * 2 + i
                            f = (qf, kf)[i][u]
                            m = split_n(l, u) * 2 + i
                            dve.wait_ge(sp_first, m + 1)
                            if i:
                                dve.wait_ge(sp_done, k)
                            tt(rem[u], f, parts[u][i][:, 0, :], ALU.subtract).then_inc(sp_r, 1)
                            dve.wait_ge(sp_mid, m + 1)
                            tt(parts[u][i][:, 2, :], rem[u], parts[u][i][:, 1, :], ALU.subtract).then_inc(sp_done, 1)

                    def step(kind, *a):
                        if kind == "s":
                            return split(*a)
                        k, b, _ = STEP[(kind, *a)]
                        o = bank[6 + b]
                        u = a[-1]
                        if kind == "ls":
                            dve.wait_ge(step_mm, k + 1)
                            ts(ve[:, u, :], o[:, 0:NT], 1e-5, None, ALU.add).then_inc(step_read[b], 1)
                        elif kind == "lb":
                            i = a[0]
                            dve.wait_ge(step_mm, k + 1)
                            read(dve, "lc", i, u)
                            tt(XC[u][:, :], XC[u][:, :], o[:, :], ALU.mult).then_inc(step_read[b], 1)
                            read(dve, kind, *a)
                            if i < 4:
                                ts(Hh[u][:, :], XC[u][:, :], MOD(i // 2, 3 * (i % 2) + 1, u), MOD(i // 2, 3 * (i % 2), u),
                                   ALU.mult, ALU.add).then_inc(ln_h, 1)
                            else:
                                ts(G[u][:, :], XC[u][:, :], V_(f"lg{i - 4}"), V_(f"lb{i - 4}"), ALU.mult, ALU.add) \
                                    .then_inc(ln_h, 1)
                        elif kind == "p" and a[0] == 0:
                            _, u, i = a
                            f = (qf, kf)[i // 2][u]
                            dve.wait_ge(step_mm, k + 1)
                            if i % 2 == 0:
                                tt(f, o[:, :], K("cos"), ALU.mult).then_inc(step_read[b], 1)
                            else:
                                if i == 3:
                                    dve.wait_ge(sp_hi, at_n(0, u) * 2 + 1)
                                tt(ropet[u], o[:, :], K("sin"), ALU.mult).then_inc(step_read[b], 1)
                                read(dve, kind, *a)
                                tt(f, f, ropet[u], ALU.add).then_inc(sp_hi, 1)
                        elif kind == "hs":
                            dve.wait_ge(step_mm, k + 1)
                            ts(st128[:, u, :], o[:, 0:128], 1e-5, None, ALU.add).then_inc(step_read[b], 1)
                            dve.wait_ge(at_sd, u + 1)
                            link(nc.vector.reciprocal(st128[:, u, :], st128[:, u, :]))
                            three_parts(u, 2 * H, at_rs)
                        elif kind == "hb":
                            u, i = a
                            f = (qf, kf)[i][u]
                            dve.wait_ge(step_mm, k + 1)
                            read(dve, "p", 1, u, i)
                            tt(f, f, o[:, :], ALU.mult).then_inc(step_read[b], 1)
                            read(dve, kind, *a)
                            ts(f, f, V_(("qg", "kg")[i]), V_(("qb", "kb")[i]), ALU.mult, ALU.add).then_inc(sp_hi, 1)
                            if i:
                                split(1, u)
                        elif kind == "a":
                            dve.wait_ge(step_mm, k + 1)
                            nc.vector.tensor_reduce(mx[a[1] % 2][:, a[2]:a[2] + 1], o[:, :], axis=AX.X,
                                                    op=ALU.max).then_inc(step_read[b], 1)
                        elif kind == "m":
                            l, n = a
                            dve.wait_ge(step_mm, k + 1)
                            if l * NU + n >= 2:
                                dve.wait_ge(m_row, 48 * (l * NU + n - 1))
                            m = m3[n % 2]
                            link(ts(m[:, 0, :], o[0:16, 0:128], -1.0, None, ALU.mult))
                            stt(mneg[:, :], o[0:16, 0:128], -1.0, m[:, 0, :], ALU.mult, ALU.subtract) \
                                .then_inc(step_read[b], 1)
                            read(dve, kind, *a)
                            link(nc.vector.tensor_copy(m[:, 1, :], mneg[:, :]))
                            tt(m[:, 2, :], mneg[:, :], m[:, 1, :], ALU.subtract).then_inc(m_spl, 1)
                            dve.wait_ge(m_spl, l * NU + n + 1)
                        elif kind == "dn":
                            dve.wait_ge(step_mm, k + 1)
                            nc.vector.reciprocal(st128[:, u, 0:64], o[:, 0:64]).then_inc(step_read[b], 1)
                            read(dve, kind, *a)
                            three_parts(u, H, den_rec)
                        elif kind == "db":
                            l, u, g = a
                            dve.wait_ge(step_mm, k + 1)
                            tt(raw[u][g], raw[u][g], o[:, :], ALU.mult).then_inc(step_read[b], 1)
                        elif kind == "y":
                            read(dve, kind, *a)
                            tt(X[u][:, :], X[u][:, :], XC[u][:, :], ALU.add).then_inc(x_att, 1)
                        elif kind == "g":
                            one = lambda v, n: v.unsqueeze(2).to_broadcast([128, NT, n])
                            dve.wait_ge(step_mm, k + 1)
                            p = o[:, 0:NT * E].rearrange("p (t e) -> p t e", t=NT)
                            link(nc.vector.tensor_reduce(s4[u], p, axis=AX.X, op=ALU.max))
                            tt(lg[u], p, one(s4[u], E), ALU.subtract).then_inc(step_read[b], 1)
                            dve.wait_ge(gt_exp, u + 1)
                            l3 = lg[u]
                            link(nc.vector.tensor_reduce(s4[u], l3, axis=AX.X, op=ALU.add))
                            link(nc.vector.reciprocal(s4[u], s4[u]))
                            link(tt(l3, l3, one(s4[u], E), ALU.mult))
                            for t in range(NT):
                                link(nc.vector.max(top[u][:, t, :], lg[u][:, t, :]))
                            for t in range(NT):
                                link(nc.vector.max_index(topi[u][:, t, :], top[u][:, t, :], lg[u][:, t, :]))
                            link(nc.vector.tensor_copy(topf[u], topi[u]))
                            link(tt(s4[u], top[u][:, :, 0], top[u][:, :, 1], ALU.add))
                            link(ts(s4[u], s4[u], 1e-20, None, ALU.add))
                            link(nc.vector.reciprocal(s4[u], s4[u]))
                            link(tt(w2v[u], top[u][:, :, 0:2], one(s4[u], 2), ALU.mult))
                            io = K("iota8").unsqueeze(1).to_broadcast([128, NT, E])
                            for j, dst in enumerate((comb[u], c2[u])):
                                link(tt(dst, io, one(topf[u][:, :, j], E), ALU.is_equal))
                                link(tt(dst, dst, one(w2v[u][:, :, j], E), ALU.mult))
                            tt(comb[u], comb[u], c2[u], ALU.add).then_inc(gt_comb, 1)
                        elif kind == "nb":
                            _, u, f = a
                            dve.wait_ge(step_mm, k + 1)
                            tt(qk[u][:, 4 + f, :], qk[u][:, 4 + f, :], o[:, :], ALU.mult).then_inc(step_read[b], 1)
                        elif kind == "wo":
                            dve.wait_ge(step_mm, k + 1)
                            tt(Hh[u][:, :], Hh[u][:, :], o[:, :], ALU.add).then_inc(step_read[b], 1)
                            read(dve, kind, *a)
                            shift(u)
                        elif kind == "fa":
                            d, u, c = a
                            dve.wait_ge(step_mm, k + 1)
                            dve.wait_ge(w1_gl, (d * SLOTS + u) * 3 + c + 1)
                            stt(gated[u][c][0:GC[c], :], o[0:GC[c], :], V_(f"b1{d}")[0:GC[c], c:c + 1],
                                gated[u][c][0:GC[c], :], ALU.add, ALU.mult).then_inc(step_read[b], 1)
                        elif kind == "f2":
                            dve.wait_ge(step_mm, k + 1)
                            stt(Hh[u][:, :], o[:, :], V_(f"b2{a[0]}"), Hh[u][:, :], ALU.add, ALU.add) \
                                .then_inc(step_read[b], 1)
                            read(dve, kind, *a)
                            if a[0] < DEPTH - 1:
                                shift(u)
                            else:
                                stt(X[u][:, :], Hh[u][:, :], MOD(1, 5, u), X[u][:, :], ALU.mult, ALU.add).then_inc(x_last, 1)

                    def shift(u):
                        nc.vector.tensor_copy(SH[u][0:64, :], Hh[u][0:64, :])
                        nc.vector.tensor_copy(SH[u][64:128, 1:S], Hh[u][64:128, 0:S - 1]).then_inc(sh_ready[u], 1)

                    def attention(l):
                        def maxima(n, steps):
                            for s in steps:
                                i = a_count(l, n, s)
                                dve.wait_ge(a_mm, i + 1)
                                nc.vector.tensor_reduce(mx[n % 2][:, s:s + 1], bank[i % 3][:, :], axis=AX.X,
                                                        op=ALU.max).then_inc(a_mx, 1)

                        if l:
                            dve.wait_ge(x_moe, SLOTS)
                        nc.vector.memset(bank[5][:, :], 0.0).then_inc(o_clear, 1)
                        if l == 0:
                            step(*start[0])
                            for s in range(16):
                                maxima(0, range(s, s + 1))
                                if s in (3, 7, 11):
                                    step(*start[s // 4 + 1])
                            step("m", 0, 0)
                            maxima(1, range(16))
                        for n in range(NU):
                            for t in range(NT):
                                if n + 2 < NU:
                                    maxima(n + 2, range(NT * t, NT * t + 2))
                                for st in att_steps[l].get((n, t), [])[0:1]:
                                    step(*st)
                                if n + 2 < NU:
                                    maxima(n + 2, range(NT * t + 2, NT * t + NT))
                                if t == 1 and n + 1 < NU:
                                    step("m", l, n + 1)
                                for st in att_steps[l].get((n, t), [])[1:]:
                                    step(*st)

                    def moe():
                        def residual(u):
                            dve.wait_ge(mo_dn, 27 * (u + 1))
                            stt(X[u][:, :], bank[4 + u][:, :], MOD(0, 5, u), X[u][:, :], ALU.mult, ALU.add) \
                                .then_inc(x_moe, 1)

                        for m in range(SLOTS * (E + 1) * 3):
                            c, u = CH[m % 3], m // 27
                            for st in early(moe_steps.get(m, []), 0):
                                step(*st)
                            dve.wait_ge(mo_sl, m + 1)
                            dve.wait_ge(mo_u, m + 1)
                            if m >= 2:
                                dve.wait_ge(mo_dn, m - 1)
                            tt(hd[u][m % 2][0:c, :], sl[u][m % 2][0:c, :], bank[2 * (m % 2) + 1][0:c, :], ALU.mult) \
                                .then_inc(mo_hd, 1)
                            if m == 28:
                                residual(0)
                            for k in (1, 2):
                                for st in early(moe_steps.get(m, []), k):
                                    step(*st)
                        residual(1)

                    def local_layer(d):
                        if d == 0:
                            dve.wait_ge(ln_h, ln_n(3, 0) + 1)
                            shift(0)
                        for i, (t, s) in enumerate((("xa", "qs"), ("xb", "qsr"), ("xai", "ks"), ("xbi", "ksr"))):
                            ts(tab[:, i, :], K(t), V_(f"{s}{d}"), None, ALU.mult).then_inc(tb_ready, 1)
                        dve.wait_ge(tb_ready, 4 * (d + 1))

                        def rotated(u, i):
                            j = (d * SLOTS + u) * 8 + i
                            dve.wait_ge(f_rot, j + 1)
                            tt(qk[u][:, i, :], bank[2 * (i % 2) + 1][:, :], tab[:, 2 * (i // 4) + 1, :], ALU.mult) \
                                .then_inc(f_t2, 1)

                        def squared_norms(u):
                            dve.wait_ge(f_stat, (d * SLOTS + u + 1) * 8)
                            ts(st128[:, u, 0:64], bank[4][:, 0:64], 1e-24, None, ALU.max).then_inc(f_n2, 1)

                        def reciprocal_norms(u):
                            if u == 0:
                                dve.wait_ge(f_sd, d + 1)
                                nc.vector.reciprocal(st128[:, u, 0:64], st128[:, u, 0:64]).then_inc(f_r1, 1)
                            dve.wait_ge(f_r1, d * SLOTS + u + 1)
                            three_parts(u, 16, f_rn)

                        for u in slots:
                            rotated(u, 0)
                            for i in range(8):
                                j = (d * SLOTS + u) * 8 + i
                                if i < 7:
                                    rotated(u, i + 1)
                                dve.wait_ge(f_t1, j + 1)
                                dve.wait_ge(f_t2, j + 1)
                                tt(qk[u][:, i, :], qk[u][:, i, :], xt[i % 2], ALU.add).then_inc(f_tt, 1)
                                if u and i == 1:
                                    reciprocal_norms(0)
                                for st in lp_steps[d][u].get(i, []):
                                    step(*st)
                            if u == 0:
                                squared_norms(0)
                            if d == 0 and u == 0:
                                dve.wait_ge(ln_h, ln_n(3, 1) + 1)
                                shift(1)
                        def masked(w):
                            u, t, hq = w // 8, w // 2 % 4, w % 2
                            lo = 0 if t else 64
                            dve.wait_ge(l_s, d * NW + w + 1)
                            if w >= 3:
                                dve.wait_ge(l_tr, d * NW + w - 2)
                            for par in range(2):
                                for j in range(2):
                                    a = (t * 8 + 2 * hq + j) * 2 + par
                                    stt(pr[w % 3][:, par, j, 64 + lo:256],
                                        bank[2 * (w % 2) + par][:, j * 192 + lo:j * 192 + 192],
                                        st128[:, u, a:a + 1], K("mask")[:, lo:192], ALU.mult, ALU.add).then_inc(l_mk, 1)
                            dve.wait_ge(l_mk, 4 * (d * NW + w + 1))
                            link(nc.vector.tensor_reduce(lm[w % 3][:, :, :], pr[w % 3][:, :, :, 64 + lo:256],
                                                         axis=AX.X, op=ALU.max))
                            ts(lm[w % 3][:, :, :], lm[w % 3][:, :, :], -8.0, None, ALU.mult).then_inc(l_nm, 1)

                        def normalise(w):
                            t = w // 2 % 4
                            lo = 64 if t else 128
                            dve.wait_ge(l_ex, 4 * (d * NW + w + 1))
                            link(nc.vector.reciprocal(lrec[w % 3][:, :, :], lsum[w % 3][:, :, :]))
                            for par in range(2):
                                for j in range(2):
                                    p = pr[w % 3][:, par, j, lo:256]
                                    r = ts(p, p, lrec[w % 3][:, par, j:j + 1], None, ALU.mult)
                            r.then_inc(l_p, 1)

                        dve.wait_ge(f_sq, (d + 1) * SLOTS * 8)
                        masked(0)
                        squared_norms(1)
                        masked(1)
                        for w in range(NW):
                            normalise(w)
                            for st in lw_steps[d].get((w - 1, 1), []):
                                step(*st)
                            if 0 < w < NW - 1:
                                masked(w + 1)
                            for st in lw_steps[d].get((w, 0), []):
                                step(*st)
                            if w == 1:
                                reciprocal_norms(1)
                        for st in lw_steps[d].get((NW - 1, 1), []):
                            step(*st)

                    def modulation(u, ahead):
                        nc.vector.tensor_copy(modu[:, :, u:u + 1].rearrange("p k o -> p o k"),
                                              of_turn(modv[:, :, :, u], ahead)).then_inc(mod_ready, 1)

                    if not only_head:
                        modulation(1, 0)
                        dve.wait_ge(mod_ready, 1)
                        attention(0)
                        moe()
                        attention(1)
                        for d in range(DEPTH):
                            local_layer(d)
                        dve.wait_ge(x_last, 1)
                    modulation(0, 0 if only_head else 1)
                    dve.wait_ge(mod_ready, 1 if only_head else 2)
                    for st in end_steps:
                        step(*st)

                @block.gpsimd
                def _(pool):
                    tt = nc.gpsimd.tensor_tensor

                    def norm_step(i, u):
                        read(pool, "ls", i, u)
                        tt(rs[:, u, :], ve[:, u, :], mhalf[:, :], ALU.pow).then_inc(ln_rstd, 1)

                    def reciprocal_norms(d, u):
                        pool.wait_ge(f_n2, d * SLOTS + u + 1)
                        n = st128[:, u, 0:64]
                        tt(n, n, mhalf[:, 0:1].to_broadcast([128, 64]), ALU.pow).then_inc(f_r1, 1)

                    def value_tile(l, u):
                        nc.gpsimd.memset(vaug[u], 0.0).then_inc(zeroed, 1)
                        pool.wait_ge(zeroed, at_n(l, u) + 1)
                        nc.gpsimd.memset(vaug[u][:, :, :, DH:DH + 1], 1.0).then_inc(vaug_one, 1)

                    def scaled(m):
                        u, e = divmod(m, E)
                        pool.wait_ge(cb_rd[m % 4], 16 * (m // 4 + 1))
                        if e >= 2:
                            pool.wait_ge(mo_u, u * 27 + 3 * e)
                        tt(hx[u][e % 2], Hh[u][:, :], cb[m % 4], ALU.mult).then_inc(hx_ready, 1)

                    def clear_stacks(pieces):
                        for k in pieces:
                            w = 2 * RING * GRP * S // 2 // CLEARS
                            nc.gpsimd.memset(stacks[:, w * k:w * (k + 1)], 0.0).then_inc(ring_clear, 1)

                    def head():
                        norm_step(0, 0)
                        if not only_head:
                            pool.wait_ge(l_pv, DEPTH * NW)
                        value_tile(0, 0)
                        if not only_head:
                            read(pool, "wo", 1, 1)
                        clear_stacks(range(CLEARS))

                    if only_head:
                        head()
                        return
                    norm_step(0, 1)
                    value_tile(0, 1)
                    for i in range(2):
                        pool.wait_ge(sp_hi, i + 1)
                        if i:
                            pool.wait_ge(sp_done, i)
                        p, f = parts[1][i], (qf, kf)[i][1]
                        nc.gpsimd.tensor_copy(p[:, 0, :], f).then_inc(sp_pool, 1)
                        pool.wait_ge(sp_pool, 3 * i + 1)
                        tt(rem[1], f, p[:, 0, :], ALU.subtract).then_inc(sp_pool, 1)
                        pool.wait_ge(sp_pool, 3 * i + 2)
                        nc.gpsimd.tensor_copy(p[:, 1, :], rem[1]).then_inc(sp_pool, 1)
                        pool.wait_ge(sp_pool, 3 * i + 3)
                        tt(p[:, 2, :], rem[1], p[:, 1, :], ALU.subtract).then_inc(sp_done, 1)
                    norm_step(1, 0)
                    pool.wait_ge(pv_done, NU * NT)
                    for e in range(2):
                        scaled(e)
                    norm_step(1, 1)
                    for e in range(2, E):
                        scaled(e)
                    scaled(E)
                    norm_step(2, 0)
                    value_tile(1, 0)
                    for e in range(1, E):
                        scaled(E + e)
                        if e == 1:
                            pool.wait_ge(mo_dn, 27)
                        if e <= CLEARS:
                            clear_stacks(range(e - 1, e))
                    norm_step(2, 1)
                    value_tile(1, 1)
                    norm_step(3, 0)
                    for d in range(DEPTH):
                        for u in slots:
                            for i in range(8):
                                j = (d * SLOTS + u) * 8 + i
                                pool.wait_ge(tb_ready, 4 * (d + 1))
                                pool.wait_ge(f_cp, j + 1)
                                if u or i >= 2:
                                    pool.wait_ge(f_tt, j - 1)
                                tt(xt[i % 2], qs[i % 2], tab[:, 2 * (i // 4), :], ALU.mult).then_inc(f_t1, 1)
                                if d == 0 and u == 0 and i == 6:
                                    norm_step(3, 1)
                                if d == 1 and u == 0 and i == 2:
                                    norm_step(4, 1)
                        reciprocal_norms(d, 1)
                        norm_step(4 + d, 0)
                    norm_step(5, 1)
                    head()
            nc.gpsimd.sem_clear(range(first, last + 1))
            nc.all_engine_barrier()

        program(None, True)
        with nc.Fori(0, B // SLOTS) as turn:
            program(turn, False)


def lay_out(v):
    f = {k: np.asarray(a) for k, a in v.items()}

    def pad(a, rows):
        out = np.zeros((rows,) + a.shape[1:], a.dtype)
        out[:a.shape[0]] = a
        return out

    def swapped(w, width):
        return np.roll(w.reshape(w.shape[0], -1, width), width // 2, axis=2).reshape(w.shape)

    att = {}
    w = f["L0_attn_w_qkv"]
    att["q0"], att["k0"], att["v0"] = w[:, :C], w[:, C:2 * C], w[:, 2 * C:]
    att["qr0"], att["kr0"] = swapped(att["q0"], DH), swapped(att["k0"], DH)
    w = f["L1_attn_w_qkv"]
    att["qT1"], att["kT1"], att["v1"] = w[:, :C].T, w[:, C:2 * C].T, w[:, 2 * C:]
    for l in range(2):
        wp = f[f"L{l}_attn_w_proj"].reshape(NG, GRP, DH, C)
        out = np.zeros((GRP, 32, NG, C), wp.dtype)
        out[:, :DH] = wp.transpose(1, 2, 0, 3)
        att[f"p{l}"] = out.reshape(128, NG * C)
    att_w = np.concatenate([att[n] for n, _ in ATT_SIZES], axis=1)

    moe = {"gate": f["L0_ffn_gate_w"].T}
    for n, s_, e_ in (("g", "shared_gate", "expert_gate"), ("u", "shared_up", "expert_up")):
        w = np.concatenate([f["L0_ffn_" + s_][None], f["L0_ffn_" + e_]])
        moe[n] = w.transpose(2, 0, 1).reshape(C, -1)
    w = np.concatenate([f["L0_ffn_shared_down"][None], f["L0_ffn_expert_down"]]).transpose(2, 0, 1)
    moe["d"] = pad(w, 384).reshape(3, 128, E + 1, C).transpose(1, 2, 0, 3).reshape(128, -1)
    moe_w = np.concatenate([moe[n] for n, _ in MOE_SIZES], axis=1)

    ffn, vec = {}, {}
    twice = lambda a: np.concatenate([a, a])
    col = lambda a: a.reshape(-1, 1)
    for d in range(DEPTH):
        w = f["L1_ffn_wqkv"][d]
        q, k, ffn[f"v{d}"] = w[:, :QKV], w[:, QKV:2 * QKV], w[:, 2 * QKV:]
        ffn[f"q{d}"], ffn[f"qr{d}"] = q, swapped(q, LD)
        ffn[f"k{d}"], ffn[f"kr{d}"] = k, swapped(k, LD)
        ffn[f"wo{d}"] = f["L1_ffn_wo"][d].reshape(4, 128, C).transpose(1, 0, 2).reshape(128, -1)
        ffn[f"w1{d}"] = f["L1_ffn_w1"][d]
        ffn[f"w2{d}"] = pad(f["L1_ffn_w2"][d], 384).reshape(3, 128, C).transpose(1, 0, 2).reshape(128, -1)
        for n, src in (("qs", "q_scale"), ("ks", "k_scale")):
            a = f["L1_ffn_" + src][d]
            vec[f"{n}{d}"] = col(twice(a))
            vec[f"{n}r{d}"] = col(twice(np.roll(a, LD // 2)))
        vec[f"lg{d}"], vec[f"lb{d}"] = col(f["L1_ffn_ln_g"][d]), col(f["L1_ffn_ln_b"][d])
        b1 = f["L1_ffn_b1"][d]
        vec[f"b1{d}"] = np.concatenate([pad(b1[k * GH:(k + 1) * GH], 384).reshape(3, 128) for k in range(2)]).T
        vec[f"b2{d}"] = col(f["L1_ffn_b2"][d])
    vec["bproj"] = col(f["L0_attn_b_proj"])
    for n, src in (("qg", "q_gamma"), ("qb", "q_beta"), ("kg", "k_gamma"), ("kb", "k_beta")):
        vec[n] = col(np.tile(f["L1_attn_" + src], H))
    ffn_w = np.concatenate([ffn[n] for n, _ in FFN_SIZES], axis=1)
    vec = np.concatenate([vec[n] for n, _ in VEC_SIZES], axis=1)
    cT = np.concatenate([f["L0_c"].T, f["L1_c"].T], axis=1)
    wmod = np.stack([f["L0_wmod"], f["L1_wmod"]])
    ones = np.full((3, H * S // 2), 0x3F803F80, np.uint32).view(np.float32)
    return {"x": pad(f["L0_attn_x"], B + SLOTS), "consts": constants(), "sel": selectors(), "ones": ones, "att_w": att_w, "moe_w": moe_w,
            "ffn_w": ffn_w, "vec": vec, "cT": cT, "wmod": wmod}


def kernel(**inputs):
    import concourse.bacc as bacc
    from concourse.bass_utils import run_bass_kernel_spmd

    nc = bacc.Bacc("TRN2", target_bir_lowering=False, num_devices=1)
    arrays, args = {}, []
    for name, a in lay_out(inputs).items():
        a = np.ascontiguousarray(a)
        arrays[f"in_{name}"] = a
        args.append(nc.dram_tensor(f"in_{name}", a.shape, mybir.dt.from_np(a.dtype), kind="ExternalInput").ap())
    args.append(nc.dram_tensor("out", (B, S, C), F32, kind="ExternalOutput").ap())
    adaln_kernel(nc, *args)
    return run_bass_kernel_spmd(nc, [arrays], core_ids=[0]).results[0]["out"]
```
